# Optimizing a Trainium2 kernel written in Bass

```python
import numpy as np
import jax
import jax.numpy as jnp

def _softmax(x, axis=-1):
    return jax.nn.softmax(x, axis=axis)

def _gelu(x):
    return jax.nn.gelu(x, approximate=True)

def _silu(x):
    return jax.nn.silu(x)

def _sigmoid(x):
    return jax.nn.sigmoid(x)

def _layernorm(x, axis=-1, eps=1e-05):
    m = jnp.mean(x, axis=axis, keepdims=True)
    v = jnp.var(x, axis=axis, keepdims=True)
    return (x - m) / jnp.sqrt(v + eps)

def _scatter_add(tgt, idx, src, axis=0):
    return tgt.at[idx].add(src)

def _segment_sum(src, seg, n):
    return jax.ops.segment_sum(src, seg, n)
kernel_name = 'mk_xattn_ffn_d4_seqx_r4_b75f92'

def setup_inputs(seed: int=0):
    np.random.seed(seed)
    _w = jnp.asarray

    def _rec_inputs():
        import jax
        import jax.numpy as jnp
        _rk = jax.random.key(seed)
        x = -0.0002928 + 1 * jax.random.normal(jax.random.fold_in(_rk, 1), (4, 512, 256), jnp.float32)
        _lenS = 512 - jax.random.randint(jax.random.fold_in(_rk, 7), (4,), 0, max(1, 512 // 4) + 1, jnp.int32)
        _lenS2 = 1601 - jax.random.randint(jax.random.fold_in(_rk, 8), (4,), 0, max(1, 1601 // 4) + 1, jnp.int32)
        _ctx_1024P = jax.random.normal(jax.random.fold_in(_rk, 11), (4, 16, 256), jnp.float32)
        _ctx_1024c = jax.random.dirichlet(jax.random.fold_in(_rk, 511), 0.3 * jnp.ones((16,), jnp.float32), (4, 1601))
        _ctx_1024t = jnp.einsum('bsk,bkd->bsd', _ctx_1024c, _ctx_1024P)
        _ctx_1024t = _ctx_1024t * jax.lax.rsqrt(jnp.mean(jnp.square(_ctx_1024t)) + 1e-12) * 0.953939
        ctx_1024 = 4.13588e-05 + 0.999923 * (_ctx_1024t + 0.3 * jax.random.normal(jax.random.fold_in(_rk, 611), (4, 1601, 256), jnp.float32))
        return (x, ctx_1024)
    x, ctx_1024 = _rec_inputs()

    def _L0_xattn_setup():
        import jax, jax.numpy as jnp
        import numpy as np
        D_MODEL = 256
        NUM_HEADS = 16
        DEPTH = D_MODEL // NUM_HEADS
        B, LQ, LKV = (4, 256, 512)

        def _xavier(key, shape):
            fan_in, fan_out = (shape[1], shape[0])
            limit = float(np.sqrt(6.0 / (fan_in + fan_out)))
            return jax.random.uniform(key, shape, jnp.float32, -limit, limit)

        def _split_heads(x, b):
            return x.reshape(b, -1, NUM_HEADS, DEPTH).transpose(0, 2, 1, 3)
        key = jax.random.key(seed)
        ks = jax.random.split(key, 6)
        return {'query': jax.random.normal(ks[0], (B, LQ, D_MODEL), jnp.float32), 'value': jax.random.normal(ks[1], (B, LKV, D_MODEL), jnp.float32), 'wq_w': _xavier(ks[2], (D_MODEL, D_MODEL)), 'wk_w': _xavier(ks[3], (D_MODEL, D_MODEL)), 'wv_w': _xavier(ks[4], (D_MODEL, D_MODEL)), 'dense_w': _xavier(ks[5], (D_MODEL, D_MODEL)), 'wq_b': jnp.zeros((D_MODEL,), jnp.float32), 'wk_b': jnp.zeros((D_MODEL,), jnp.float32), 'wv_b': jnp.zeros((D_MODEL,), jnp.float32), 'dense_b': jnp.zeros((D_MODEL,), jnp.float32)}
    _L0_xattn_all = _L0_xattn_setup()
    _L0_xattn_in = {k: v for k, v in _L0_xattn_all.items() if k in ('wq_w', 'wk_w', 'wv_w', 'dense_w', 'wq_b', 'wk_b', 'wv_b', 'dense_b')}
    del _L0_xattn_all

    def _L0_ffn_setup():
        import jax, jax.numpy as jnp
        import numpy as np
        key = jax.random.key(seed)
        k1, k2, k3 = jax.random.split(key, 3)
        B, S, D, E, H = (4, 512, 256, 8, 256)
        x = jax.random.normal(k1, (B, S, D), dtype=jnp.float32)
        Wg = jax.random.normal(k2, (D, E), dtype=jnp.float32) / np.sqrt(D)
        We = jax.random.normal(k3, (E, D, H), dtype=jnp.float32) / np.sqrt(D)
        be = jnp.zeros((E, H), dtype=jnp.float32)
        return {'x': x, 'Wg': Wg, 'We': We, 'be': be}
    _L0_ffn_all = _L0_ffn_setup()
    _L0_ffn_in = {k: v for k, v in _L0_ffn_all.items() if k in ('Wg', 'We', 'be')}
    del _L0_ffn_all

    def _L1_xattn_setup():
        import jax, jax.numpy as jnp
        import numpy as np
        import math
        D_MODEL = 256
        NHEAD = 16
        FACTOR = 1
        B, L = (2, 1024)

        def _autocorr_forward(query, key, value, Wq, bq, Wk, bk, Wv, bv, Wo, bo):
            Bq, Lq, d = query.shape
            Lk = key.shape[1]
            H = NHEAD
            Dk = d // H
            Q = (query @ Wq + bq).reshape(Bq, Lq, H, Dk).transpose(0, 2, 1, 3)
            K = (key @ Wk + bk).reshape(Bq, Lk, H, Dk).transpose(0, 2, 1, 3)
            V = (value @ Wv + bv).reshape(Bq, Lk, H, Dk).transpose(0, 2, 1, 3)
            if Lk > Lq:
                K = K[:, :, :Lq, :]
                V = V[:, :, :Lq, :]
            elif Lq > Lk:
                pad = [(0, 0), (0, 0), (0, Lq - Lk), (0, 0)]
                K = jnp.pad(K, pad)
                V = jnp.pad(V, pad)
            Lloc = Lq
            Qf = jnp.fft.rfft(Q, axis=2)
            Kf = jnp.fft.rfft(K, axis=2)
            corr = jnp.fft.irfft(Qf * jnp.conj(Kf), n=Lloc, axis=2)
            corr_mean = corr.mean(axis=-1)
            top_k = min(max(1, int(FACTOR * math.log(Lloc + 1))), Lloc)
            w, idx = jax.lax.top_k(corr_mean, top_k)
            w = jax.nn.softmax(w, axis=-1)
            ar = jnp.arange(Lloc)
            shifted = (ar[None, None, None, :] + idx[..., None]) % Lloc
            rolled = jnp.take_along_axis(V[:, :, None, :, :], shifted[..., None], axis=3)
            out = jnp.einsum('bhk,bhkld->bhld', w, rolled)
            out = out.transpose(0, 2, 1, 3).reshape(Bq, Lq, d)
            return out @ Wo + bo
        key = jax.random.key(seed)
        ks = jax.random.split(key, 12)
        s = 0.02
        inp = {'query': jax.random.normal(ks[0], (B, L, D_MODEL), dtype=jnp.float32), 'key': jax.random.normal(ks[1], (B, L, D_MODEL), dtype=jnp.float32), 'value': jax.random.normal(ks[2], (B, L, D_MODEL), dtype=jnp.float32), 'Wq': jax.random.normal(ks[3], (D_MODEL, D_MODEL), dtype=jnp.float32) * s, 'bq': jnp.zeros((D_MODEL,), dtype=jnp.float32), 'Wk': jax.random.normal(ks[4], (D_MODEL, D_MODEL), dtype=jnp.float32) * s, 'bk': jnp.zeros((D_MODEL,), dtype=jnp.float32), 'Wv': jax.random.normal(ks[5], (D_MODEL, D_MODEL), dtype=jnp.float32) * s, 'bv': jnp.zeros((D_MODEL,), dtype=jnp.float32), 'Wo': jax.random.normal(ks[6], (D_MODEL, D_MODEL), dtype=jnp.float32) * s, 'bo': jnp.zeros((D_MODEL,), dtype=jnp.float32)}
        return inp
    _L1_xattn_all = _L1_xattn_setup()
    _L1_xattn_in = {k: v for k, v in _L1_xattn_all.items() if k in ('Wq', 'bq', 'Wk', 'bk', 'Wv', 'bv', 'Wo', 'bo')}
    del _L1_xattn_all

    def _L1_ffn_setup():
        import jax, jax.numpy as jnp
        import numpy as np
        H = 256
        I = 1024
        E = 4
        LN_EPS = 1e-12

        def _layer_norm(x, gamma, beta, eps=LN_EPS):
            mu = jnp.mean(x, axis=-1, keepdims=True)
            var = jnp.mean(jnp.square(x - mu), axis=-1, keepdims=True)
            return (x - mu) * jax.lax.rsqrt(var + eps) * gamma + beta
        key = jax.random.key(seed)
        ks = jax.random.split(key, 8)
        B, S = (4, 128)
        scale = 0.02
        return {'hidden_states': jax.random.normal(ks[0], (B, S, H), jnp.float32), 'W_router': jax.random.normal(ks[1], (H, E), jnp.float32) * scale, 'W1': jax.random.normal(ks[2], (E, H, I), jnp.float32) * scale, 'b1': jax.random.normal(ks[3], (E, I), jnp.float32) * scale, 'Wo': jax.random.normal(ks[4], (I, H), jnp.float32) * scale, 'bo': jax.random.normal(ks[5], (H,), jnp.float32) * scale, 'ln_gamma': jnp.ones((H,), jnp.float32), 'ln_beta': jnp.zeros((H,), jnp.float32)}
    _L1_ffn_all = _L1_ffn_setup()
    _L1_ffn_in = {k: v for k, v in _L1_ffn_all.items() if k in ('W_router', 'W1', 'b1', 'Wo', 'bo', 'ln_gamma', 'ln_beta')}
    del _L1_ffn_all

    def _L2_xattn_setup():
        import jax, jax.numpy as jnp
        import numpy as np
        EMBED_DIM = 256
        NUM_HEADS = 16
        HEAD_DIM = EMBED_DIM // NUM_HEADS
        key = jax.random.key(seed)
        ks = jax.random.split(key, 7)
        B, S, E = (2, 512, EMBED_DIM)
        bound = float(np.sqrt(6.0 / (E + E)))
        mkw = lambda k: jax.random.uniform(k, (E, E), jnp.float32, -bound, bound)
        return {'query': jax.random.normal(ks[0], (B, S, E), jnp.float32), 'key': jax.random.normal(ks[1], (B, S, E), jnp.float32), 'value': jax.random.normal(ks[2], (B, S, E), jnp.float32), 'Wq': mkw(ks[3]), 'Wk': mkw(ks[4]), 'Wv': mkw(ks[5]), 'Wo': mkw(ks[6])}
    _L2_xattn_all = _L2_xattn_setup()
    _L2_xattn_in = {k: v for k, v in _L2_xattn_all.items() if k in ('Wq', 'Wk', 'Wv', 'Wo')}
    del _L2_xattn_all

    def _L2_ffn_setup():
        import jax, jax.numpy as jnp
        import numpy as np
        B, T, C, H, E, K = (4, 256, 256, 256, 8, 2)

        def _swiglu(x):
            a, b = jnp.split(x, 2, axis=-1)
            return jax.nn.silu(a) * b
        key = jax.random.key(seed)
        ks = jax.random.split(key, 6)
        s = 0.02
        x = jax.random.normal(ks[0], (B, T, C), jnp.float32)
        w_shared_in = jax.random.normal(ks[1], (C, 2 * H), jnp.float32) * s
        w_shared_out = jax.random.normal(ks[2], (H, C), jnp.float32) * s
        w1_shared = jax.random.normal(ks[3], (C, 2 * H), jnp.float32) * s
        w2 = jax.random.normal(ks[4], (E, H, C), jnp.float32) * s
        w_gate = jax.random.normal(ks[5], (C, E), jnp.float32) * s
        gate_bias = jnp.zeros((E,), jnp.float32)
        return {'x': x, 'w_shared_in': w_shared_in, 'w_shared_out': w_shared_out, 'w1_shared': w1_shared, 'w2': w2, 'w_gate': w_gate, 'gate_bias': gate_bias}
    _L2_ffn_all = _L2_ffn_setup()
    _L2_ffn_in = {k: v for k, v in _L2_ffn_all.items() if k in ('w_shared_in', 'w_shared_out', 'w1_shared', 'w2', 'w_gate', 'gate_bias')}
    del _L2_ffn_all

    def _L3_xattn_setup():
        import jax, jax.numpy as jnp
        import numpy as np
        HIDDEN = 256
        NUM_HEADS = 16
        HEAD_DIM = HIDDEN // NUM_HEADS
        SCALE = 1.0 / float(np.sqrt(HEAD_DIM))
        key = jax.random.key(seed)
        ks = jax.random.split(key, 10)
        B, SQ, SKV = (2, 512, 1024)
        init = 0.02
        return {'query_states': jax.random.normal(ks[0], (B, SQ, HIDDEN), dtype=jnp.float32), 'key_value_states': jax.random.normal(ks[1], (B, SKV, HIDDEN), dtype=jnp.float32), 'Wq': jax.random.normal(ks[2], (HIDDEN, HIDDEN), dtype=jnp.float32) * init, 'bq': jnp.zeros((HIDDEN,), dtype=jnp.float32), 'Wk': jax.random.normal(ks[3], (HIDDEN, HIDDEN), dtype=jnp.float32) * init, 'bk': jnp.zeros((HIDDEN,), dtype=jnp.float32), 'Wv': jax.random.normal(ks[4], (HIDDEN, HIDDEN), dtype=jnp.float32) * init, 'bv': jnp.zeros((HIDDEN,), dtype=jnp.float32), 'Wo': jax.random.normal(ks[5], (HIDDEN, HIDDEN), dtype=jnp.float32) * init, 'bo': jnp.zeros((HIDDEN,), dtype=jnp.float32)}
    _L3_xattn_all = _L3_xattn_setup()
    _L3_xattn_in = {k: v for k, v in _L3_xattn_all.items() if k in ('Wq', 'bq', 'Wk', 'bk', 'Wv', 'bv', 'Wo', 'bo')}
    del _L3_xattn_all

    def _L3_ffn_setup():
        import jax, jax.numpy as jnp
        import numpy as np
        H = 256
        RH = 128
        E = 16
        B, S = (4, 512)
        TEMP = 1.0
        key = jax.random.key(seed)
        ks = jax.random.split(key, 12)
        sc = lambda fan_in: 1.0 / np.sqrt(fan_in)
        return {'hidden_states': jax.random.normal(ks[0], (B, S, H), dtype=jnp.float32), 'W1': jax.random.uniform(ks[1], (H, RH), jnp.float32, -sc(H), sc(H)), 'b1': jax.random.uniform(ks[2], (RH,), jnp.float32, -sc(H), sc(H)), 'W2': jax.random.uniform(ks[3], (RH, E), jnp.float32, -sc(RH), sc(RH)), 'b2': jax.random.uniform(ks[4], (E,), jnp.float32, -sc(RH), sc(RH)), 'Wg1': jax.random.uniform(ks[5], (H, RH), jnp.float32, -sc(H), sc(H)), 'bg1': jax.random.uniform(ks[6], (RH,), jnp.float32, -sc(H), sc(H)), 'Wg2': jax.random.uniform(ks[7], (RH, 1), jnp.float32, -sc(RH), sc(RH)), 'bg2': jax.random.uniform(ks[8], (1,), jnp.float32, -sc(RH), sc(RH)), 'expert_scales': jax.random.normal(ks[9], (E, H), dtype=jnp.float32), 'expert_biases': jax.random.normal(ks[10], (E, H), dtype=jnp.float32)}
    _L3_ffn_all = _L3_ffn_setup()
    _L3_ffn_in = {k: v for k, v in _L3_ffn_all.items() if k in ('W1', 'b1', 'W2', 'b2', 'Wg1', 'bg1', 'Wg2', 'bg2', 'expert_scales', 'expert_biases')}
    del _L3_ffn_all
    return {'x': x, 'ctx_1024': ctx_1024, 'L0_xattn_wq_w': _L0_xattn_in['wq_w'], 'L0_xattn_wk_w': _L0_xattn_in['wk_w'], 'L0_xattn_wv_w': _L0_xattn_in['wv_w'], 'L0_xattn_dense_w': _L0_xattn_in['dense_w'], 'L0_xattn_wq_b': _L0_xattn_in['wq_b'], 'L0_xattn_wk_b': _L0_xattn_in['wk_b'], 'L0_xattn_wv_b': _L0_xattn_in['wv_b'], 'L0_xattn_dense_b': _L0_xattn_in['dense_b'], 'L0_ffn_Wg': _L0_ffn_in['Wg'], 'L0_ffn_We': _L0_ffn_in['We'], 'L0_ffn_be': _L0_ffn_in['be'], 'L1_xattn_Wq': _L1_xattn_in['Wq'], 'L1_xattn_bq': _L1_xattn_in['bq'], 'L1_xattn_Wk': _L1_xattn_in['Wk'], 'L1_xattn_bk': _L1_xattn_in['bk'], 'L1_xattn_Wv': _L1_xattn_in['Wv'], 'L1_xattn_bv': _L1_xattn_in['bv'], 'L1_xattn_Wo': _L1_xattn_in['Wo'], 'L1_xattn_bo': _L1_xattn_in['bo'], 'L1_ffn_W_router': _L1_ffn_in['W_router'], 'L1_ffn_W1': _L1_ffn_in['W1'], 'L1_ffn_b1': _L1_ffn_in['b1'], 'L1_ffn_Wo': _L1_ffn_in['Wo'], 'L1_ffn_bo': _L1_ffn_in['bo'], 'L1_ffn_ln_gamma': _L1_ffn_in['ln_gamma'], 'L1_ffn_ln_beta': _L1_ffn_in['ln_beta'], 'L2_xattn_Wq': _L2_xattn_in['Wq'], 'L2_xattn_Wk': _L2_xattn_in['Wk'], 'L2_xattn_Wv': _L2_xattn_in['Wv'], 'L2_xattn_Wo': _L2_xattn_in['Wo'], 'L2_ffn_w_shared_in': _L2_ffn_in['w_shared_in'], 'L2_ffn_w_shared_out': _L2_ffn_in['w_shared_out'], 'L2_ffn_w1_shared': _L2_ffn_in['w1_shared'], 'L2_ffn_w2': _L2_ffn_in['w2'], 'L2_ffn_w_gate': _L2_ffn_in['w_gate'], 'L2_ffn_gate_bias': _L2_ffn_in['gate_bias'], 'L3_xattn_Wq': _L3_xattn_in['Wq'], 'L3_xattn_bq': _L3_xattn_in['bq'], 'L3_xattn_Wk': _L3_xattn_in['Wk'], 'L3_xattn_bk': _L3_xattn_in['bk'], 'L3_xattn_Wv': _L3_xattn_in['Wv'], 'L3_xattn_bv': _L3_xattn_in['bv'], 'L3_xattn_Wo': _L3_xattn_in['Wo'], 'L3_xattn_bo': _L3_xattn_in['bo'], 'L3_ffn_W1': _L3_ffn_in['W1'], 'L3_ffn_b1': _L3_ffn_in['b1'], 'L3_ffn_W2': _L3_ffn_in['W2'], 'L3_ffn_b2': _L3_ffn_in['b2'], 'L3_ffn_Wg1': _L3_ffn_in['Wg1'], 'L3_ffn_bg1': _L3_ffn_in['bg1'], 'L3_ffn_Wg2': _L3_ffn_in['Wg2'], 'L3_ffn_bg2': _L3_ffn_in['bg2'], 'L3_ffn_expert_scales': _L3_ffn_in['expert_scales'], 'L3_ffn_expert_biases': _L3_ffn_in['expert_biases']}

def reference(x, ctx_1024, L0_xattn_wq_w, L0_xattn_wk_w, L0_xattn_wv_w, L0_xattn_dense_w, L0_xattn_wq_b, L0_xattn_wk_b, L0_xattn_wv_b, L0_xattn_dense_b, L0_ffn_Wg, L0_ffn_We, L0_ffn_be, L1_xattn_Wq, L1_xattn_bq, L1_xattn_Wk, L1_xattn_bk, L1_xattn_Wv, L1_xattn_bv, L1_xattn_Wo, L1_xattn_bo, L1_ffn_W_router, L1_ffn_W1, L1_ffn_b1, L1_ffn_Wo, L1_ffn_bo, L1_ffn_ln_gamma, L1_ffn_ln_beta, L2_xattn_Wq, L2_xattn_Wk, L2_xattn_Wv, L2_xattn_Wo, L2_ffn_w_shared_in, L2_ffn_w_shared_out, L2_ffn_w1_shared, L2_ffn_w2, L2_ffn_w_gate, L2_ffn_gate_bias, L3_xattn_Wq, L3_xattn_bq, L3_xattn_Wk, L3_xattn_bk, L3_xattn_Wv, L3_xattn_bv, L3_xattn_Wo, L3_xattn_bo, L3_ffn_W1, L3_ffn_b1, L3_ffn_W2, L3_ffn_b2, L3_ffn_Wg1, L3_ffn_bg1, L3_ffn_Wg2, L3_ffn_bg2, L3_ffn_expert_scales, L3_ffn_expert_biases):
    import jax
    import jax.numpy as jnp

    def _L0_xattn_ref(query, value, wq_w, wk_w, wv_w, dense_w, wq_b, wk_b, wv_b, dense_b):
        import jax, jax.numpy as jnp
        import numpy as np
        D_MODEL = 256
        NUM_HEADS = 16
        DEPTH = D_MODEL // NUM_HEADS
        B, LQ, LKV = (4, 256, 512)

        def _xavier(key, shape):
            fan_in, fan_out = (shape[1], shape[0])
            limit = float(np.sqrt(6.0 / (fan_in + fan_out)))
            return jax.random.uniform(key, shape, jnp.float32, -limit, limit)

        def _split_heads(x, b):
            return x.reshape(b, -1, NUM_HEADS, DEPTH).transpose(0, 2, 1, 3)
        b = query.shape[0]
        q = query @ wq_w.T + wq_b
        k = value @ wk_w.T + wk_b
        v = value @ wv_w.T + wv_b
        q = _split_heads(q, b)
        k = _split_heads(k, b)
        v = _split_heads(v, b)
        scale = jnp.sqrt(jnp.asarray(DEPTH, q.dtype))
        scores = jnp.einsum('bhqd,bhkd->bhqk', q, k) / scale
        attn = jax.nn.softmax(scores, axis=-1)
        ctx = jnp.einsum('bhqk,bhkd->bhqd', attn, v)
        ctx = ctx.transpose(0, 2, 1, 3).reshape(b, -1, D_MODEL)
        return ctx @ dense_w.T + dense_b

    def _L0_ffn_ref(x, Wg, We, be):
        import jax, jax.numpy as jnp
        import numpy as np
        B, S, D = x.shape
        E = Wg.shape[1]
        T = B * S
        xf = x.reshape(T, D)
        gates = jax.nn.softmax(xf @ Wg, axis=-1)
        top_g, top_i = jax.lax.top_k(gates, 2)
        top_g = top_g / jnp.sum(top_g, axis=-1, keepdims=True)
        tok = jnp.arange(T)
        dispatch = jnp.zeros((E, T), dtype=gates.dtype)
        for i in range(2):
            dispatch = dispatch.at[top_i[:, i], tok].add(top_g[:, i])
        y = jnp.einsum('td,edh->eth', xf, We) + be[:, None, :]
        out = jnp.einsum('et,eth->th', dispatch, y)
        return out.reshape(B, S, -1)

    def _L1_xattn_ref(query, key, value, Wq, bq, Wk, bk, Wv, bv, Wo, bo):
        import jax, jax.numpy as jnp
        import numpy as np
        import math
        D_MODEL = 256
        NHEAD = 16
        FACTOR = 1
        B, L = (2, 1024)

        def _autocorr_forward(query, key, value, Wq, bq, Wk, bk, Wv, bv, Wo, bo):
            Bq, Lq, d = query.shape
            Lk = key.shape[1]
            H = NHEAD
            Dk = d // H
            Q = (query @ Wq + bq).reshape(Bq, Lq, H, Dk).transpose(0, 2, 1, 3)
            K = (key @ Wk + bk).reshape(Bq, Lk, H, Dk).transpose(0, 2, 1, 3)
            V = (value @ Wv + bv).reshape(Bq, Lk, H, Dk).transpose(0, 2, 1, 3)
            if Lk > Lq:
                K = K[:, :, :Lq, :]
                V = V[:, :, :Lq, :]
            elif Lq > Lk:
                pad = [(0, 0), (0, 0), (0, Lq - Lk), (0, 0)]
                K = jnp.pad(K, pad)
                V = jnp.pad(V, pad)
            Lloc = Lq
            Qf = jnp.fft.rfft(Q, axis=2)
            Kf = jnp.fft.rfft(K, axis=2)
            corr = jnp.fft.irfft(Qf * jnp.conj(Kf), n=Lloc, axis=2)
            corr_mean = corr.mean(axis=-1)
            top_k = min(max(1, int(FACTOR * math.log(Lloc + 1))), Lloc)
            w, idx = jax.lax.top_k(corr_mean, top_k)
            w = jax.nn.softmax(w, axis=-1)
            ar = jnp.arange(Lloc)
            shifted = (ar[None, None, None, :] + idx[..., None]) % Lloc
            rolled = jnp.take_along_axis(V[:, :, None, :, :], shifted[..., None], axis=3)
            out = jnp.einsum('bhk,bhkld->bhld', w, rolled)
            out = out.transpose(0, 2, 1, 3).reshape(Bq, Lq, d)
            return out @ Wo + bo
        return _autocorr_forward(query, key, value, Wq, bq, Wk, bk, Wv, bv, Wo, bo)

    def _L1_ffn_ref(hidden_states, W_router, W1, b1, Wo, bo, ln_gamma, ln_beta):
        import jax, jax.numpy as jnp
        import numpy as np
        H = 256
        I = 1024
        E = 4
        LN_EPS = 1e-12

        def _layer_norm(x, gamma, beta, eps=LN_EPS):
            mu = jnp.mean(x, axis=-1, keepdims=True)
            var = jnp.mean(jnp.square(x - mu), axis=-1, keepdims=True)
            return (x - mu) * jax.lax.rsqrt(var + eps) * gamma + beta
        B, S, _ = hidden_states.shape
        x = hidden_states.reshape(-1, H)
        logits = x @ W_router
        expert_idx = jnp.argmax(logits, axis=-1)
        h = jnp.einsum('th,ehi->tei', x, W1) + b1
        h = jax.nn.gelu(h, approximate=False)
        onehot = jax.nn.one_hot(expert_idx, E, dtype=x.dtype)
        intermediate = jnp.einsum('te,tei->ti', onehot, h)
        y = intermediate @ Wo + bo + x
        y = _layer_norm(y, ln_gamma, ln_beta)
        return y.reshape(B, S, H)

    def _L2_xattn_ref(query, key, value, Wq, Wk, Wv, Wo):
        import jax, jax.numpy as jnp
        import numpy as np
        EMBED_DIM = 256
        NUM_HEADS = 16
        HEAD_DIM = EMBED_DIM // NUM_HEADS
        B, L, E = query.shape
        H, D = (NUM_HEADS, HEAD_DIM)
        scale = D ** (-0.5)
        q = (query @ Wq.T).reshape(B, L, H, D) * scale
        k = (key @ Wk.T).reshape(B, -1, H, D)
        v = (value @ Wv.T).reshape(B, -1, H, D)
        scores = jax.nn.sigmoid(jnp.einsum('blhd,bshd->bhls', q, k))
        o = jnp.einsum('bhls,bshd->blhd', scores, v).reshape(B, L, E)
        return o @ Wo.T

    def _L2_ffn_ref(x, w_shared_in, w_shared_out, w1_shared, w2, w_gate, gate_bias):
        import jax, jax.numpy as jnp
        import numpy as np
        B, T, C, H, E, K = (4, 256, 256, 256, 8, 2)

        def _swiglu(x):
            a, b = jnp.split(x, 2, axis=-1)
            return jax.nn.silu(a) * b
        Bx, Tx, Cx = x.shape
        S = Bx * Tx
        fx = x.reshape(S, Cx)
        shared_out = _swiglu(fx @ w_shared_in) @ w_shared_out
        logits = fx @ w_gate + gate_bias
        probs = jax.nn.softmax(logits, axis=-1)
        top_val, top_idx = jax.lax.top_k(probs, K)
        wdense = jnp.zeros((S, E), probs.dtype).at[jnp.arange(S)[:, None], top_idx].add(top_val)
        hid = _swiglu(fx @ w1_shared)
        routed_out = jnp.zeros_like(shared_out)
        for e in range(E):
            routed_out = routed_out + wdense[:, e:e + 1] * (hid @ w2[e])
        return (shared_out + routed_out).reshape(Bx, Tx, Cx)

    def _L3_xattn_ref(query_states, key_value_states, Wq, bq, Wk, bk, Wv, bv, Wo, bo):
        import jax, jax.numpy as jnp
        import numpy as np
        HIDDEN = 256
        NUM_HEADS = 16
        HEAD_DIM = HIDDEN // NUM_HEADS
        SCALE = 1.0 / float(np.sqrt(HEAD_DIM))
        B, SQ, _ = query_states.shape
        _, SKV, _ = key_value_states.shape
        q = query_states @ Wq.T + bq
        k = key_value_states @ Wk.T + bk
        v = key_value_states @ Wv.T + bv
        q = q.reshape(B, SQ, NUM_HEADS, HEAD_DIM).transpose(0, 2, 1, 3) * SCALE
        k = k.reshape(B, SKV, NUM_HEADS, HEAD_DIM).transpose(0, 2, 1, 3)
        v = v.reshape(B, SKV, NUM_HEADS, HEAD_DIM).transpose(0, 2, 1, 3)
        scores = jnp.einsum('bhqd,bhkd->bhqk', q, k)
        attn = jax.nn.softmax(scores, axis=-1)
        ctx = jnp.einsum('bhqk,bhkd->bhqd', attn, v)
        ctx = ctx.transpose(0, 2, 1, 3).reshape(B, SQ, HIDDEN)
        return ctx @ Wo.T + bo

    def _L3_ffn_ref(hidden_states, W1, b1, W2, b2, Wg1, bg1, Wg2, bg2, expert_scales, expert_biases):
        import jax, jax.numpy as jnp
        import numpy as np
        H = 256
        RH = 128
        E = 16
        B, S = (4, 512)
        TEMP = 1.0
        b, s, h = hidden_states.shape
        flat = hidden_states.reshape(-1, h)
        routing_scores = jax.nn.relu(flat @ W1 + b1) @ W2 + b2
        routing_scores = routing_scores / TEMP
        gate = jax.nn.sigmoid(jnp.tanh(flat @ Wg1 + bg1) @ Wg2 + bg2)
        routing_scores = routing_scores * gate
        expert_probs = jax.nn.softmax(routing_scores, axis=-1)
        top_idx = jnp.argmax(expert_probs, axis=-1)
        scales = expert_scales[top_idx]
        biases = expert_biases[top_idx]
        routed = flat * scales + biases
        return routed.reshape(b, s, h)
    x = x + _L0_xattn_ref(_layernorm(x, axis=-1), ctx_1024, L0_xattn_wq_w, L0_xattn_wk_w, L0_xattn_wv_w, L0_xattn_dense_w, L0_xattn_wq_b, L0_xattn_wk_b, L0_xattn_wv_b, L0_xattn_dense_b)
    x = x + _L0_ffn_ref(_layernorm(x, axis=-1), L0_ffn_Wg, L0_ffn_We, L0_ffn_be)
    x = x + _L1_xattn_ref(_layernorm(x, axis=-1), ctx_1024, ctx_1024, L1_xattn_Wq, L1_xattn_bq, L1_xattn_Wk, L1_xattn_bk, L1_xattn_Wv, L1_xattn_bv, L1_xattn_Wo, L1_xattn_bo)
    x = x + _L1_ffn_ref(_layernorm(x, axis=-1), L1_ffn_W_router, L1_ffn_W1, L1_ffn_b1, L1_ffn_Wo, L1_ffn_bo, L1_ffn_ln_gamma, L1_ffn_ln_beta)
    x = x + _L2_xattn_ref(_layernorm(x, axis=-1), ctx_1024, ctx_1024, L2_xattn_Wq, L2_xattn_Wk, L2_xattn_Wv, L2_xattn_Wo)
    x = x + _L2_ffn_ref(_layernorm(x, axis=-1), L2_ffn_w_shared_in, L2_ffn_w_shared_out, L2_ffn_w1_shared, L2_ffn_w2, L2_ffn_w_gate, L2_ffn_gate_bias)
    x = x + _L3_xattn_ref(_layernorm(x, axis=-1), ctx_1024, L3_xattn_Wq, L3_xattn_bq, L3_xattn_Wk, L3_xattn_bk, L3_xattn_Wv, L3_xattn_bv, L3_xattn_Wo, L3_xattn_bo)
    x = x + _L3_ffn_ref(_layernorm(x, axis=-1), L3_ffn_W1, L3_ffn_b1, L3_ffn_W2, L3_ffn_b2, L3_ffn_Wg1, L3_ffn_bg1, L3_ffn_Wg2, L3_ffn_bg2, L3_ffn_expert_scales, L3_ffn_expert_biases)
    return x

_drawn_inputs = setup_inputs


def setup_inputs(seed=0):
    import zlib

    import numpy as np

    out = dict(_drawn_inputs(seed))
    spreads = {'L0_xattn_wq_b': (0.0, 0.471),
     'L0_xattn_wk_b': (0.0, 2.0),
     'L0_xattn_wv_b': (0.0, 0.1),
     'L0_xattn_dense_b': (0.0, 0.1),
     'L0_ffn_be': (0.0, 0.581),
     'L1_xattn_bq': (0.0, 2.0),
     'L1_xattn_bk': (0.0, 2.0),
     'L1_xattn_bv': (0.0, 0.8),
     'L1_xattn_bo': (0.0, 0.462),
     'L1_ffn_ln_gamma': (1.0, 0.6),
     'L1_ffn_ln_beta': (0.0, 0.772),
     'L2_ffn_gate_bias': (0.0, 2.0),
     'L3_xattn_bq': (0.0, 2.0),
     'L3_xattn_bk': (0.0, 2.0),
     'L3_xattn_bv': (0.0, 2.0),
     'L3_xattn_bo': (0.0, 2.0)}
    factors = {'L1_xattn_Wq': 8.0,
     'L1_xattn_Wk': 8.0,
     'L1_xattn_Wv': 4.946,
     'L1_xattn_Wo': 4.524,
     'L1_ffn_W_router': 5.816,
     'L1_ffn_W1': 4.952,
     'L1_ffn_b1': 42.783,
     'L1_ffn_Wo': 4.951,
     'L1_ffn_bo': 64.0,
     'L2_ffn_w_shared_in': 8.0,
     'L2_ffn_w_shared_out': 8.0,
     'L2_ffn_w1_shared': 22.336,
     'L2_ffn_w2': 24.984,
     'L2_ffn_w_gate': 25.641,
     'L3_xattn_Wq': 27.666,
     'L3_xattn_Wk': 28.54,
     'L3_xattn_Wv': 24.94,
     'L3_xattn_Wo': 24.106,
     'L3_ffn_W1': 25.665,
     'L3_ffn_b1': 64.0,
     'L3_ffn_W2': 8.0,
     'L3_ffn_b2': 200.0,
     'L3_ffn_expert_scales': 23.606,
     'L3_ffn_expert_biases': 24.859}
    for name, (base, spread) in spreads.items():
        noise = np.random.default_rng([zlib.crc32(name.encode()), seed]).standard_normal(out[name].shape)
        drawn = base * np.exp(spread * noise) if base else spread * noise
        out[name] = jnp.asarray(drawn.astype(out[name].dtype))
    for name, factor in factors.items():
        out[name] = (out[name] * factor).astype(out[name].dtype)
    return out
```

```python
from contextlib import ExitStack

import numpy as np
import concourse.bass as bass
from concourse import mybir

F32 = mybir.dt.float32
BF16 = mybir.dt.bfloat16
U32 = mybir.dt.uint32
ALU = mybir.AluOpType
ACT = mybir.ActivationFunctionType
AX = mybir.AxisListType

P = 128
BATCH, SEQ, DM = 4, 512, 256
CTX = 1601
HEADS, DH = 16, 16
TOK = BATCH * SEQ
TILES = TOK // P
KC = DM // P
BANK = 512
LN_EPS = 1e-5

GROUP = 4
GROUPS = HEADS // GROUP
KEY_CHUNKS = [(k, min(P, CTX - k)) for k in range(0, CTX, P)]
KEY_BLOCKS = [(k, min(BANK, CTX - k)) for k in range(0, CTX, BANK)]
MAX_SPLIT = 4
MAX_BLOCKS = [(CTX * i // MAX_SPLIT, CTX * (i + 1) // MAX_SPLIT - CTX * i // MAX_SPLIT) for i in range(MAX_SPLIT)]
K_PART = [0, 1, 2, 0, 1, 2, 0]
Q_PART = [0, 0, 0, 1, 1, 1, 2]
PAIR_ROWS = DH * len(K_PART)
MAX_ROWS = 3
STACK = PAIR_ROWS + MAX_ROWS
VW = DH + 1


class Count:

    def __init__(self, sem):
        self.sem, self.n = sem, 0


def flat(needs):
    for t in needs:
        if isinstance(t, list):
            yield from flat(t)
        elif t is not None:
            yield t


class Queue:

    def __init__(self, engine, done):
        self.engine, self.done, self.items, self.passed = engine, done, [], {}

    def __call__(self, emit, *needs, done=None, by=1, signal=True):
        most = {}
        for count, value in flat(needs):
            most[count] = max(value, most.get(count, 0))
        waits = [(c, v) for c, v in most.items() if self.passed.get(c, 0) < v]
        self.passed.update(waits)
        count = (done or self.done) if signal else None
        if count:
            count.n += by
        self.items.append((waits, emit, count, by))
        return (count, count.n) if count else None

    def run(self, eng):
        for waits, emit, count, by in self.items:
            for c, v in waits:
                eng.wait_ge(c.sem, v)
            ins = emit(eng)
            if count:
                ins.then_inc(count.sem, by)


class Slot:

    def __init__(self, ap, count=None):
        self.ap, self.free, self.count = ap, [], count


class Ring:
    def __init__(self, slots):
        self.slots, self.at = slots, -1

    def next(self):
        self.at += 1
        return self.slots[self.at % len(self.slots)]


def build(nc, I, out, stop=99):
    with ExitStack() as top:
        sem_n = [0]

        def new_count(name):
            sem_n[0] += 1
            return Count(top.enter_context(nc.semaphore(f"{name}_{sem_n[0]}")))

        pe = Queue("tensor", new_count("pe_done"))
        dve = Queue("vector", new_count("dve_done"))
        act = Queue("scalar", new_count("act_done"))
        pool = Queue("gpsimd", new_count("pool_done"))
        sp = Queue("sync", None)
        compute = [pe, dve, act, pool]
        dma_counts = []

        def dma_count(name):
            c = new_count(name)
            dma_counts.append(c)
            return c

        def load(count, dst, src, *needs):
            return sp(lambda e: e.dma_start(dst, src), *needs, done=count, by=16)

        def fence():
            return [(q.done, q.done.n) for q in compute if q.done.n] + [(c, c.n) for c in dma_counts if c.n]

        def sbuf(scope, name, shape, dt=F32):
            sem_n[0] += 1
            return scope.enter_context(nc.sbuf_tensor(f"{name}_{sem_n[0]}", shape, dt))

        def scratch(name, shape, dt):
            return nc.dram_tensor(name, shape, dt, kind="Internal").ap()

        x = sbuf(top, "x", [P, TILES, DM])
        hT = sbuf(top, "hT", [P, KC, TOK])
        ident = sbuf(top, "ident", [P, P])
        identb = sbuf(top, "identb", [P, P], BF16)
        sel_den = sbuf(top, "sel_den", [P, GROUP])
        stats = sbuf(top, "stats", [P, TILES, 6])
        meanvar = sbuf(top, "meanvar", [P, TILES, 2])
        veps = sbuf(top, "veps", [P, TILES])
        rstd = sbuf(top, "rstd", [P, TILES])
        ntmp = sbuf(top, "ntmp", [P, TILES])
        psum = top.enter_context(nc.psum_tensor("psum", [P, 8, BANK], F32))
        banks = [Slot(psum[:, i, :]) for i in range(8)]

        def mm(dst, pairs, *needs, tile_position=None):
            for i, (lhsT, rhs) in enumerate(pairs):
                first, last = i == 0, i == len(pairs) - 1

                def emit(e, lhsT=lhsT, rhs=rhs, first=first, last=last):
                    if tile_position is None:
                        return e.matmul(dst, lhsT, rhs, start=first, stop=last)
                    return e.matmul(dst, lhsT, rhs, start=first, stop=last, tile_position=tile_position)

                token = pe(emit, *(needs if first else ()), signal=last)
            return token

        x_in = dma_count("x_in")
        x_ready = load(x_in, x[:, :, :], I["x"].rearrange("b s d -> (b s) d").rearrange("(t p) d -> p t d", p=P))
        zero = pool(lambda e: e.memset(ident[:, :], 0.0))
        ident_ready = pool(lambda e: e.affine_select(out=ident[:, :], in_=ident[:, :], compare_op=ALU.not_equal,
                                                     fill=1.0, base=0, pattern=[[-1, P]], channel_multiplier=1), zero)
        identb_ready = pool(lambda e: e.tensor_copy(identb[:, :], ident[:, :]), ident_ready)
        zero = pool(lambda e: e.memset(sel_den[:, :], 0.0))
        sel_ready = pool(lambda e: e.affine_select(out=sel_den[:, :], in_=sel_den[:, :], compare_op=ALU.not_equal,
                                                   fill=1.0, base=-DH, pattern=[[-32, GROUP]], channel_multiplier=1), zero)

        state = {"x": [x_ready]}

        def layer_norm_stats(src, needs, eps):
            for t in range(TILES):
                s = dve(lambda e, t=t: e.bn_stats(stats[:, t, :], src[:, t, :]), needs)
            for t in range(TILES):
                a = dve(lambda e, t=t: e.bn_aggr(meanvar[:, t, :], stats[:, t, :]), s)
            v = dve(lambda e: e.tensor_scalar(veps[:, :], meanvar[:, :, 1], eps, None, ALU.add), a)
            sq = act(lambda e: e.activation(rstd[:, :], veps[:, :], ACT.Sqrt), v)
            r = dve(lambda e: e.reciprocal(rstd[:, :], rstd[:, :]), sq)
            n = dve(lambda e: e.tensor_tensor(ntmp[:, :], rstd[:, :], rstd[:, :], ALU.mult), r)
            n = dve(lambda e: e.tensor_tensor(ntmp[:, :], ntmp[:, :], veps[:, :], ALU.mult), n)
            n = dve(lambda e: e.tensor_scalar(ntmp[:, :], ntmp[:, :], -0.5, 1.5, ALU.mult, ALU.add), n)
            return dve(lambda e: e.tensor_tensor(rstd[:, :], rstd[:, :], ntmp[:, :], ALU.mult), n)

        def normed(dst, src, t, *needs):
            return dve(lambda e: e.tensor_scalar(dst, src, meanvar[:, t, 0:1], rstd[:, t:t + 1],
                                                 ALU.subtract, ALU.mult), *needs)

        def layer_norm(h, start):
            ready = layer_norm_stats(x, [state["x"], start], LN_EPS)
            ring = Ring(banks)
            hs = []
            whole = []
            for g in range(TILES // 4):
                tiles = []
                for t in range(4 * g, 4 * g + 4):
                    tiles.append(normed(h[:, t, :], x[:, t, :], t, ready, start))
                hs += tiles
                for c in range(KC):
                    bank = ring.next()
                    for i in range(4):
                        tr = pe(lambda e, i=i, c=c, g=g, bank=bank: e.transpose(
                            bank.ap[:, i * P:(i + 1) * P], h[:, 4 * g + i, c * P:(c + 1) * P], ident[:, :]),
                            tiles[i], ident_ready, start, bank.free)
                    dst = hT[:, c, g * BANK:(g + 1) * BANK]
                    bank.free = [act(lambda e, dst=dst, bank=bank: e.activation(dst, bank.ap, ACT.Copy), tr, start)]
                whole.append(list(bank.free))
            return hs, whole

        def load_weight(scope, count, name, src, start):
            n_in, n_out = src.shape
            w = sbuf(scope, name, [P, n_in // P, n_out])
            return w, load(count, w[:, :, :], src.rearrange("(k p) n -> p k n", p=P), start)

        def load_columns(scope, count, name, src, start):
            n = src.shape[0]
            w = sbuf(scope, name, [P, n // P])
            return w, sp(lambda e: e.dma_start(w[:, :], src.rearrange("(k p) -> p k", p=P),
                                               allow_slow_non_contiguous=True), start, done=count, by=16)

        def load_rows(scope, count, name, src, start):
            n = src.shape[0]
            w = sbuf(scope, name, [P, n])
            return w, load(count, w[:, :], src.rearrange("(a n) -> a n", a=1).partition_broadcast(P), start)

        k_parts_dram = scratch("k_parts_dram", [2, HEADS, 3 * DH, CTX], BF16)
        q_parts_dram = scratch("q_parts_dram", [2, HEADS, PAIR_ROWS, SEQ], BF16)

        def attention(tag, softmax, biased):
            start = fence()
            with ExitStack() as sc:
                W = dma_count(f"{tag}_weights")
                wk, _ = load_weight(sc, W, "wk", I[f"{tag}_wk"], start)
                wq, _ = load_weight(sc, W, "wq", I[f"{tag}_wq"], start)
                wv, _ = load_weight(sc, W, "wv", I[f"{tag}_wv"], start)
                wo = sbuf(sc, "wo", [P, GROUPS, DM])
                wo_zero = pool(lambda e: e.memset(wo[:, :, :], 0.0), start)
                wo_src = I[f"{tag}_wo"].rearrange("(g j d) n -> j d g n", g=GROUPS, j=GROUP)
                for j in range(GROUP):
                    w_ready = load(W, wo[32 * j:32 * j + DH, :, :], wo_src[j], wo_zero)
                if biased:
                    bk, _ = load_columns(sc, W, "bk", I[f"{tag}_bk"], start)
                    bq, _ = load_columns(sc, W, "bq", I[f"{tag}_bq"], start)
                    bv, _ = load_rows(sc, W, "bv", I[f"{tag}_bv"], start)
                    bo, w_ready = load_rows(sc, W, "bo", I[f"{tag}_bo"], start)
                ctxT = Slot(sbuf(sc, "ctxT", [P, KC, CTX]), dma_count(f"{tag}_ctx"))
                kp = Slot(sbuf(sc, "kp", [P, KC, 3, CTX], BF16))
                kp_stores = [dma_count(f"{tag}_kp{c}") for c in range(KC)]
                qp = Slot(sbuf(sc, "qp", [P, KC, 3, SEQ], BF16), dma_count(f"{tag}_qp"))
                rest = Ring([Slot(sbuf(sc, "rest", [P, BANK])) for _ in range(2)])
                vt = Ring([Slot(sbuf(sc, "vt", [P, len(KEY_CHUNKS), HEADS, VW])) for _ in range(2)])
                kst = [Slot(sbuf(sc, "kst", [P, GROUP, CTX], BF16), dma_count(f"{tag}_kst{i}")) for i in range(3)]
                qst = [Slot(sbuf(sc, "qst", [P, GROUP, SEQ], BF16), dma_count(f"{tag}_qst{i}")) for i in range(3)]
                probs = Ring([Slot(sbuf(sc, "probs", [P, 2 * BANK])) for _ in range(5)])
                accs = Slot(sbuf(sc, "accs", [P, BANK]))
                rsmall = sbuf(sc, "rsmall", [P, 4 * GROUP])
                rden = Slot(sbuf(sc, "rden", [P, 4 * GROUP, 32]))
                ctxn = Slot(sbuf(sc, "ctxn", [P, GROUPS, SEQ]))
                mpart = Slot(sbuf(sc, "mpart", [P, 4 * GROUP, MAX_SPLIT]))
                mrow = sbuf(sc, "mrow", [P, 4 * GROUP])
                mrest = sbuf(sc, "mrest", [P, 4 * GROUP])
                mpb = sbuf(sc, "mpb", [P, MAX_ROWS, 4 * GROUP], BF16)
                mT = Slot(sbuf(sc, "mT", [MAX_ROWS * 4 * GROUP, P], BF16), dma_count(f"{tag}_mT"))

                s_slots = Ring([Slot(psum[:, 0:2, :].rearrange("p a n -> p (a n)")),
                                Slot(psum[:, 2:4, :].rearrange("p a n -> p (a n)"))])
                acc = Slot(psum[:, 4, :])
                m_banks = Ring([Slot(psum[:, 5, :]), Slot(psum[:, 6, :])])
                misc = Ring([Slot(psum[:, 7, :])] + ([] if softmax else [Slot(psum[:, 5, :]), Slot(psum[:, 6, :])]))

                with ExitStack() as hsc:
                    h = ctxn_view = None
                    hrow = [Slot(probs.slots[i].ap[:, :].rearrange("p (t d) -> p t d", d=DM)) for i in range(4)]
                    ready = layer_norm_stats(x, [state["x"], start], LN_EPS)
                    ring = Ring(banks)
                    hT_ready = []
                    for g in range(TILES // 4):
                        tiles = [normed(hrow[g].ap[:, i, :], x[:, 4 * g + i, :], 4 * g + i, ready, start)
                                 for i in range(4)]
                        for c in range(KC):
                            bank = ring.next()
                            for i in range(4):
                                tr = pe(lambda e, i=i, c=c, g=g, bank=bank: e.transpose(
                                    bank.ap[:, i * P:(i + 1) * P], hrow[g].ap[:, i, c * P:(c + 1) * P], ident[:, :]),
                                    tiles[i], ident_ready, start, bank.free)
                            dst = hT[:, c, g * BANK:(g + 1) * BANK]
                            bank.free = [act(lambda e, dst=dst, bank=bank: e.activation(dst, bank.ap, ACT.Copy), tr)]
                        probs.slots[g].free = [tr]
                        hT_ready.append(list(bank.free))
                    ln_read = tiles[-1]
                in_psum = hT_ready[-1]
                for s in s_slots.slots + [acc] + m_banks.slots + misc.slots:
                    s.free = list(in_psum)
                for b in banks:
                    b.free = []

                ones = wo_zero
                for s in kst:
                    ones = pool(lambda e, s=s: e.memset(s.ap[96:P, :, :], 1.0), start, ones)
                    s.free = [ones]
                for s in vt.slots:
                    ones = pool(lambda e, s=s: e.memset(s.ap[:, :, :, DH:VW], 1.0), start, ones)
                    s.free = [ones]
                if biased:
                    bo_rows = bo[:, :].unsqueeze(1).to_broadcast([P, TILES, DM])
                    x_biased = pool(lambda e: e.tensor_tensor(x[:, :, :], x[:, :, :], bo_rows, ALU.add),
                                    ln_read, w_ready, ones)
                    bq_scaled = dve(lambda e: e.tensor_scalar(bq[:, :], bq[:, :], DH ** -0.5, None, ALU.mult), w_ready)
                else:
                    x_biased, bq_scaled = ln_read, None

                acc.free = [dve(lambda e: e.memset(acc.ap, 0.0), acc.free)]
                x_tokens = []

                S = {}

                def load_ctx(b):
                    def step():
                        S["ctx"] = load(ctxT.count, ctxT.ap[:, :, :],
                                        I["ctxT"][:, b, :].rearrange("(k p) s -> p k s", p=P), ctxT.free, start)
                        ctxT.free = []
                    return [step]

                def split(dst, part_slot, bank, n, bias, scale, mmt):
                    r = rest.next()
                    v = r.ap[:, 0:n]
                    if bias is None:
                        r0 = act(lambda e: e.activation(v, bank.ap[:, 0:n], ACT.Copy, scale=scale), mmt, r.free)
                    else:
                        r0 = act(lambda e: e.activation(v, bank.ap[:, 0:n], ACT.Identity, bias=bias, scale=scale),
                                 mmt, r.free, bq_scaled)
                    bank.free = [r0]
                    hi = dve(lambda e: e.tensor_copy(dst(0), v), r0, part_slot.free)
                    r1 = dve(lambda e: e.tensor_tensor(v, v, dst(0), ALU.subtract), hi)
                    mid = dve(lambda e: e.tensor_copy(dst(1), v), r1, part_slot.free)
                    lo = pool(lambda e: e.tensor_tensor(dst(2), v, dst(1), ALU.subtract), mid, part_slot.free)
                    r.free = [lo]
                    return [hi, mid, lo]

                def make_keys(b, c):
                    steps = []
                    for k0, kn in KEY_BLOCKS:
                        def step(k0=k0, kn=kn):
                            bank = misc.next()
                            t = mm(bank.ap[:, 0:kn], [(wk[:, k, c * P:(c + 1) * P], ctxT.ap[:, k, k0:k0 + kn])
                                                      for k in range(KC)], S["ctx"], w_ready, bank.free)
                            ctxT.free.append(t)
                            S.setdefault(("kp", b, c), []).append(split(
                                lambda part: kp.ap[:, c, part, k0:k0 + kn], kp, bank, kn,
                                bk[:, c:c + 1] if biased else None, 1.0, t))
                        steps.append(step)

                    def store():
                        last = None
                        for part in range(3):
                            dst = k_parts_dram[b % 2, 8 * c:8 * c + 8, part * DH:(part + 1) * DH, :]
                            last = load(kp_stores[c], dst, kp.ap[:, c, part, :],
                                        S[("kp", b, c)], S.get(("kst_read", b - 2)))
                        S["k_stored", b, c] = last
                        kp.free = [last] if c == 0 else kp.free + [last]
                    return steps + [store]

                def make_queries(b):
                    steps = []
                    for c in range(KC):
                        def step(c=c):
                            bank = misc.next()
                            t = mm(bank.ap, [(wq[:, k, c * P:(c + 1) * P], hT[:, k, b * SEQ:(b + 1) * SEQ])
                                             for k in range(KC)], hT_ready[b], w_ready, bank.free)
                            S.setdefault(("qp", b), []).append(split(
                                lambda part: qp.ap[:, c, part, :], qp, bank, SEQ,
                                bq[:, c:c + 1] if biased else None, DH ** -0.5, t))
                        steps.append(step)

                    def store():
                        for c in range(KC):
                            for j, part in enumerate(Q_PART):
                                dst = q_parts_dram[b % 2, 8 * c:8 * c + 8, j * DH:(j + 1) * DH, :]
                                last = load(qp.count, dst, qp.ap[:, c, part, :], S[("qp", b)],
                                            S.get(("kst_read", b - 2)))
                        S["q_stored", b] = last
                        qp.free = [last]
                    return steps + [store]

                def make_values(b):
                    slot = vt.slots[b % 2]
                    steps = []
                    for i in range(0, len(KEY_CHUNKS), 2):
                        def step(i=i):
                            bank = misc.next()
                            chunks = KEY_CHUNKS[i:i + 2]
                            for j, (k0, kn) in enumerate(chunks):
                                t = mm(bank.ap[0:kn, j * DM:(j + 1) * DM],
                                       [(ctxT.ap[:, k, k0:k0 + kn], wv[:, k, :]) for k in range(KC)],
                                       S["ctx"], w_ready, bank.free)
                            n = len(chunks)
                            dst = slot.ap[0:kn, i:i + n, :, 0:DH]
                            src = bank.ap[0:kn, 0:n * DM].rearrange("p (c h d) -> p c h d", c=n, d=DH)
                            if biased:
                                rows = bv[0:kn, :].rearrange("p (h d) -> p h d", d=DH).unsqueeze(1)
                                rows = rows.to_broadcast([kn, n, HEADS, DH])
                                e = dve(lambda e: e.tensor_tensor(dst, src, rows, ALU.add), t, slot.free, w_ready)
                            else:
                                e = dve(lambda e: e.tensor_copy(dst, src), t, slot.free)
                            ctxT.free.append(t)
                            bank.free = [e]
                            S["v", b] = [e, slot.free]
                        steps.append(step)
                    return steps

                def load_unit(u):
                    b, g = divmod(u, GROUPS)

                    def step():
                        ks, qs = kst[u % 3], qst[u % 3]
                        stored = [S["k_stored", b, 4 * g // 8], S["q_stored", b]]
                        src = k_parts_dram[b % 2, 4 * g:4 * g + 4, :, :].rearrange("h r t -> r h t")
                        load(ks.count, ks.ap[0:48, :, :], src, stored, ks.free)
                        load(ks.count, ks.ap[48:96, :, :], src, stored, ks.free)
                        t = load(ks.count, ks.ap[96:PAIR_ROWS, :, :], src[0:DH], stored, ks.free)
                        q = load(qs.count, qs.ap[0:PAIR_ROWS, :, :],
                                 q_parts_dram[b % 2, 4 * g:4 * g + 4, :, :].rearrange("h r t -> r h t"),
                                 stored, qs.free)
                        S["unit", u] = [t, q, list(ks.free)]
                        if g == GROUPS - 1:
                            S["kst_read", b] = [t, q]
                    return [step]

                def maxima(u):
                    ks, qs = kst[u % 3], qst[u % 3]
                    steps = []
                    for h in range(GROUP):
                        for qt in range(SEQ // P):
                            def step(h=h, qt=qt):
                                row = h * (SEQ // P) + qt
                                for i, (k0, kn) in enumerate(MAX_BLOCKS):
                                    bank = m_banks.next()
                                    t = mm(bank.ap[:, 0:kn], [(qs.ap[0:PAIR_ROWS, h, qt * P:(qt + 1) * P],
                                                               ks.ap[0:PAIR_ROWS, h, k0:k0 + kn])],
                                           S["unit", u], bank.free)
                                    r = dve(lambda e, bank=bank, kn=kn, i=i: e.tensor_reduce(
                                        mpart.ap[:, row, i:i + 1], bank.ap[:, 0:kn], AX.X, ALU.max), t, mpart.free)
                                    bank.free = [r]
                                S["max", u] = r
                            steps.append(step)

                    def close():
                        t = dve(lambda e: e.tensor_reduce(mrow[:, :], mpart.ap[:, :, :], AX.X, ALU.max), S["max", u])
                        mpart.free = [t]
                        a = dve(lambda e: e.tensor_scalar(mpb[:, 0, :], mrow[:, :], -1.0, None, ALU.mult), t,
                                S.get("mpb_free"))
                        a = dve(lambda e: e.scalar_tensor_tensor(out=mrest[:, :], in0=mrow[:, :], scalar=-1.0,
                                                                 in1=mpb[:, 0, :], op0=ALU.mult, op1=ALU.subtract), a)
                        a = dve(lambda e: e.tensor_copy(mpb[:, 1, :], mrest[:, :]), a)
                        a = dve(lambda e: e.tensor_tensor(mpb[:, 2, :], mrest[:, :], mpb[:, 1, :], ALU.subtract), a)
                        S["mparts", u] = a

                    def turn():
                        bank = misc.next()
                        rows = MAX_ROWS * 4 * GROUP
                        view = bank.ap.bitcast(BF16)[0:rows, 0:P]
                        t = pe(lambda e: e.transpose(view, mpb[:, :, :].rearrange("p a b -> p (a b)"), identb[:, :]),
                               S["mparts", u], identb_ready, bank.free)
                        S["mpb_free"] = t
                        c = act(lambda e: e.activation(mT.ap[:, :], view, ACT.Copy), t, mT.free)
                        bank.free = [c]
                        for i in range(MAX_ROWS):
                            d = load(mT.count, qs.ap[PAIR_ROWS + i:PAIR_ROWS + i + 1, :, :]
                                     .rearrange("p h (a q) -> p (h a) q", q=P),
                                     mT.ap[i * 4 * GROUP:(i + 1) * 4 * GROUP, :], c, qs.free, S["unit", u])
                        mT.free = [d]
                        S["maxrows", u] = d
                    return steps + [close, turn]

                def finish(u):
                    b, g = divmod(u, GROUPS)

                    def evacuate():
                        if softmax:
                            t = dve(lambda e: e.tensor_copy(accs.ap[:, :], acc.ap), S["acc", u], accs.free)
                        else:
                            t = dve(lambda e: e.tensor_copy(ctxn.ap[:, g, :], acc.ap), S["acc", u], ctxn.free)
                            S["ctxn", b] = t
                        acc.free = [t]
                        S["accs", u] = t

                    def denominators():
                        bank = misc.next()
                        for qt in range(SEQ // P):
                            t = mm(bank.ap[:, qt * GROUP:(qt + 1) * GROUP],
                                   [(accs.ap[:, qt * P:(qt + 1) * P], sel_den[:, :])], S["accs", u], sel_ready, bank.free)
                        r = dve(lambda e: e.reciprocal(rsmall[:, :], bank.ap[:, 0:4 * GROUP]), t, rden.free)
                        bank.free = [r]
                        r = dve(lambda e: e.tensor_copy(
                            rden.ap[:, :, :], rsmall[:, :].unsqueeze(2).to_broadcast([P, 4 * GROUP, 32])), r)
                        S["rden", u] = r

                    def divide():
                        bank = misc.next()
                        for qt in range(SEQ // P):
                            spread = rden.ap[:, qt * GROUP:(qt + 1) * GROUP, :].rearrange("p j r -> p (j r)")
                            t = mm(bank.ap[:, qt * P:(qt + 1) * P], [(spread, ident[:, :])],
                                   S["rden", u], bank.free)
                        r = dve(lambda e: e.tensor_tensor(ctxn.ap[:, g, :], accs.ap[:, :], bank.ap, ALU.mult),
                                t, ctxn.free)
                        rden.free, accs.free, bank.free = [t], [r], [r]
                        S["ctxn", b] = r
                    return [evacuate], ([denominators, divide] if softmax else [])

                def project(b):
                    steps = []
                    for t0 in range(0, SEQ // P, 2):
                        def step(t0=t0):
                            bank = misc.next()
                            for j in range(2):
                                q0 = (t0 + j) * P
                                t = mm(bank.ap[:, j * DM:(j + 1) * DM],
                                       [(ctxn.ap[:, g, q0:q0 + P], wo[:, g, :]) for g in range(GROUPS)],
                                       S["ctxn", b], w_ready, bank.free)
                            rows = x[:, 4 * b + t0:4 * b + t0 + 2, :].rearrange("p t d -> p (t d)")
                            a = dve(lambda e: e.tensor_tensor(rows, rows, bank.ap, ALU.add), t, x_biased)
                            bank.free = [a]
                            x_tokens.append(a)
                            ctxn.free = [t]
                        steps.append(step)
                    return steps

                def attend(u):
                    b, g = divmod(u, GROUPS)
                    ks, qs = kst[u % 3], qst[u % 3]
                    rows = STACK if softmax else PAIR_ROWS
                    steps = []
                    made = {}

                    def scores(kc, pair):
                        k0, kn = KEY_CHUNKS[kc]
                        slot, p = s_slots.next(), probs.next()
                        for i in range(2):
                            h = 2 * pair + i
                            t = mm(slot.ap[0:kn, i * BANK:(i + 1) * BANK],
                                   [(ks.ap[0:rows, h, k0:k0 + kn], qs.ap[0:rows, h, :])],
                                   S["unit", u], S.get(("maxrows", u)), slot.free)
                        a = act(lambda e: e.activation(p.ap[0:kn, :], slot.ap[0:kn, :],
                                                       ACT.Exp if softmax else ACT.Sigmoid), t, p.free)
                        slot.free = [a]
                        made[kc, pair] = (p, a)
                        if kc == len(KEY_CHUNKS) - 1 and pair == 1:
                            ks.free, qs.free = [t], [t]

                    def values(kc):
                        k0, kn = KEY_CHUNKS[kc]
                        for h in range(GROUP):
                            p, a = made[kc, h // 2]
                            lhsT = vt.slots[b % 2].ap[0:kn, kc, GROUP * g + h, :]
                            rhs = p.ap[0:kn, (h % 2) * BANK:(h % 2 + 1) * BANK]
                            dst = acc.ap[32 * h:32 * h + VW, :]
                            t = pe(lambda e, dst=dst, lhsT=lhsT, rhs=rhs, h=h: e.matmul(
                                dst, lhsT, rhs, start=kc == 0, stop=kc == len(KEY_CHUNKS) - 1,
                                tile_position=(0, 32 * h)), a, S["v", b], acc.free)
                            p.free = [t]
                        S["acc", u] = t
                        if g == GROUPS - 1:
                            vt.slots[b % 2].free = [t]

                    for kc in range(len(KEY_CHUNKS)):
                        steps.append(lambda kc=kc: scores(kc, 0))
                        steps.append(lambda kc=kc: scores(kc, 1))
                        if kc:
                            steps.append(lambda kc=kc: values(kc - 1))
                    steps.append(lambda: values(len(KEY_CHUNKS) - 1))
                    return steps

                def interleave(main, side):
                    done = 0
                    for i, step in enumerate(main):
                        step()
                        want = (i + 1) * len(side) // len(main)
                        while done < want:
                            side[done]()
                            done += 1

                UNITS = BATCH * GROUPS
                side = load_ctx(0) + make_keys(0, 0) + make_queries(0) + load_unit(0) + load_unit(1)
                side += make_keys(0, 1) + make_values(0) + load_ctx(1)
                if softmax:
                    side += maxima(0)
                for step in side:
                    step()
                for u in range(UNITS):
                    b, g = divmod(u, GROUPS)
                    side = []
                    if u + 2 < UNITS:
                        side += load_unit(u + 2)
                    if u:
                        side += finish(u - 1)[1]
                        if g == 0:
                            side += project(b - 1)
                    if b + 1 < BATCH:
                        if g == 0:
                            side += make_queries(b + 1) + make_keys(b + 1, 0)
                        if g == 1:
                            side += make_keys(b + 1, 1)
                        if g == 2:
                            side += make_values(b + 1)
                            if b + 2 < BATCH:
                                side += load_ctx(b + 2)
                    if softmax and u + 1 < UNITS:
                        side += maxima(u + 1)
                    interleave(attend(u), side)
                    finish(u)[0][0]()
                for step in finish(UNITS - 1)[1] + project(BATCH - 1):
                    step()
                for b in banks:
                    b.free = [(dve.done, dve.done.n), (act.done, act.done.n)]
                state["x"] = x_tokens

        def banks_free():
            for b in banks:
                b.free = fence()

        def iota_rows(sc, n, start):
            t32 = sbuf(sc, "iota_i", [P, n], mybir.dt.int32)
            t = sbuf(sc, "iota", [P, n])
            a = pool(lambda e: e.iota(t32[:, :], pattern=[[1, n]], base=0, channel_multiplier=0), start)
            return t, pool(lambda e: e.tensor_copy(t[:, :], t32[:, :]), a)

        def tokens_logits(dst, w, w_ready, hT_ready, n, bank, K=KC, lhs=None):
            for t in range(TILES):
                tok = mm(bank.ap[:, t * n:(t + 1) * n],
                         [(hT[:, k, t * P:(t + 1) * P], w[:, k, :]) for k in range(K)],
                         hT_ready, w_ready, bank.free)
            c = dve(lambda e: e.tensor_copy(dst[:, :, :].rearrange("p t e -> p (t e)"), bank.ap[:, 0:TILES * n]), tok)
            bank.free = [c]
            return c

        def over(ap2, n):
            return ap2.unsqueeze(2).to_broadcast([P, TILES, n])

        def softmax_rows(sc, v, n, ready, divide=True):
            m = sbuf(sc, "smax", [P, TILES])
            a = dve(lambda e: e.tensor_reduce(m[:, :], v[:, :, :], AX.X, ALU.max), ready)
            a = dve(lambda e: e.tensor_tensor(v[:, :, :], v[:, :, :], over(m[:, :], n), ALU.subtract), a)
            a = act(lambda e: e.activation(v[:, :, :], v[:, :, :], ACT.Exp), a)
            if divide:
                a = dve(lambda e: e.tensor_reduce(m[:, :], v[:, :, :], AX.X, ALU.add), a)
                a = dve(lambda e: e.reciprocal(m[:, :], m[:, :]), a)
                a = dve(lambda e: e.tensor_tensor(v[:, :, :], v[:, :, :], over(m[:, :], n), ALU.mult), a)
            return a

        def top_onehots(sc, v, n, k, iota, ready):
            top8 = sbuf(sc, "top8", [P, TILES, 8])
            idx = sbuf(sc, "idx", [P, TILES, 8], U32)
            idxf = sbuf(sc, "idxf", [P, TILES, 8])
            for t in range(TILES):
                a = dve(lambda e, t=t: e.max(top8[:, t, :], v[:, t, :]), ready)
            for t in range(TILES):
                a = dve(lambda e, t=t: e.max_index(idx[:, t, :], top8[:, t, :], v[:, t, :]), a)
            a = dve(lambda e: e.tensor_copy(idxf[:, :, :], idx[:, :, :]), a)
            hot = []
            for i in range(k):
                o = sbuf(sc, "hot", [P, TILES, n])
                a = dve(lambda e, o=o, i=i: e.tensor_tensor(
                    o[:, :, :], iota[:, 0:n].unsqueeze(1).to_broadcast([P, TILES, n]), over(idxf[:, :, i], n),
                    ALU.is_equal), a)
                hot.append(o)
            return hot, top8, a

        def turn_rows(dst, src, n_rows, width, needs, start):
            toks = []
            for g in range(TILES // 4):
                bank = banks[g % 8]
                for i in range(4):
                    t = pe(lambda e, g=g, i=i, bank=bank: e.transpose(
                        bank.ap[0:n_rows, i * P:(i + 1) * P], src[:, 4 * g + i, :], ident[:, :]), needs, bank.free)
                c = act(lambda e, g=g, bank=bank: e.activation(dst[:, g * BANK:(g + 1) * BANK],
                                                               bank.ap[0:n_rows, :], ACT.Copy), t)
                bank.free = [c]
                toks.append(c)
            return toks

        def ffn0():
            E = 8
            start = fence()
            banks_free()
            with ExitStack() as sc:
                W = dma_count("ffn0_w")
                h = sbuf(sc, "h", [P, TILES, DM])
                we = sbuf(sc, "we", [P, KC, E, DM])
                for k in range(KC):
                    load(W, we[:, k, :, :], I["L0_ffn_We"][:, k * P:(k + 1) * P, :].rearrange("e p n -> p e n"), start)
                be = sbuf(sc, "be", [E, DM])
                load(W, be[:, :], I["L0_ffn_be"], start)
                wg, w_ready = load_weight(sc, W, "wg", I["L0_ffn_Wg"], start)
                iota, iota_ready = iota_rows(sc, E, start)
                _, hT_ready = layer_norm(h, start)
                gates = sbuf(sc, "gates", [P, TILES, E])
                g = tokens_logits(gates, wg, w_ready, hT_ready, E, banks[0])
                g = softmax_rows(sc, gates, E, g)
                hot, top8, g = top_onehots(sc, gates, E, 2, iota, [g, iota_ready])
                s = sbuf(sc, "s", [P, TILES])
                w2 = sbuf(sc, "w2", [P, TILES, 2])
                disp = sbuf(sc, "disp", [P, TILES, E])
                g = dve(lambda e: e.tensor_tensor(s[:, :], top8[:, :, 0], top8[:, :, 1], ALU.add), g)
                g = dve(lambda e: e.reciprocal(s[:, :], s[:, :]), g)
                g = dve(lambda e: e.tensor_tensor(w2[:, :, :], top8[:, :, 0:2], over(s[:, :], 2), ALU.mult), g)
                for i in range(2):
                    g = dve(lambda e, i=i: e.tensor_tensor(hot[i][:, :, :], hot[i][:, :, :], over(w2[:, :, i], E),
                                                           ALU.mult), g)
                g = dve(lambda e: e.tensor_tensor(disp[:, :, :], hot[0][:, :, :], hot[1][:, :, :], ALU.add), g)
                dT = sbuf(sc, "dT", [E, TOK])
                dT_ready = turn_rows(dT, disp, E, E, g, start)
                ring = Ring(banks)
                xt = []
                for t in range(TILES):
                    for e2 in range(E // 2):
                        bank = ring.next()
                        m = mm(bank.ap, [(hT[:, k, t * P:(t + 1) * P],
                                          we[:, k, 2 * e2:2 * e2 + 2, :].rearrange("p e n -> p (e n)"))
                                         for k in range(KC)], hT_ready, w_ready, bank.free)
                        for i in range(2):
                            ex = 2 * e2 + i
                            a = dve(lambda e, t=t, i=i, ex=ex, bank=bank: e.scalar_tensor_tensor(
                                out=x[:, t, :], in0=bank.ap[:, i * DM:(i + 1) * DM], scalar=disp[:, t, ex:ex + 1],
                                in1=x[:, t, :], op0=ALU.mult, op1=ALU.add), m, g, xt[-1:])
                            xt = [a]
                        bank.free = [a]
                    bank = ring.next()
                    m = mm(bank.ap[:, 0:DM], [(dT[:, t * P:(t + 1) * P], be[:, :])], dT_ready, w_ready, bank.free)
                    a = dve(lambda e, t=t, bank=bank: e.tensor_tensor(x[:, t, :], x[:, t, :], bank.ap[:, 0:DM],
                                                                      ALU.add), m, xt)
                    xt = [a]
                    bank.free = [a]
                state["x"] = xt

        def autocorrelation():
            TOP = 6
            FC = SEQ // P
            start = fence()
            banks_free()
            with ExitStack() as sc:
                W = dma_count("l1x_w")
                h = sbuf(sc, "h", [P, TILES, DM])
                wq, _ = load_weight(sc, W, "wq", I["L1_xattn_Wq"], start)
                wk, _ = load_weight(sc, W, "wk", I["L1_xattn_Wk"], start)
                wv, _ = load_weight(sc, W, "wv", I["L1_xattn_Wv"], start)
                wo, _ = load_weight(sc, W, "wo", I["L1_xattn_Wo"], start)
                bq, _ = load_rows(sc, W, "bq", I["L1_xattn_bq"], start)
                bk, _ = load_rows(sc, W, "bk", I["L1_xattn_bk"], start)
                bv, _ = load_rows(sc, W, "bv", I["L1_xattn_bv"], start)
                bo, _ = load_rows(sc, W, "bo", I["L1_xattn_bo"], start)
                fwd, _ = load_weight(sc, W, "fwd", I["dft"], start)
                inv, w_ready = load_weight(sc, W, "inv", I["idft"], start)
                ctx = Ring([Slot(sbuf(sc, "ctx", [P, KC, SEQ]), dma_count(f"l1x_ctx{i}")) for i in range(2)])
                iota, iota_ready = iota_rows(sc, SEQ, start)
                _, hT_ready = layer_norm(h, start)
                x_biased = pool(lambda e: e.tensor_tensor(
                    x[:, :, :], x[:, :, :], bo[:, :].unsqueeze(1).to_broadcast([P, TILES, DM]), ALU.add),
                    w_ready, hT_ready)
                time_ = Ring([Slot(sbuf(sc, "time", [P, FC, DM])) for _ in range(3)])
                qf = Slot(sbuf(sc, "qf", [P, FC, DM]))
                kf = Slot(sbuf(sc, "kf", [P, FC, DM]))
                vf = [sbuf(sc, "vf", [P, FC, DM]) for _ in range(BATCH)]
                prod = Ring([Slot(sbuf(sc, "prod", [P, 2, DM])) for _ in range(2)])
                cross = [sbuf(sc, "cross", [P, 2, BATCH * HEADS]) for _ in range(4)]
                ring = Ring(banks)
                vf_ready, cross_ready = [], []

                def linear(dst, left, w, bias, left_ready):
                    for t0 in (0, 2):
                        bank = ring.next()
                        for j in range(2):
                            m = mm(bank.ap[:, j * DM:(j + 1) * DM],
                                   [(left(k, t0 + j), w[:, k, :]) for k in range(KC)], left_ready, w_ready, bank.free)
                        a = dve(lambda e, t0=t0, bank=bank: e.tensor_tensor(
                            dst.ap[:, t0:t0 + 2, :], bank.ap.rearrange("p (t d) -> p t d", d=DM),
                            bias[:, :].unsqueeze(1).to_broadcast([P, 2, DM]), ALU.add), m, dst.free)
                        bank.free = [a]
                    return m, a

                def spectrum(dst, dst_free, src, src_ready):
                    for f0 in range(0, FC, 2):
                        bank = ring.next()
                        for j in range(2):
                            f = f0 + j
                            m = mm(bank.ap[:, j * DM:(j + 1) * DM],
                                   [(fwd[:, t, f * P:(f + 1) * P], src[:, t, :]) for t in range(FC)],
                                   src_ready, w_ready, bank.free)
                        a = act(lambda e, f0=f0, bank=bank: e.activation(
                            dst[:, f0:f0 + 2, :].rearrange("p f d -> p (f d)"), bank.ap, ACT.Copy), m, dst_free)
                        bank.free = [a]
                    return m, a

                for b in range(BATCH):
                    c = ctx.next()
                    c_ready = load(c.count, c.ap[:, :, :],
                                   I["ctxT"][:, b, 0:SEQ].rearrange("(k p) s -> p k s", p=P), c.free, start)
                    q, k_, v = time_.slots
                    _, q_ready = linear(q, lambda k, t: hT[:, k, b * SEQ + t * P:b * SEQ + (t + 1) * P], wq, bq, hT_ready)
                    _, k_ready = linear(k_, lambda k, t: c.ap[:, k, t * P:(t + 1) * P], wk, bk, c_ready)
                    cm, v_ready = linear(v, lambda k, t: c.ap[:, k, t * P:(t + 1) * P], wv, bv, c_ready)
                    c.free = [cm]
                    m, qf_ready = spectrum(qf.ap, qf.free, q.ap, q_ready)
                    q.free = [m]
                    m, kf_ready = spectrum(kf.ap, kf.free, k_.ap, k_ready)
                    k_.free = [m]
                    m, a = spectrum(vf[b], [], v.ap, v_ready)
                    v.free = [m]
                    vf_ready.append(a)
                    for i, (qo, ko) in enumerate(((0, 0), (2, 2), (2, 0), (0, 2))):
                        p = prod.next()
                        a = dve(lambda e, qo=qo, ko=ko, p=p: e.tensor_tensor(
                            p.ap[:, :, :], qf.ap[:, qo:qo + 2, :], kf.ap[:, ko:ko + 2, :], ALU.mult),
                            qf_ready, kf_ready, p.free)
                        qf.free = kf.free = [a]
                        r = dve(lambda e, i=i, b=b, p=p: e.tensor_reduce(
                            cross[i][:, :, b * HEADS:(b + 1) * HEADS],
                            p.ap[:, :, :].rearrange("p f (h d) -> p f h d", d=DH), AX.X, ALU.add), a)
                        p.free = [r]
                        cross_ready = [r]

                NB = BATCH * HEADS
                re, im = cross[0], cross[2]
                qiki = cross[1]
                hold = sbuf(sc, "hold", [1, NB])
                a = dve(lambda e: e.tensor_copy(hold[:, :], cross[0][0:1, 0, :]), cross_ready)
                a = dve(lambda e: e.tensor_tensor(re[:, :, :], cross[0][:, :, :], qiki[:, :, :], ALU.add), a)
                a = dve(lambda e: e.tensor_copy(re[0:1, 0, :], hold[:, :]), a)
                a = dve(lambda e: e.tensor_tensor(im[:, :, :], cross[2][:, :, :], cross[3][:, :, :], ALU.subtract), a)
                a = dve(lambda e: e.tensor_copy(im[0:1, 0, :], qiki[0:1, 0, :]), a)
                bank = ring.next()
                m = mm(bank.ap[0:NB, :], [(re[:, 0, :], inv[:, 0, :]), (re[:, 1, :], inv[:, 1, :]),
                                          (im[:, 0, :], inv[:, 2, :]), (im[:, 1, :], inv[:, 3, :])],
                       a, w_ready, bank.free)
                corr = sbuf(sc, "corr", [NB, SEQ])
                a = dve(lambda e, bank=bank: e.tensor_scalar(corr[:, :], bank.ap[0:NB, :], 1.0 / DH, None, ALU.mult), m)
                bank.free = [a]
                top8 = sbuf(sc, "top8", [NB, 8])
                idx = sbuf(sc, "idx", [NB, 8], U32)
                idxf = sbuf(sc, "idxf", [NB, 8])
                neg = sbuf(sc, "neg", [NB, 1])
                tot = sbuf(sc, "tot", [NB, 1])
                wts = sbuf(sc, "wts", [NB, 8])
                a = dve(lambda e: e.max(top8[:, :], corr[:, :]), a)
                a = dve(lambda e: e.max_index(idx[:, :], top8[:, :], corr[:, :]), a)
                a = dve(lambda e: e.tensor_copy(idxf[:, :], idx[:, :]), a)
                a = dve(lambda e: e.tensor_scalar(neg[:, :], top8[:, 0:1], -1.0, None, ALU.mult), a)
                a = act(lambda e: e.activation(wts[:, 0:TOP], top8[:, 0:TOP], ACT.Exp, bias=neg[:, 0:1]), a)
                a = dve(lambda e: e.tensor_reduce(tot[:, :], wts[:, 0:TOP], AX.X, ALU.add), a)
                a = dve(lambda e: e.reciprocal(tot[:, :], tot[:, :]), a)
                a = dve(lambda e: e.tensor_scalar(wts[:, 0:TOP], wts[:, 0:TOP], tot[:, 0:1], None, ALU.mult), a)
                kern = sbuf(sc, "kern", [NB, SEQ])
                term = sbuf(sc, "term", [NB, SEQ])
                for i in range(TOP):
                    dst = kern if i == 0 else term
                    a = dve(lambda e, i=i, dst=dst: e.tensor_scalar(
                        dst[:, :], iota[0:NB, :], idxf[:, i:i + 1], wts[:, i:i + 1], ALU.is_equal, ALU.mult),
                        a, iota_ready)
                    if i:
                        a = dve(lambda e: e.tensor_tensor(kern[:, :], kern[:, :], term[:, :], ALU.add), a)
                kernT = sbuf(sc, "kernT", [P, FC, NB])
                bank = ring.next()
                for t in range(FC):
                    m = pe(lambda e, t=t, bank=bank: e.transpose(bank.ap[:, t * NB:(t + 1) * NB],
                                                                 kern[:, t * P:(t + 1) * P], ident[0:NB, 0:NB]),
                           a, bank.free)
                a = act(lambda e, bank=bank: e.activation(kernT[:, :, :].rearrange("p t n -> p (t n)"),
                                                          bank.ap[:, 0:FC * NB], ACT.Copy), m)
                bank.free = [a]
                bank = ring.next()
                for f in range(FC):
                    m = mm(bank.ap[:, f * NB:(f + 1) * NB],
                           [(fwd[:, t, f * P:(f + 1) * P], kernT[:, t, :]) for t in range(FC)], a, bank.free)
                cr, ci = sbuf(sc, "cr", [P, 2, NB]), sbuf(sc, "ci", [P, 2, NB])
                cr2 = sbuf(sc, "cr2", [P, 2, NB])
                view = bank.ap[:, 0:FC * NB].rearrange("p (f n) -> p f n", n=NB)
                a1 = dve(lambda e: e.tensor_copy(cr[:, :, :], view[:, 0:2, :]), m)
                a2 = dve(lambda e: e.tensor_copy(cr2[:, :, :], view[:, 0:2, :]), m)
                a3 = dve(lambda e: e.tensor_copy(ci[:, :, :], view[:, 2:4, :]), m)
                a4 = dve(lambda e: e.tensor_copy(cr2[0:1, 0, :], ci[0:1, 0, :]), a3)
                a5 = dve(lambda e: e.memset(ci[0:1, 0, :], 0.0), a4)
                bank.free = [a3]
                of = Ring([Slot(sbuf(sc, "of", [P, FC, DM])) for _ in range(2)])
                oT = Ring([Slot(sbuf(sc, "oT", [P, KC, SEQ])) for _ in range(2)])
                xt = []
                for b in range(BATCH):
                    o = of.next()

                    def spread(c, f):
                        return c[:, f, b * HEADS:(b + 1) * HEADS].unsqueeze(2).to_broadcast([P, HEADS, DH])

                    def heads(v):
                        return v.rearrange("p (h d) -> p h d", d=DH)

                    for f in range(2):
                        p1, p2 = prod.next(), prod.next()
                        plans = ((0, cr, 2, ci, o.ap[:, f, :], ALU.add), (2, cr2, 0, ci, o.ap[:, 2 + f, :], ALU.subtract))
                        for n, (v1, c1, v2, c2, dst, op) in enumerate(plans):
                            def times(p, v, c, n=n, f=f, b=b):
                                left, right = heads(vf[b][:, v + f, :]), spread(c, f)
                                return dve(lambda e: e.tensor_tensor(heads(p.ap[:, n, :]), left, right, ALU.mult),
                                           a5, vf_ready[b], p.free)

                            m1, m2 = times(p1, v1, c1), times(p2, v2, c2)
                            s = dve(lambda e, dst=dst, op=op, n=n, p1=p1, p2=p2: e.tensor_tensor(
                                dst, p1.ap[:, n, :], p2.ap[:, n, :], op), m1, m2, o.free)
                        p1.free = p2.free = [s]
                    ot = oT.next()
                    for c in range(KC):
                        bank = ring.next()
                        m = mm(bank.ap, [(o.ap[:, f, c * P:(c + 1) * P], inv[:, f, :]) for f in range(FC)],
                               s, bank.free)
                        a = act(lambda e, c=c, bank=bank, ot=ot: e.activation(ot.ap[:, c, :], bank.ap, ACT.Copy),
                                m, ot.free)
                        bank.free = [a]
                    o.free = [m]
                    for t0 in (0, 2):
                        bank = ring.next()
                        for j in range(2):
                            q0 = (t0 + j) * P
                            m = mm(bank.ap[:, j * DM:(j + 1) * DM],
                                   [(ot.ap[:, k, q0:q0 + P], wo[:, k, :]) for k in range(KC)], a, bank.free)
                        rows = x[:, 4 * b + t0:4 * b + t0 + 2, :].rearrange("p t d -> p (t d)")
                        xa = dve(lambda e, rows=rows, bank=bank: e.tensor_tensor(rows, rows, bank.ap, ALU.add),
                                 m, x_biased)
                        bank.free = [xa]
                        xt.append(xa)
                    ot.free = [m]
                state["x"] = xt

        def ffn1():
            E, INNER = 4, 1024
            IC = INNER // P
            start = fence()
            banks_free()
            with ExitStack() as sc:
                W = dma_count("ffn1_w")
                h = sbuf(sc, "h", [P, TILES, DM])
                w1 = sbuf(sc, "w1", [P, KC, E, INNER])
                for k in range(KC):
                    load(W, w1[:, k, :, :], I["L1_ffn_W1"][:, k * P:(k + 1) * P, :].rearrange("e p n -> p e n"), start)
                b1 = sbuf(sc, "b1", [E, INNER])
                load(W, b1[:, :], I["L1_ffn_b1"], start)
                wo, _ = load_weight(sc, W, "wo", I["L1_ffn_Wo"], start)
                bo, _ = load_rows(sc, W, "bo", I["L1_ffn_bo"], start)
                gam, _ = load_rows(sc, W, "gam", I["L1_ffn_ln_gamma"], start)
                bet, _ = load_rows(sc, W, "bet", I["L1_ffn_ln_beta"], start)
                wr, w_ready = load_weight(sc, W, "wr", I["L1_ffn_W_router"], start)
                iota, iota_ready = iota_rows(sc, 8, start)
                h_ready, hT_ready = layer_norm(h, start)
                logits = sbuf(sc, "logits", [P, TILES, 8])
                low = dve(lambda e: e.memset(logits[:, :, :], -3.4e38), start)
                bank = banks[0]
                for t in range(TILES):
                    m = mm(bank.ap[:, t * E:(t + 1) * E],
                           [(hT[:, k, t * P:(t + 1) * P], wr[:, k, :]) for k in range(KC)],
                           hT_ready, w_ready, bank.free)
                a = dve(lambda e, bank=bank: e.tensor_copy(logits[:, :, 0:E],
                                                bank.ap[:, 0:TILES * E].rearrange("p (t e) -> p t e", e=E)), m, low)
                bank.free = [a]
                hot, _, a = top_onehots(sc, logits, 8, 1, iota, [a, iota_ready])
                hotT = sbuf(sc, "hotT", [8, TOK])
                hotT_ready = turn_rows(hotT, hot[0], 8, 8, a, start)
                pick = sbuf(sc, "pick", [E, E, P])
                z = pool(lambda e: e.memset(pick[:, :, :], 0.0), start)
                pick_ready = pool(lambda e: e.affine_select(
                    out=pick[:, :, :], in_=pick[:, :, :], compare_op=ALU.not_equal, fill=1.0, base=0,
                    pattern=[[-1, E], [0, P]], channel_multiplier=1), z)
                hb = pool(lambda e: e.tensor_tensor(h[:, :, :], h[:, :, :],
                                                    bo[:, :].unsqueeze(1).to_broadcast([P, TILES, DM]), ALU.add),
                          w_ready, hT_ready, h_ready)
                masked = Ring([Slot(sbuf(sc, "masked", [P, E, KC, BANK])) for _ in range(1)])
                inner = Ring([Slot(sbuf(sc, "inner", [P, IC, BANK])) for _ in range(1)])
                ring = Ring(banks)
                ys = []
                for g in range(TILES // 4):
                    cols = slice(g * BANK, (g + 1) * BANK)
                    mk = masked.next()
                    for ex in range(E):
                        bank = ring.next()
                        m = mm(bank.ap, [(pick[:, ex, :], hotT[0:E, cols])], hotT_ready[g], pick_ready, bank.free)
                        for k in range(KC):
                            a = dve(lambda e, ex=ex, k=k, bank=bank, mk=mk, cols=cols: e.tensor_tensor(
                                mk.ap[:, ex, k, :], hT[:, k, cols], bank.ap, ALU.mult), m, mk.free)
                        bank.free = [a]
                    inn = inner.next()
                    for i in range(IC):
                        bank = ring.next()
                        pairs = [(b1[:, i * P:(i + 1) * P], hotT[0:E, cols])]
                        pairs += [(w1[:, k, ex, i * P:(i + 1) * P], mk.ap[:, ex, k, :])
                                  for ex in range(E) for k in range(KC)]
                        m = mm(bank.ap, pairs, a, w_ready, bank.free)
                        gl = act(lambda e, i=i, bank=bank, inn=inn: e.activation(inn.ap[:, i, :], bank.ap, ACT.Gelu),
                                 m, inn.free)
                        bank.free = [gl]
                    mk.free = [m]
                    for t0 in (0, 2):
                        bank = ring.next()
                        for j in range(2):
                            q0 = (t0 + j) * P
                            m = mm(bank.ap[:, j * DM:(j + 1) * DM],
                                   [(inn.ap[:, i, q0:q0 + P], wo[:, i, :]) for i in range(IC)], gl, bank.free)
                        rows = h[:, 4 * g + t0:4 * g + t0 + 2, :].rearrange("p t d -> p (t d)")
                        y = dve(lambda e, rows=rows, bank=bank: e.tensor_tensor(rows, rows, bank.ap, ALU.add), m, hb)
                        bank.free = [y]
                        ys.append(y)
                    inn.free = [m]
                r = layer_norm_stats(h, ys, 1e-12)
                for t in range(TILES):
                    n = normed(h[:, t, :], h[:, t, :], t, r)
                gmul = pool(lambda e: e.tensor_tensor(h[:, :, :], h[:, :, :],
                                                      gam[:, :].unsqueeze(1).to_broadcast([P, TILES, DM]), ALU.mult), n)
                xb = dve(lambda e: e.tensor_tensor(x[:, :, :], x[:, :, :],
                                                   bet[:, :].unsqueeze(1).to_broadcast([P, TILES, DM]), ALU.add), n)
                state["x"] = [dve(lambda e: e.tensor_tensor(x[:, :, :], x[:, :, :], h[:, :, :], ALU.add), gmul, xb)]

        def ffn2():
            E = 8
            start = fence()
            banks_free()
            with ExitStack() as sc:
                W = dma_count("ffn2_w")
                h = sbuf(sc, "h", [P, TILES, DM])
                wsi, _ = load_weight(sc, W, "wsi", I["L2_ffn_w_shared_in"], start)
                w1, _ = load_weight(sc, W, "w1", I["L2_ffn_w1_shared"], start)
                w2 = sbuf(sc, "w2", [P, KC, E, DM])
                for k in range(KC):
                    load(W, w2[:, k, :, :], I["L2_ffn_w2"][:, k * P:(k + 1) * P, :].rearrange("e p n -> p e n"), start)
                wso, _ = load_weight(sc, W, "wso", I["L2_ffn_w_shared_out"], start)
                gb, _ = load_rows(sc, W, "gb", I["L2_ffn_gate_bias"], start)
                wg, w_ready = load_weight(sc, W, "wg", I["L2_ffn_w_gate"], start)
                iota, iota_ready = iota_rows(sc, E, start)
                _, hT_ready = layer_norm(h, start)
                probs = sbuf(sc, "probs", [P, TILES, E])
                g = tokens_logits(probs, wg, w_ready, hT_ready, E, banks[0])
                g = dve(lambda e: e.tensor_tensor(probs[:, :, :], probs[:, :, :],
                                                  gb[:, :].unsqueeze(1).to_broadcast([P, TILES, E]), ALU.add), g)
                g = softmax_rows(sc, probs, E, g)
                hot, top8, g = top_onehots(sc, probs, E, 2, iota, [g, iota_ready])
                for i in range(2):
                    g = dve(lambda e, i=i: e.tensor_tensor(hot[i][:, :, :], hot[i][:, :, :], over(top8[:, :, i], E),
                                                           ALU.mult), g)
                disp = sbuf(sc, "disp", [P, TILES, E])
                g = dve(lambda e: e.tensor_tensor(disp[:, :, :], hot[0][:, :, :], hot[1][:, :, :], ALU.add), g)
                ring = Ring(banks)
                hidden = Ring([Slot(sbuf(sc, "hidden", [P, 2, KC, BANK])) for _ in range(2)])
                silu = Ring([Slot(sbuf(sc, "silu", [P, BANK])) for _ in range(2)])
                xt = []
                for gq in range(TILES // 4):
                    cols = slice(gq * BANK, (gq + 1) * BANK)
                    hid = hidden.next()
                    for which, w in enumerate((wsi, w1)):
                        for c in range(KC):
                            ba, bb = ring.next(), ring.next()
                            ma = mm(ba.ap, [(w[:, k, c * P:(c + 1) * P], hT[:, k, cols]) for k in range(KC)],
                                    hT_ready, w_ready, ba.free)
                            mb = mm(bb.ap, [(w[:, k, DM + c * P:DM + (c + 1) * P], hT[:, k, cols]) for k in range(KC)],
                                    bb.free)
                            s = silu.next()
                            a = act(lambda e, s=s, ba=ba: e.activation(s.ap[:, :], ba.ap, ACT.Silu), ma, s.free)
                            ba.free = [a]
                            hd = dve(lambda e, s=s, bb=bb, which=which, c=c, hid=hid: e.tensor_tensor(
                                hid.ap[:, which, c, :], s.ap[:, :], bb.ap, ALU.mult), a, mb, hid.free)
                            s.free = bb.free = [hd]
                            s.free, bb.free = [hd], [hd]
                    for j in range(4):
                        t = 4 * gq + j
                        bank = ring.next()
                        m = mm(bank.ap[:, 0:DM], [(hid.ap[:, 0, k, j * P:(j + 1) * P], wso[:, k, :]) for k in range(KC)],
                               hd, bank.free)
                        a = dve(lambda e, t=t, bank=bank: e.tensor_tensor(x[:, t, :], x[:, t, :], bank.ap[:, 0:DM],
                                                                          ALU.add), m, state["x"])
                        bank.free = [a]
                        for e2 in range(E // 2):
                            bank = ring.next()
                            m = mm(bank.ap, [(hid.ap[:, 1, k, j * P:(j + 1) * P],
                                              w2[:, k, 2 * e2:2 * e2 + 2, :].rearrange("p e n -> p (e n)"))
                                             for k in range(KC)], bank.free)
                            for i in range(2):
                                ex = 2 * e2 + i
                                a = dve(lambda e, t=t, i=i, ex=ex, bank=bank: e.scalar_tensor_tensor(
                                    out=x[:, t, :], in0=bank.ap[:, i * DM:(i + 1) * DM], scalar=disp[:, t, ex:ex + 1],
                                    in1=x[:, t, :], op0=ALU.mult, op1=ALU.add), m, g, a)
                            bank.free = [a]
                    hid.free = [m]
                state["x"] = [a]

        def ffn3():
            E, RH = 16, 128
            start = fence()
            banks_free()
            with ExitStack() as sc:
                W = dma_count("ffn3_w")
                h = sbuf(sc, "h", [P, TILES, DM])
                w1, _ = load_weight(sc, W, "w1", I["L3_ffn_W1"], start)
                wg1, _ = load_weight(sc, W, "wg1", I["L3_ffn_Wg1"], start)
                w2, _ = load_weight(sc, W, "w2", I["L3_ffn_W2"], start)
                wg2, _ = load_weight(sc, W, "wg2", I["L3_ffn_Wg2"], start)
                b1, _ = load_columns(sc, W, "b1", I["L3_ffn_b1"], start)
                bg1, _ = load_columns(sc, W, "bg1", I["L3_ffn_bg1"], start)
                b2, _ = load_rows(sc, W, "b2", I["L3_ffn_b2"], start)
                bg2, _ = load_rows(sc, W, "bg2", I["L3_ffn_bg2"], start)
                sb_ = sbuf(sc, "scale_bias", [E, 2, DM])
                load(W, sb_[:, 0, :], I["L3_ffn_expert_scales"], start)
                w_ready = load(W, sb_[:, 1, :], I["L3_ffn_expert_biases"], start)
                iota, iota_ready = iota_rows(sc, E, start)
                _, hT_ready = layer_norm(h, start)
                relu = sbuf(sc, "relu", [P, TOK])
                tanh = sbuf(sc, "tanh", [P, TOK])
                ring = Ring(banks)
                for g in range(TILES // 4):
                    cols = slice(g * BANK, (g + 1) * BANK)
                    for dst, w, b, fn in ((relu, w1, b1, ACT.Relu), (tanh, wg1, bg1, ACT.Tanh)):
                        bank = ring.next()
                        m = mm(bank.ap, [(w[:, k, :], hT[:, k, cols]) for k in range(KC)],
                               hT_ready, w_ready, bank.free)
                        a = act(lambda e, dst=dst, b=b, fn=fn, cols=cols, bank=bank: e.activation(
                            dst[:, cols], bank.ap, fn, bias=b[:, 0:1]), m)
                        bank.free = [a]
                routes = sbuf(sc, "routes", [P, TILES, E])
                gate = sbuf(sc, "gate", [P, TILES])
                bank, bank2 = ring.next(), ring.next()
                for t in range(TILES):
                    m = mm(bank.ap[:, t * E:(t + 1) * E], [(relu[:, t * P:(t + 1) * P], w2[:, 0, :])], a, bank.free)
                for t in range(TILES):
                    m2 = mm(bank2.ap[:, t:t + 1], [(tanh[:, t * P:(t + 1) * P], wg2[:, 0, :])], bank2.free)
                r = dve(lambda e, bank=bank: e.tensor_tensor(routes[:, :, :],
                                                  bank.ap[:, 0:TILES * E].rearrange("p (t e) -> p t e", e=E),
                                                  b2[:, :].unsqueeze(1).to_broadcast([P, TILES, E]), ALU.add), m, w_ready)
                bank.free = [r]
                s = act(lambda e, bank2=bank2: e.activation(gate[:, :], bank2.ap[:, 0:TILES], ACT.Sigmoid, bias=bg2[:, 0:1]), m2)
                bank2.free = [s]
                r = dve(lambda e: e.tensor_tensor(routes[:, :, :], routes[:, :, :], over(gate[:, :], E), ALU.mult), r, s)
                r = softmax_rows(sc, routes, E, r)
                hot, _, r = top_onehots(sc, routes, E, 1, iota, [r, iota_ready])
                hotT = sbuf(sc, "hotT", [E, TOK])
                hotT_ready = turn_rows(hotT, hot[0], E, E, r, start)
                ring = Ring(banks)
                store = dma_count("store")
                for t in range(TILES):
                    bank = ring.next()
                    m = mm(bank.ap, [(hotT[:, t * P:(t + 1) * P], sb_[:, :, :].rearrange("e a d -> e (a d)"))],
                           hotT_ready, bank.free)
                    a = dve(lambda e, t=t, bank=bank: e.tensor_tensor(h[:, t, :], h[:, t, :], bank.ap[:, 0:DM],
                                                                      ALU.mult), m)
                    a2 = dve(lambda e, t=t, bank=bank: e.tensor_tensor(x[:, t, :], x[:, t, :], bank.ap[:, DM:2 * DM],
                                                                       ALU.add), m)
                    a = dve(lambda e, t=t: e.tensor_tensor(x[:, t, :], x[:, t, :], h[:, t, :], ALU.add), a, a2)
                    bank.free = [a2]
                state["x"] = [a]

        layers = [lambda: attention("L0", True, True), ffn0, autocorrelation, ffn1,
                  lambda: attention("L2", False, False), ffn2, lambda: attention("L3", True, True), ffn3]
        for n in LAYERS:
            layers[n]()
        store = new_count("store")
        stored = load(store, out.rearrange("b s d -> (b s) d").rearrange("(t p) d -> p t d", p=P), x[:, :, :],
                      state["x"])
        sp(lambda e: e.nop(), stored, signal=False)

        block = top.enter_context(nc.Block())

        @block.tensor
        def _(e):
            pe.run(e)

        @block.vector
        def _(e):
            dve.run(e)

        @block.scalar
        def _(e):
            act.run(e)

        @block.gpsimd
        def _(e):
            pool.run(e)

        @block.sync
        def _(e):
            sp.run(e)


LAYERS = range(8)


def dft_tables():
    n, half = SEQ, SEQ // 2
    t = np.arange(n)
    f = np.arange(half)
    angle = 2 * np.pi * ((t[:, None] * f[None, :]) % n) / n
    nyquist = np.where(t % 2 == 0, 1.0, -1.0)
    fwd = np.concatenate([np.cos(angle), -np.sin(angle)], 1)
    fwd[:, half] = nyquist
    weight = np.where(f == 0, 1.0, 2.0) / n
    inv = np.concatenate([(np.cos(angle) * weight).T, (-np.sin(angle) * weight).T], 0)
    inv[half] = nyquist / n
    return fwd.astype(np.float32), inv.astype(np.float32)


TRANSPOSED = {"L0_wq": "L0_xattn_wq_w", "L0_wk": "L0_xattn_wk_w", "L0_wv": "L0_xattn_wv_w", "L0_wo": "L0_xattn_dense_w",
              "L2_wq": "L2_xattn_Wq", "L2_wk": "L2_xattn_Wk", "L2_wv": "L2_xattn_Wv", "L2_wo": "L2_xattn_Wo",
              "L3_wq": "L3_xattn_Wq", "L3_wk": "L3_xattn_Wk", "L3_wv": "L3_xattn_Wv", "L3_wo": "L3_xattn_Wo"}
RENAMED = {"L0_bq": "L0_xattn_wq_b", "L0_bk": "L0_xattn_wk_b", "L0_bv": "L0_xattn_wv_b", "L0_bo": "L0_xattn_dense_b",
           "L3_bq": "L3_xattn_bq", "L3_bk": "L3_xattn_bk", "L3_bv": "L3_xattn_bv", "L3_bo": "L3_xattn_bo"}
AS_IS = ["x", "L0_ffn_Wg", "L0_ffn_We", "L0_ffn_be",
         "L1_xattn_Wq", "L1_xattn_bq", "L1_xattn_Wk", "L1_xattn_bk", "L1_xattn_Wv", "L1_xattn_bv", "L1_xattn_Wo",
         "L1_xattn_bo", "L1_ffn_W_router", "L1_ffn_W1", "L1_ffn_b1", "L1_ffn_Wo", "L1_ffn_bo", "L1_ffn_ln_gamma",
         "L1_ffn_ln_beta", "L2_ffn_w_shared_in", "L2_ffn_w_shared_out", "L2_ffn_w1_shared", "L2_ffn_w2",
         "L2_ffn_w_gate", "L2_ffn_gate_bias", "L3_ffn_W1", "L3_ffn_b1", "L3_ffn_W2", "L3_ffn_b2", "L3_ffn_Wg1",
         "L3_ffn_bg1", "L3_ffn_Wg2", "L3_ffn_bg2", "L3_ffn_expert_scales", "L3_ffn_expert_biases"]


def kernel(**inputs):
    import numpy as _np
    import concourse.bacc as _bacc
    from concourse import mybir as _mybir
    from concourse.bass_utils import run_bass_kernel_spmd as _run

    arrays = {name: _np.ascontiguousarray(inputs[name]) for name in AS_IS}
    arrays |= {name: _np.ascontiguousarray(inputs[src]) for name, src in RENAMED.items()}
    arrays |= {name: _np.ascontiguousarray(_np.asarray(inputs[src]).T) for name, src in TRANSPOSED.items()}
    arrays["ctxT"] = _np.ascontiguousarray(_np.asarray(inputs["ctx_1024"]).transpose(2, 0, 1))
    arrays["dft"], arrays["idft"] = dft_tables()

    nc = _bacc.Bacc("TRN2", target_bir_lowering=False, num_devices=1)
    named, I = {}, {}
    for name, a in arrays.items():
        named[f"in_{name}"] = a
        I[name] = nc.dram_tensor(f"in_{name}", a.shape, _mybir.dt.from_np(a.dtype), kind="ExternalInput").ap()
    out = nc.dram_tensor("out_dram", (BATCH, SEQ, DM), F32, kind="ExternalOutput").ap()
    build(nc, I, out)
    r = _run(nc, [named], core_ids=[0])
    return r.results[0]["out_dram"]
```

```python
from contextlib import ExitStack

import numpy as np
import concourse.bass as bass
from concourse import mybir

F32 = mybir.dt.float32
BF16 = mybir.dt.bfloat16
U32 = mybir.dt.uint32
ALU = mybir.AluOpType
ACT = mybir.ActivationFunctionType
AX = mybir.AxisListType

P = 128
BATCH, SEQ, DM = 4, 512, 256
CTX = 1601
HEADS, DH = 16, 16
TOK = BATCH * SEQ
TILES = TOK // P
KC = DM // P
BANK = 512
LN_EPS = 1e-5

GROUP = 4
GROUPS = HEADS // GROUP
KEY_CHUNKS = [(k, min(P, CTX - k)) for k in range(0, CTX, P)]
KEY_BLOCKS = [(k, min(BANK, CTX - k)) for k in range(0, CTX, BANK)]
MAX_SPLIT = 4
MAX_BLOCKS = [(CTX * i // MAX_SPLIT, CTX * (i + 1) // MAX_SPLIT - CTX * i // MAX_SPLIT) for i in range(MAX_SPLIT)]
K_PART = [0, 1, 2, 0, 1, 2, 0]
Q_PART = [0, 0, 0, 1, 1, 1, 2]
PAIR_ROWS = DH * len(K_PART)
MAX_ROWS = 3
STACK = PAIR_ROWS + MAX_ROWS
LEAD = 0.25
LAG = 1
BEHIND = 2
PROBS = 10
VW = DH + 1


class Count:

    def __init__(self, sem):
        self.sem, self.n = sem, 0


def flat(needs):
    for t in needs:
        if isinstance(t, list):
            yield from flat(t)
        elif t is not None:
            yield t


class Queue:

    def __init__(self, engine, done):
        self.engine, self.done, self.items, self.passed = engine, done, [], {}

    def __call__(self, emit, *needs, done=None, by=1, signal=True):
        most = {}
        for count, value in flat(needs):
            most[count] = max(value, most.get(count, 0))
        waits = [(c, v) for c, v in most.items() if self.passed.get(c, 0) < v]
        self.passed.update(waits)
        count = (done or self.done) if signal else None
        if count:
            count.n += by
        self.items.append((waits, emit, count, by))
        return (count, count.n) if count else None

    def run(self, eng):
        for waits, emit, count, by in self.items:
            for c, v in waits:
                eng.wait_ge(c.sem, v)
            ins = emit(eng)
            if count:
                ins.then_inc(count.sem, by)


class Slot:

    def __init__(self, ap, count=None):
        self.ap, self.free, self.count = ap, [], count


class Ring:
    def __init__(self, slots):
        self.slots, self.at = slots, -1

    def next(self):
        self.at += 1
        return self.slots[self.at % len(self.slots)]


def spread_over(steps, begin, end):
    return [(begin + (i + 0.5) * (end - begin) / len(steps), step) for i, step in enumerate(steps)]


def in_time(timed):
    for _, _, step in sorted((time, n, step) for n, (time, step) in enumerate(timed)):
        step()


def build(nc, I, out):
    with ExitStack() as top:
        sem_n = [0]

        def new_count(name):
            sem_n[0] += 1
            return Count(top.enter_context(nc.semaphore(f"{name}_{sem_n[0]}")))

        pe = Queue("tensor", new_count("pe_done"))
        dve = Queue("vector", new_count("dve_done"))
        act = Queue("scalar", new_count("act_done"))
        pool = Queue("gpsimd", new_count("pool_done"))
        sp = Queue("sync", None)
        compute = [pe, dve, act, pool]
        dma_counts = []

        def dma_count(name):
            c = new_count(name)
            dma_counts.append(c)
            return c

        input_count = new_count

        def load(count, dst, src, *needs):
            return sp(lambda e: e.dma_start(dst, src), *needs, done=count, by=16)

        def fence():
            return [(q.done, q.done.n) for q in compute if q.done.n] + [(c, c.n) for c in dma_counts if c.n]

        def sbuf(scope, name, shape, dt=F32):
            sem_n[0] += 1
            return scope.enter_context(nc.sbuf_tensor(f"{name}_{sem_n[0]}", shape, dt))

        def scratch(name, shape, dt):
            return nc.dram_tensor(name, shape, dt, kind="Internal").ap()

        x = sbuf(top, "x", [P, TILES, DM])
        hT = sbuf(top, "hT", [P, KC, TOK])
        hT_ready = [None] * BATCH
        hT_free = [[] for _ in range(BATCH)]
        x_ready = [[] for _ in range(BATCH)]
        ahead = [False] * BATCH
        hrow = Ring([Slot(sbuf(top, "hrow", [P, DM])) for _ in range(4)])
        half = sbuf(top, "half", [P, 4])
        ident = sbuf(top, "ident", [P, P])
        identb = sbuf(top, "identb", [P, P], BF16)
        sel_den = sbuf(top, "sel_den", [P, GROUP])
        stats = sbuf(top, "stats", [P, TILES, 6])
        meanvar = sbuf(top, "meanvar", [P, TILES, 2])
        veps = sbuf(top, "veps", [P, TILES])
        rstd = sbuf(top, "rstd", [P, TILES])
        ntmp = sbuf(top, "ntmp", [P, TILES])
        psum = top.enter_context(nc.psum_tensor("psum", [P, 8, BANK], F32))
        banks = [Slot(psum[:, i, :]) for i in range(8)]

        def mm(dst, pairs, *needs, tile_position=None):
            for i, (lhsT, rhs) in enumerate(pairs):
                first, last = i == 0, i == len(pairs) - 1

                def emit(e, lhsT=lhsT, rhs=rhs, first=first, last=last):
                    if tile_position is None:
                        return e.matmul(dst, lhsT, rhs, start=first, stop=last)
                    return e.matmul(dst, lhsT, rhs, start=first, stop=last, tile_position=tile_position)

                token = pe(emit, *(needs if first else ()), signal=last)
            return token

        x_in = [dma_count(f"x_in{b}") for b in range(BATCH)]

        def idle():
            pass

        def tiles_of(b):
            return slice(4 * b, 4 * b + 4)

        def load_x():
            for b in range(BATCH):
                x_ready[b] = [load(x_in[b], x[:, 4 * b:4 * b + 4, :], I["x"][b].rearrange("(t p) d -> p t d", p=P))]

        half_ready = pool(lambda e: e.memset(half[:, :], -0.5))
        zero = pool(lambda e: e.memset(ident[:, :], 0.0))
        ident_ready = pool(lambda e: e.affine_select(out=ident[:, :], in_=ident[:, :], compare_op=ALU.not_equal,
                                                     fill=1.0, base=0, pattern=[[-1, P]], channel_multiplier=1), zero)
        identb_ready = pool(lambda e: e.tensor_copy(identb[:, :], ident[:, :]), ident_ready)
        zero = pool(lambda e: e.memset(sel_den[:, :], 0.0))
        sel_ready = pool(lambda e: e.affine_select(out=sel_den[:, :], in_=sel_den[:, :], compare_op=ALU.not_equal,
                                                   fill=1.0, base=-DH, pattern=[[-32, GROUP]], channel_multiplier=1), zero)

        def rsqrt(ts, eps, stat=(meanvar, veps, rstd, ntmp)):
            mv, v, r, n = stat[0], stat[1][:, ts], stat[2][:, ts], stat[3][:, ts]
            S = {}

            def power(needs):
                a = dve(lambda e: e.tensor_scalar(v, mv[:, ts, 1], eps, None, ALU.add), needs)
                S["power"] = pool(lambda e: e.tensor_tensor(r, v, half[:, :], ALU.pow), a, half_ready)

            def newton():
                a = dve(lambda e: e.tensor_tensor(n, r, r, ALU.mult), S["power"])
                a = dve(lambda e: e.tensor_tensor(n, n, v, ALU.mult), a)
                a = dve(lambda e: e.tensor_scalar(n, n, -0.5, 1.5, ALU.mult, ALU.add), a)
                return dve(lambda e: e.tensor_tensor(r, r, n, ALU.mult), a)
            return power, newton

        def moments(src, t, needs, mv=meanvar):
            a = dve(lambda e: e.bn_stats(stats[:, t, :], src), needs)
            return dve(lambda e: e.bn_aggr(mv[:, t, :], stats[:, t, :]), a)

        def normed(dst, src, t, *needs, stat=(meanvar, rstd)):
            return dve(lambda e: e.tensor_scalar(dst, src, stat[0][:, t, 0:1], stat[1][:, t:t + 1],
                                                 ALU.subtract, ALU.mult), *needs)

        def layer_norm(b, ring):
            S = {"rows": []}
            power, newton = rsqrt(tiles_of(b), LN_EPS)

            def statistics(i):
                for t in range(4 * b + i, 4 * b + i + 2):
                    S["stats"] = moments(x[:, t, :], t, x_ready[b])

            def root():
                S["rstd"] = newton()

            def normalise(i):
                for t in range(4 * b + i, 4 * b + i + 2):
                    h = hrow.next()
                    S["rows"].append((h, normed(h.ap[:, :], x[:, t, :], t, S["rstd"], h.free)))

            def turn(i):
                bank = ring.next()
                for j, (h, ready) in enumerate(S["rows"][i:i + 2]):
                    for c in range(KC):
                        at = (KC * j + c) * P
                        tr = pe(lambda e, h=h, c=c, at=at: e.transpose(
                            bank.ap[:, at:at + P], h.ap[:, c * P:(c + 1) * P], ident[:, :]),
                            ready, ident_ready, bank.free)
                    h.free = [tr]
                src = bank.ap.rearrange("p (t c q) -> p c t q", c=KC, q=P)
                cols = slice((4 * b + i) * P, (4 * b + i + 2) * P)
                dst = hT[:, :, cols].rearrange("p c (t q) -> p c t q", q=P)
                w = act(lambda e: e.activation(dst, src, ACT.Copy), tr, hT_free[b])
                bank.free = [w]
                hT_ready[b] = hT_ready[b] + [w] if i else [w]
                if i:
                    hT_free[b] = []
            return [lambda: statistics(0), lambda: statistics(2), lambda: power(S["stats"]), root,
                    lambda: normalise(0), lambda: normalise(2), idle, lambda: turn(0), lambda: turn(2)]

        def own_layer_norms():
            mine = [b for b in range(BATCH) if not ahead[b]]
            ahead[:] = [False] * BATCH
            return mine

        def next_layer_norm(b, ring):
            ahead[b] = True
            return layer_norm(b, ring)

        def fill_weight(count, w, src, *needs):
            return load(count, w[:, :, :], src.rearrange("(k p) n -> p k n", p=P), *needs)

        def fill_columns(count, w, src, *needs):
            return sp(lambda e: e.dma_start(w[:, :], src.rearrange("(k p) -> p k", p=P),
                                            allow_slow_non_contiguous=True), *needs, done=count, by=16)

        def fill_rows(count, w, src, *needs):
            return load(count, w[:, :], src.rearrange("(a n) -> a n", a=1).partition_broadcast(P), *needs)

        k_parts_dram = scratch("k_parts_dram", [2, HEADS, 3 * DH, CTX], BF16)
        q_parts_dram = scratch("q_parts_dram", [2, HEADS, PAIR_ROWS, SEQ], BF16)

        def attention_inputs(tag, biased):
            def place(sc):
                w = {name: sbuf(sc, name, [P, KC, DM]) for name in ("wk", "wq", "wv")}
                w["wo"] = sbuf(sc, "wo", [P, GROUPS, DM])
                w["ctxT"] = Slot(sbuf(sc, "ctxT", [P, KC, CTX]), input_count(f"{tag}_ctx"))
                if biased:
                    w["bk"], w["bq"] = sbuf(sc, "bk", [P, KC]), sbuf(sc, "bq", [P, KC])
                    w["bv"], w["bo"] = sbuf(sc, "bv", [P, DM]), sbuf(sc, "bo", [P, DM])

                def start_loads(start, behind):
                    WK, W = input_count(f"{tag}_key_weights"), input_count(f"{tag}_weights")
                    w["wk_ready"] = fill_weight(WK, w["wk"], I[f"{tag}_wk"], start, behind)
                    if biased:
                        w["wk_ready"] = fill_columns(WK, w["bk"], I[f"{tag}_bk"], start, behind)
                    w["ctx_ready"] = load(w["ctxT"].count, w["ctxT"].ap[:, :, :],
                                          I["ctxT"][:, 0, :].rearrange("(k p) s -> p k s", p=P), start, behind)
                    if not x_ready[0]:
                        load_x()
                    fill_weight(W, w["wq"], I[f"{tag}_wq"], start, behind)
                    fill_weight(W, w["wv"], I[f"{tag}_wv"], start, behind)
                    w["wo_zero"] = pool(lambda e: e.memset(w["wo"][:, :, :], 0.0), start)
                    if biased:
                        fill_columns(W, w["bq"], I[f"{tag}_bq"], start, behind)
                        fill_rows(W, w["bv"], I[f"{tag}_bv"], start, behind)
                        fill_rows(W, w["bo"], I[f"{tag}_bo"], start, behind)
                    wo_src = I[f"{tag}_wo"].rearrange("(g j d) n -> j d g n", g=GROUPS, j=GROUP)
                    for j in range(GROUP):
                        w["ready"] = load(W, w["wo"][32 * j:32 * j + DH, :, :], wo_src[j], w["wo_zero"])
                return w, start_loads
            return place

        def attention(tag, softmax, biased, w):
            start = fence()
            mine = own_layer_norms()
            with ExitStack() as sc:
                wk, wq, wv, wo, ctxT = w["wk"], w["wq"], w["wv"], w["wo"], w["ctxT"]
                wk_ready, w_ready, wo_zero = w["wk_ready"], w["ready"], w["wo_zero"]
                if biased:
                    bk, bq, bv, bo = w["bk"], w["bq"], w["bv"], w["bo"]
                S = {"ctx": w["ctx_ready"]}

                def load_ctx(b):
                    def step():
                        S["ctx"] = load(ctxT.count, ctxT.ap[:, :, :],
                                        I["ctxT"][:, b, :].rearrange("(k p) s -> p k s", p=P), ctxT.free)
                        ctxT.free = []
                    return [step]

                wide = 1 if softmax else 2
                kp = Slot(sbuf(sc, "kp", [P, KC, 3, CTX], BF16))
                kp_stores = [dma_count(f"{tag}_kp{c}") for c in range(KC)]
                qp = Slot(sbuf(sc, "qp", [P, KC, 3, SEQ], BF16))
                qp_stores = [dma_count(f"{tag}_qp{c}") for c in range(KC)]
                rest = Ring([Slot(sbuf(sc, "rest", [P, BANK])) for _ in range(2)])
                vt = Ring([Slot(sbuf(sc, "vt", [P, len(KEY_CHUNKS), HEADS, VW])) for _ in range(2)])
                kst = [Slot(sbuf(sc, "kst", [P, GROUP, CTX], BF16), dma_count(f"{tag}_kst{i}")) for i in range(3)]
                qst = [Slot(sbuf(sc, "qst", [P, GROUP, SEQ], BF16), dma_count(f"{tag}_qst{i}")) for i in range(3)]
                probs = Ring([Slot(sbuf(sc, "probs", [P, wide, BANK])) for _ in range(PROBS // wide)])
                accs = Slot(sbuf(sc, "accs", [P, BANK]))
                rsmall = sbuf(sc, "rsmall", [P, 4 * GROUP])
                rden = Slot(sbuf(sc, "rden", [P, 4 * GROUP, 32]))
                ctxn = Slot(sbuf(sc, "ctxn", [P, GROUPS, SEQ]))
                mpart = Slot(sbuf(sc, "mpart", [P, 4 * GROUP, MAX_SPLIT]))
                mrow = sbuf(sc, "mrow", [P, 4 * GROUP])
                mrest = sbuf(sc, "mrest", [P, 4 * GROUP])
                mpb = sbuf(sc, "mpb", [P, MAX_ROWS, 4 * GROUP], BF16)
                mT = Slot(sbuf(sc, "mT", [MAX_ROWS * 4 * GROUP, P], BF16), dma_count(f"{tag}_mT"))

                s_slots = Ring([banks[i:i + wide] for i in ((0, 1, 2) if softmax else (0, 2, 4))])
                acc = banks[3 if softmax else 6]
                m_banks = Ring(banks[4:7])
                misc = Ring(banks[7:8])
                prelude = Ring([banks[i] for i in ((4, 5, 6, 7) if softmax else (3, 4, 5, 7))])
                turn_banks = Ring(banks[0:3])

                S["ones"] = wo_zero

                def fill_ones(slot, part, engine=pool):
                    def step():
                        S["ones"] = engine(lambda e: e.memset(part, 1.0), start, S["ones"])
                        slot.free = [S["ones"]]
                    return step

                if softmax:
                    fill_ones(kst[0], kst[0].ap[:, :, :], dve)()
                for s in vt.slots:
                    fill_ones(s, s.ap[:, :, :, DH:VW])()
                ones_later = [fill_ones(s, s.ap[:, :, :]) for s in kst[1:]] if softmax else []

                def add_output_bias():
                    if biased:
                        bo_rows = bo[:, :].unsqueeze(1).to_broadcast([P, TILES, DM])
                        S["x_biased"] = pool(lambda e: e.tensor_tensor(x[:, :, :], x[:, :, :], bo_rows, ALU.add),
                                             hT_ready, w_ready, S["ones"], x_ready)
                    else:
                        S["x_biased"] = x_ready

                acc.free = [dve(lambda e: e.memset(acc.ap, 0.0), acc.free)]


                def split(dst, part_slot, bank, n, bias, mmt):
                    r = rest.next()
                    v = r.ap[:, 0:n]
                    src = bank.ap[:, 0:n]
                    if bias is None:
                        hi = act(lambda e: e.activation(dst(0), src, ACT.Copy), mmt, part_slot.free)
                        r1 = dve(lambda e: e.tensor_tensor(v, src, dst(0), ALU.subtract), hi, r.free)
                    else:
                        hi = act(lambda e: e.activation(dst(0), src, ACT.Identity, bias=bias), mmt,
                                 w_ready, part_slot.free)
                        r1 = dve(lambda e: e.scalar_tensor_tensor(out=v, in0=src, scalar=bias, in1=dst(0),
                                                                  op0=ALU.add, op1=ALU.subtract), hi, r.free)
                    bank.free = [r1]
                    mid = act(lambda e: e.activation(dst(1), v, ACT.Copy), r1)
                    lo = pool(lambda e: e.tensor_tensor(dst(2), v, dst(1), ALU.subtract), mid)
                    r.free = [lo]
                    return [mid, lo]

                def make_keys(b, c, misc=misc):
                    steps = []
                    for k0, kn in KEY_BLOCKS:
                        def step(k0=k0, kn=kn):
                            bank = misc.next()
                            t = mm(bank.ap[:, 0:kn], [(wk[:, k, c * P:(c + 1) * P], ctxT.ap[:, k, k0:k0 + kn])
                                                      for k in range(KC)], S["ctx"], wk_ready, bank.free)
                            ctxT.free.append(t)
                            S.setdefault(("kp", b, c), []).append(split(
                                lambda part: kp.ap[:, c, part, k0:k0 + kn], kp, bank, kn,
                                bk[:, c:c + 1] if biased else None, t))
                        steps.append(step)

                    def store():
                        dst = k_parts_dram[b % 2, 8 * c:8 * c + 8].rearrange("h (d a) t -> (h d) a t", a=3)
                        last = load(kp_stores[c], dst, kp.ap[:, c, :, :],
                                    S[("kp", b, c)], S.get(("kst_read", b - 2)))
                        S["k_stored", b, c] = last
                        kp.free = [last] if c == 0 else kp.free + [last]
                    return steps + [store]

                def make_queries(b, misc=misc):
                    steps = []
                    for c in range(KC):
                        def step(c=c):
                            bank = misc.next()
                            t = mm(bank.ap, [(wq[:, k, c * P:(c + 1) * P], hT[:, k, b * SEQ:(b + 1) * SEQ])
                                             for k in range(KC)], hT_ready[b], w_ready, bank.free)
                            S["qp", b, c] = split(lambda part: qp.ap[:, c, part, :], qp, bank, SEQ,
                                                  bq[:, c:c + 1] if biased else None, t)
                            hT_free[b].append(t)
                        steps.append(step)

                        def store(c=c):
                            for j, part in enumerate(Q_PART):
                                first, step_ = divmod(j, 3)
                                rows = slice(3 * DH * first + step_, min(3 * DH * (first + 1), PAIR_ROWS),
                                             3 if first < 2 else 1)
                                last = load(qp_stores[c], q_parts_dram[b % 2, 8 * c:8 * c + 8, rows, :],
                                            qp.ap[:, c, part, :], S["qp", b, c], S.get(("kst_read", b - 2)))
                            S["q_stored", b, c] = last
                            qp.free = [last] if c == 0 else qp.free + [last]
                        steps.append(store)
                    return steps

                def make_values(b, misc=misc):
                    slot = vt.slots[b % 2]
                    steps = []
                    for i in range(0, len(KEY_CHUNKS), 2):
                        def step(i=i):
                            bank = misc.next()
                            chunks = KEY_CHUNKS[i:i + 2]
                            for j, (k0, kn) in enumerate(chunks):
                                t = mm(bank.ap[0:kn, j * DM:(j + 1) * DM],
                                       [(ctxT.ap[:, k, k0:k0 + kn], wv[:, k, :]) for k in range(KC)],
                                       S["ctx"], w_ready, bank.free)
                            n = len(chunks)
                            dst = slot.ap[0:kn, i:i + n, :, 0:DH]
                            src = bank.ap[0:kn, 0:n * DM].rearrange("p (c h d) -> p c h d", c=n, d=DH)
                            if biased:
                                rows = bv[0:kn, :].rearrange("p (h d) -> p h d", d=DH).unsqueeze(1)
                                rows = rows.to_broadcast([kn, n, HEADS, DH])
                                e = dve(lambda e: e.tensor_tensor(dst, src, rows, ALU.add), t, slot.free, w_ready)
                            else:
                                e = dve(lambda e: e.tensor_copy(dst, src), t, slot.free)
                            ctxT.free.append(t)
                            bank.free = [e]
                            S["v", b] = [e, slot.free]
                        steps.append(step)
                    return steps

                def load_unit(u):
                    b, g = divmod(u, GROUPS)

                    def step():
                        ks, qs = kst[u % 3], qst[u % 3]
                        stored = [S["k_stored", b, 4 * g // 8], S["q_stored", b, 4 * g // 8]]
                        src = k_parts_dram[b % 2, 4 * g:4 * g + 4, :, :].rearrange("h r t -> r h t")
                        load(ks.count, ks.ap[0:48, :, :], src, stored, ks.free)
                        load(ks.count, ks.ap[48:96, :, :], src, stored, ks.free)
                        t = load(ks.count, ks.ap[96:PAIR_ROWS, :, :], src[0:3 * DH:3], stored, ks.free)
                        q = load(qs.count, qs.ap[0:PAIR_ROWS, :, :],
                                 q_parts_dram[b % 2, 4 * g:4 * g + 4, :, :].rearrange("h r t -> r h t"),
                                 stored, qs.free)
                        S["unit", u] = [t, q, list(ks.free)]
                        if g == GROUPS - 1:
                            S["kst_read", b] = [t, q]
                    return [step]

                def maxima(u):
                    ks, qs = kst[u % 3], qst[u % 3]
                    steps = []
                    for h in range(GROUP):
                        for qt in range(SEQ // P):
                            row = h * (SEQ // P) + qt
                            for i, (k0, kn) in enumerate(MAX_BLOCKS):
                                def step(h=h, qt=qt, row=row, i=i, k0=k0, kn=kn):
                                    bank = m_banks.next()
                                    t = mm(bank.ap[:, 0:kn], [(qs.ap[0:PAIR_ROWS, h, qt * P:(qt + 1) * P],
                                                               ks.ap[0:PAIR_ROWS, h, k0:k0 + kn])],
                                           S["unit", u], bank.free)
                                    r = dve(lambda e: e.tensor_reduce(mpart.ap[:, row, i:i + 1], bank.ap[:, 0:kn],
                                                                      AX.X, ALU.max), t, mpart.free)
                                    bank.free = [r]
                                    S["max", u] = r
                                steps.append(step)

                    def close():
                        t = dve(lambda e: e.tensor_reduce(mrow[:, :], mpart.ap[:, :, :], AX.X, ALU.max), S["max", u])
                        mpart.free = [t]
                        a = dve(lambda e: e.tensor_scalar(mpb[:, 0, :], mrow[:, :], -1.0, None, ALU.mult), t,
                                S.get("mpb_free"))
                        a = dve(lambda e: e.scalar_tensor_tensor(out=mrest[:, :], in0=mrow[:, :], scalar=-1.0,
                                                                 in1=mpb[:, 0, :], op0=ALU.mult, op1=ALU.subtract), a)
                        a = dve(lambda e: e.tensor_copy(mpb[:, 1, :], mrest[:, :]), a)
                        a = dve(lambda e: e.tensor_tensor(mpb[:, 2, :], mrest[:, :], mpb[:, 1, :], ALU.subtract), a)
                        S["mparts", u] = a

                    def turn():
                        bank = misc.next()
                        rows = MAX_ROWS * 4 * GROUP
                        view = bank.ap.bitcast(BF16)[0:rows, 0:P]
                        t = pe(lambda e: e.transpose(view, mpb[:, :, :].rearrange("p a b -> p (a b)"), identb[:, :]),
                               S["mparts", u], identb_ready, bank.free)
                        S["mpb_free"] = t
                        c = act(lambda e: e.activation(mT.ap[:, :], view, ACT.Copy), t, mT.free)
                        bank.free = [c]
                        for i in range(MAX_ROWS):
                            d = load(mT.count, qs.ap[PAIR_ROWS + i:PAIR_ROWS + i + 1, :, :]
                                     .rearrange("p h (a q) -> p (h a) q", q=P),
                                     mT.ap[i * 4 * GROUP:(i + 1) * 4 * GROUP, :], c, qs.free, S["unit", u])
                        mT.free = [d]
                        S["maxrows", u] = d
                    return steps + [close, turn]

                def finish(u):
                    b, g = divmod(u, GROUPS)

                    def evacuate():
                        if softmax:
                            t = act(lambda e: e.activation(accs.ap[:, :], acc.ap, ACT.Copy), S["acc", u], accs.free)
                        else:
                            t = dve(lambda e: e.tensor_copy(ctxn.ap[:, g, :], acc.ap), S["acc", u], ctxn.free)
                            S["ctxn", b] = t
                        acc.free = [t]
                        S["accs", u] = t

                    def denominators():
                        bank = misc.next()
                        for qt in range(SEQ // P):
                            t = mm(bank.ap[:, qt * GROUP:(qt + 1) * GROUP],
                                   [(accs.ap[:, qt * P:(qt + 1) * P], sel_den[:, :])], S["accs", u], sel_ready, bank.free)
                        r = dve(lambda e: e.reciprocal(rsmall[:, :], bank.ap[:, 0:4 * GROUP]), t, rden.free)
                        bank.free = [r]
                        r = pool(lambda e: e.tensor_copy(
                            rden.ap[:, :, :], rsmall[:, :].unsqueeze(2).to_broadcast([P, 4 * GROUP, 32])), r)
                        S["rden", u] = r

                    def divide():
                        bank = misc.next()
                        for qt in range(SEQ // P):
                            spread = rden.ap[:, qt * GROUP:(qt + 1) * GROUP, :].rearrange("p j r -> p (j r)")
                            t = mm(bank.ap[:, qt * P:(qt + 1) * P], [(spread, ident[:, :])],
                                   S["rden", u], bank.free)
                        r = dve(lambda e: e.tensor_tensor(ctxn.ap[:, g, :], accs.ap[:, :], bank.ap, ALU.mult),
                                t, ctxn.free)
                        rden.free, accs.free, bank.free = [t], [r], [r]
                        S["ctxn", b] = r
                    return [evacuate], ([denominators, divide] if softmax else [])

                def project(b):
                    steps = []
                    for t0 in range(0, SEQ // P, 2):
                        def step(t0=t0):
                            bank = misc.next()
                            for j in range(2):
                                q0 = (t0 + j) * P
                                t = mm(bank.ap[:, j * DM:(j + 1) * DM],
                                       [(ctxn.ap[:, g, q0:q0 + P], wo[:, g, :]) for g in range(GROUPS)],
                                       S["ctxn", b], w_ready, bank.free)
                            rows = x[:, 4 * b + t0:4 * b + t0 + 2, :].rearrange("p t d -> p (t d)")
                            a = dve(lambda e: e.tensor_tensor(rows, rows, bank.ap, ALU.add), t, S["x_biased"])
                            bank.free = [a]
                            x_ready[b] = [a] if t0 == 0 else x_ready[b] + [a]
                            ctxn.free = [t]
                        steps.append(step)
                    return steps

                def attend(u):
                    b, g = divmod(u, GROUPS)
                    ks, qs = kst[u % 3], qst[u % 3]
                    rows = STACK if softmax else PAIR_ROWS
                    steps = []
                    made = {}

                    def scores(kc, h0):
                        k0, kn = KEY_CHUNKS[kc]
                        slots, p = s_slots.next(), probs.next()
                        for h, slot in enumerate(slots, h0):
                            t = mm(slot.ap[0:kn, :], [(ks.ap[0:rows, h, k0:k0 + kn], qs.ap[0:rows, h, :])],
                                   S["unit", u], S.get(("maxrows", u)), slot.free)
                        at = banks.index(slots[0])
                        src = psum[0:kn, at:at + wide, :]
                        a = act(lambda e: e.activation(p.ap[0:kn, :, :], src, ACT.Exp if softmax else ACT.Sigmoid,
                                                       scale=DH ** -0.5), t, p.free)
                        for slot in slots:
                            slot.free = [a]
                        p.free = []
                        made[kc, h0] = (p, a)
                        if kc == len(KEY_CHUNKS) - 1 and h0 + wide == GROUP:
                            ks.free, qs.free = [t], [t]

                    def values(kc):
                        k0, kn = KEY_CHUNKS[kc]
                        all_made = [made[kc, h][1] for h in range(0, GROUP, wide)]
                        for h in range(GROUP):
                            p, _ = made[kc, h - h % wide]
                            lhsT = vt.slots[b % 2].ap[0:kn, kc, GROUP * g + h, :]
                            dst, rhs = acc.ap[32 * h:32 * h + VW, :], p.ap[0:kn, h % wide, :]
                            t = pe(lambda e, dst=dst, lhsT=lhsT, rhs=rhs, h=h: e.matmul(
                                dst, lhsT, rhs, start=kc == 0, stop=kc == len(KEY_CHUNKS) - 1,
                                tile_position=(0, 32 * h)), all_made, S["v", b], acc.free)
                            p.free = [t]
                        S["acc", u] = t
                        if g == GROUPS - 1:
                            vt.slots[b % 2].free = [t]

                    for kc in range(len(KEY_CHUNKS)):
                        for h in range(0, GROUP, wide):
                            steps.append(lambda kc=kc, h=h: scores(kc, h))
                            if kc >= LAG and h == BEHIND:
                                steps.append(lambda kc=kc: values(kc - LAG))
                    for kc in range(len(KEY_CHUNKS) - LAG, len(KEY_CHUNKS)):
                        steps.append(lambda kc=kc: values(kc))
                    return steps

                UNITS = BATCH * GROUPS
                timed = spread_over(make_keys(0, 0, prelude), -3.5, -2.5)
                if 0 in mine:
                    timed += spread_over(layer_norm(0, turn_banks), -3.4, -2.6)
                timed += spread_over([s for b in mine if b for s in layer_norm(b, turn_banks)], -2, -1.5)
                timed += spread_over(make_queries(0, prelude), -2.4, -2.2)
                timed += spread_over(load_unit(0), -2.1, -2.1)
                timed += spread_over(make_keys(0, 1, prelude), -2, -1.6)
                timed += spread_over(make_values(0, Ring(misc.slots + (banks[0:3] if softmax else banks[3:4]))), -1.5, -0.3)
                timed += list(zip((-1.45, -1.1), ones_later))
                timed += spread_over(load_unit(1), -1.2, -1.2)
                timed += spread_over(load_ctx(1), -0.25, -0.25)
                timed += spread_over([add_output_bias], -0.2, -0.2)
                for b in range(BATCH):
                    first = b * GROUPS
                    if b + 1 < BATCH:
                        timed += spread_over(make_queries(b + 1), first + 0.05, first + 0.4)
                        timed += spread_over(make_keys(b + 1, 0), first + 0.9, first + 1.7)
                        timed += spread_over(make_keys(b + 1, 1), first + 1.8, first + 2.5)
                        timed += spread_over(make_values(b + 1), first + 2.5, first + 3.8)
                    if b + 2 < BATCH:
                        timed += spread_over(load_ctx(b + 2), first + 3.85, first + 3.85)
                    timed += spread_over(project(b), first + GROUPS + 0.45, first + GROUPS + 0.95)
                    if b + 1 < BATCH:
                        timed += spread_over(next_layer_norm(b, misc), first + GROUPS + 1.3, first + GROUPS + 1.9)
                for u in range(UNITS):
                    timed += spread_over(attend(u), u, u + 1)
                    evacuate, divide = finish(u)
                    timed += spread_over(evacuate, u + 1, u + 1)
                    timed += spread_over(divide, u + 1.1, u + 1.4) if divide else []
                    if softmax:
                        timed += spread_over(maxima(u), u - 1 - LEAD if u else -1.2, u - LEAD)
                    if u + 2 < UNITS:
                        timed += spread_over(load_unit(u + 2), u + 0.02, u + 0.02)
                in_time(timed)
        def iota_rows(sc, n, start):
            t32 = sbuf(sc, "iota_i", [P, n], mybir.dt.int32)
            t = sbuf(sc, "iota", [P, n])
            a = pool(lambda e: e.iota(t32[:, :], pattern=[[1, n]], base=0, channel_multiplier=0), start)
            return t, pool(lambda e: e.tensor_copy(t[:, :], t32[:, :]), a)

        def rows_of(g):
            return slice(g * SEQ, (g + 1) * SEQ)

        def over(ap2, n):
            return ap2.unsqueeze(2).to_broadcast([P, 4, n])

        class Gates:

            def __init__(self, sc, n, top):
                self.n, self.iota = n, iota_rows(sc, n, fence())
                self.v = sbuf(sc, "gate_v", [P, TILES, n])
                self.m = sbuf(sc, "gate_m", [P, TILES])
                self.top8 = sbuf(sc, "gate_top8", [P, TILES, 8])
                self.idx = sbuf(sc, "gate_idx", [P, TILES, 8], U32)
                self.idxf = sbuf(sc, "gate_idxf", [P, TILES, 8])
                self.hot = [sbuf(sc, "gate_hot", [P, TILES, n]) for _ in range(top)]
                self.done = [None] * BATCH

            def softmax(self, g):
                ts = tiles_of(g)
                v, m = self.v[:, ts, :], self.m[:, ts]

                def exponentials():
                    a = dve(lambda e: e.tensor_reduce(m, v, AX.X, ALU.max), self.done[g])
                    a = dve(lambda e: e.tensor_tensor(v, v, over(m, self.n), ALU.subtract), a)
                    self.done[g] = act(lambda e: e.activation(v, v, ACT.Exp), a)

                def divide():
                    a = dve(lambda e: e.tensor_reduce(m, v, AX.X, ALU.add), self.done[g])
                    a = dve(lambda e: e.reciprocal(m, m), a)
                    self.done[g] = dve(lambda e: e.tensor_tensor(v, v, over(m, self.n), ALU.mult), a)
                return [exponentials, idle, divide]

            def largest(self, g):
                ts = tiles_of(g)

                def values():
                    for t in range(4 * g, 4 * g + 4):
                        a = dve(lambda e, t=t: e.max(self.top8[:, t, :], self.v[:, t, :]), self.done[g])
                    self.done[g] = a

                def places():
                    for t in range(4 * g, 4 * g + 4):
                        a = dve(lambda e, t=t: e.max_index(self.idx[:, t, :], self.top8[:, t, :], self.v[:, t, :]),
                                self.done[g])
                    self.done[g] = dve(lambda e: e.tensor_copy(self.idxf[:, ts, :], self.idx[:, ts, :]), a)

                def onehots():
                    iota, iota_ready = self.iota
                    for i, o in enumerate(self.hot):
                        a = dve(lambda e, o=o, i=i: e.tensor_tensor(
                            o[:, ts, :], iota[:, :].unsqueeze(1).to_broadcast([P, 4, self.n]),
                            over(self.idxf[:, ts, i], self.n), ALU.is_equal), self.done[g], iota_ready)
                    self.done[g] = a
                return [values, places, onehots]

            def weigh(self, g, weight):
                ts = tiles_of(g)
                for i, o in enumerate(self.hot):
                    a = dve(lambda e, o=o, i=i: e.tensor_tensor(o[:, ts, :], o[:, ts, :], over(weight(i), self.n),
                                                                ALU.mult), self.done[g])
                self.done[g] = dve(lambda e: e.tensor_tensor(self.v[:, ts, :], self.hot[0][:, ts, :],
                                                             self.hot[1][:, ts, :], ALU.add), a)

        def turn_gates(dst, src, g, n_rows, ring, needs, dst_free=None):
            bank = ring.next()
            for i in range(4):
                t = pe(lambda e, i=i: e.transpose(bank.ap[0:n_rows, i * P:(i + 1) * P], src[:, 4 * g + i, :],
                                                  ident[:, :]), needs, bank.free)
            c = act(lambda e: e.activation(dst, bank.ap[0:n_rows, :], ACT.Copy), t, dst_free)
            bank.free = [c]
            return c

        def by_batch(prepare, main, ring, before=None):
            mine = own_layer_norms()
            timed = [(-2, before)] if before else []
            for g in range(BATCH):
                at = g - 1 if g else -1
                ready = (layer_norm(g, ring) if g in mine else []) + prepare(g)
                timed += spread_over(ready, at + 0.1, at + 0.85)
                timed += spread_over(main(g), g, g + 1)
                if g + 1 < BATCH:
                    timed += spread_over(next_layer_norm(g, ring), g + 1.1, g + 1.9)
            in_time(timed)

        def place_vectors(sc, **columns):
            return {name: sbuf(sc, name, [P, n]) for name, n in columns.items()}

        E0 = 8

        def ffn0_inputs(sc):
            w = {"we": sbuf(sc, "we", [P, KC, E0, DM]), "be": sbuf(sc, "be", [E0, DM]), "wg": sbuf(sc, "wg", [P, KC, E0])}

            def start_loads(start, behind):
                G, W = input_count("ffn0_gate"), input_count("ffn0_w")
                w["gate_ready"] = fill_weight(G, w["wg"], I["L0_ffn_Wg"], start, behind)
                load(W, w["be"][:, :], I["L0_ffn_be"], start, behind)
                for k in range(KC):
                    w["ready"] = load(W, w["we"][:, k, :, :],
                                      I["L0_ffn_We"][:, k * P:(k + 1) * P, :].rearrange("e p n -> p e n"), start, behind)
            return w, start_loads

        def ffn0(w):
            with ExitStack() as sc:
                gates = Gates(sc, E0, 2)
                dT = sbuf(sc, "dT", [E0, TOK])
                dT_ready = {}
                ring = Ring(banks)

                def prepare(g):
                    ts = tiles_of(g)

                    def logits():
                        token_logits(gates, g, w["wg"], w["gate_ready"], ring)

                    def shares():
                        top, m = gates.top8[:, ts, :], gates.m[:, ts]
                        a = dve(lambda e: e.tensor_tensor(m, top[:, :, 0], top[:, :, 1], ALU.add), gates.done[g])
                        a = dve(lambda e: e.reciprocal(m, m), a)
                        gates.done[g] = dve(lambda e: e.tensor_tensor(top[:, :, 0:2], top[:, :, 0:2], over(m, 2),
                                                                      ALU.mult), a)

                    def turn():
                        dT_ready[g] = turn_gates(dT[:, rows_of(g)], gates.v, g, E0, ring, gates.done[g])
                    return [logits] + gates.softmax(g) + gates.largest(g) + [
                        shares, lambda: gates.weigh(g, lambda i: gates.top8[:, ts, i]), idle, turn]

                def main(g):
                    steps = []
                    for t in range(4 * g, 4 * g + 4):
                        cols = slice(t * P, (t + 1) * P)
                        for e2 in range(E0 // 2):
                            def step(t=t, e2=e2, cols=cols):
                                bank = ring.next()
                                m = mm(bank.ap, [(hT[:, k, cols], w["we"][:, k, 2 * e2:2 * e2 + 2, :]
                                                  .rearrange("p e n -> p (e n)")) for k in range(KC)],
                                       hT_ready[g], w["ready"], bank.free)
                                hT_free[g] = [m]
                                for i in range(2):
                                    a = dve(lambda e, i=i: e.scalar_tensor_tensor(
                                        out=x[:, t, :], in0=bank.ap[:, i * DM:(i + 1) * DM],
                                        scalar=gates.v[:, t, 2 * e2 + i:2 * e2 + i + 1],
                                        in1=x[:, t, :], op0=ALU.mult, op1=ALU.add), m, gates.done[g], x_ready[g])
                                    x_ready[g] = [a]
                                bank.free = [a]
                            steps.append(step)

                        def biases(t=t, cols=cols):
                            bank = ring.next()
                            m = mm(bank.ap[:, 0:DM], [(dT[:, cols], w["be"][:, :])], dT_ready[g], w["ready"], bank.free)
                            a = dve(lambda e: e.tensor_tensor(x[:, t, :], x[:, t, :], bank.ap[:, 0:DM], ALU.add),
                                    m, x_ready[g])
                            x_ready[g] = bank.free = [a]
                        steps.append(biases)
                    return steps
                by_batch(prepare, main, ring)

        def token_logits(gates, g, w, w_ready, ring, after=lambda dst, src, m: dve(
                lambda e: e.tensor_copy(dst, src), m)):
            n = w.shape[2]
            bank = ring.next()
            for i in range(4):
                t = 4 * g + i
                m = mm(bank.ap[:, i * n:(i + 1) * n], [(hT[:, k, t * P:(t + 1) * P], w[:, k, :]) for k in range(KC)],
                       hT_ready[g], w_ready, bank.free)
            hT_free[g] = [m]
            src = bank.ap[:, 0:4 * n].rearrange("p (t e) -> p t e", e=n)
            gates.done[g] = after(gates.v[:, tiles_of(g), 0:n], src, m)
            bank.free = [gates.done[g]]

        FC = SEQ // P

        def autocorrelation_inputs(sc):
            w = {name: sbuf(sc, name, [P, KC, DM]) for name in ("wq", "wk", "wv", "wo")}
            w |= place_vectors(sc, bq=DM, bk=DM, bv=DM, bo=DM)
            w |= {name: sbuf(sc, name, [P, FC, SEQ]) for name in ("fwd", "inv")}

            def start_loads(start, behind):
                W = input_count("l1x_w")
                for name in ("wq", "wk", "wv", "wo"):
                    fill_weight(W, w[name], I["L1_xattn_W" + name[1]], start, behind)
                for name in ("bq", "bk", "bv", "bo"):
                    fill_rows(W, w[name], I["L1_xattn_" + name], start, behind)
                fill_weight(W, w["fwd"], I["dft"], start, behind)
                w["ready"] = fill_weight(W, w["inv"], I["idft"], start, behind)
            return w, start_loads

        def autocorrelation(w):
            TOP = 6
            NB = BATCH * HEADS
            start = fence()
            mine = own_layer_norms()
            w_ready, fwd, inv = w["ready"], w["fwd"], w["inv"]
            with ExitStack() as sc:
                ctx = [Slot(sbuf(sc, "ctx", [P, KC, SEQ]), dma_count(f"l1x_ctx{i}")) for i in range(BATCH)]
                ctx_ready = [load(ctx[b].count, ctx[b].ap[:, :, :],
                                  I["ctxT"][:, b, 0:SEQ].rearrange("(k p) s -> p k s", p=P), start)
                             for b in range(BATCH)]
                iota, iota_ready = iota_rows(sc, SEQ, start)
                time_ = Ring([Slot(sbuf(sc, "time", [P, FC, DM])) for _ in range(2)])
                freq = Ring([Slot(sbuf(sc, "freq", [P, FC, DM])) for _ in range(2)])
                vf = [sbuf(sc, "vf", [P, FC, DM]) for _ in range(BATCH)]
                prod = Ring([Slot(sbuf(sc, "prod", [P, 2, DM])) for _ in range(2)])
                cross = [sbuf(sc, "cross", [P, 2, NB]) for _ in range(4)]
                for s in time_.slots + freq.slots + prod.slots:
                    s.free = [start]
                ring = Ring(banks)
                vf_ready, S = {}, {"cross": []}

                def linear(left, name, left_ready, on_read):
                    dst = time_.next()
                    bias = w["b" + name]

                    def step(t0):
                        bank = ring.next()
                        for j in range(2):
                            m = mm(bank.ap[:, j * DM:(j + 1) * DM],
                                   [(left(k, t0 + j), w["w" + name][:, k, :]) for k in range(KC)],
                                   left_ready(), w_ready, bank.free)
                        a = dve(lambda e: e.tensor_tensor(
                            dst.ap[:, t0:t0 + 2, :], bank.ap.rearrange("p (t d) -> p t d", d=DM),
                            bias[:, :].unsqueeze(1).to_broadcast([P, 2, DM]), ALU.add), m, dst.free)
                        bank.free = [a]
                        dst.ready = a
                        on_read(m)
                    return dst, [lambda: step(0), lambda: step(2)]

                def spectrum(dst, src):
                    def step(f0):
                        bank = ring.next()
                        for j in range(2):
                            f = f0 + j
                            m = mm(bank.ap[:, j * DM:(j + 1) * DM],
                                   [(fwd[:, t, f * P:(f + 1) * P], src.ap[:, t, :]) for t in range(FC)],
                                   src.ready, w_ready, bank.free)
                        a = act(lambda e: e.activation(dst.ap[:, f0:f0 + 2, :].rearrange("p f d -> p (f d)"),
                                                       bank.ap, ACT.Copy), m, dst.free)
                        bank.free = [a]
                        dst.ready = a
                        if f0:
                            src.free = [m]
                    return [lambda: step(0), lambda: step(2)]

                def correlate(b):
                    def use_hT(m):
                        hT_free[b] = [m]

                    q, q_steps = linear(lambda k, t: hT[:, k, b * SEQ + t * P:b * SEQ + (t + 1) * P], "q",
                                        lambda: hT_ready[b], use_hT)
                    k_, k_steps = linear(lambda k, t: ctx[b].ap[:, k, t * P:(t + 1) * P], "k",
                                         lambda: ctx_ready[b], lambda m: None)
                    qf, kf = freq.next(), freq.next()

                    def products():
                        for i, (qo, ko) in enumerate(((0, 0), (2, 2), (2, 0), (0, 2))):
                            p = prod.next()
                            a = dve(lambda e, qo=qo, ko=ko, p=p: e.tensor_tensor(
                                p.ap[:, :, :], qf.ap[:, qo:qo + 2, :], kf.ap[:, ko:ko + 2, :], ALU.mult),
                                qf.ready, kf.ready, p.free)
                            qf.free = kf.free = [a]
                            r = dve(lambda e, i=i, p=p: e.tensor_reduce(
                                cross[i][:, :, b * HEADS:(b + 1) * HEADS],
                                p.ap[:, :, :].rearrange("p f (h d) -> p f h d", d=DH), AX.X, ALU.add), a, start)
                            p.free = [r]
                            S["cross"] = [r]
                    return q_steps + k_steps + spectrum(qf, q) + spectrum(kf, k_) + [products]

                def value_spectrum(b):
                    v, steps = linear(lambda k, t: ctx[b].ap[:, k, t * P:(t + 1) * P], "v",
                                      lambda: ctx_ready[b], lambda m: None)
                    dst = Slot(vf[b])
                    dst.free = [start]

                    def done():
                        vf_ready[b] = dst.ready
                    return steps + spectrum(dst, v) + [done]

                hold = sbuf(sc, "hold", [1, NB])
                corr = sbuf(sc, "corr", [NB, SEQ])
                top8 = sbuf(sc, "top8", [NB, 8])
                idx = sbuf(sc, "idx", [NB, 8], U32)
                idxf = sbuf(sc, "idxf", [NB, 8])
                neg = sbuf(sc, "neg", [NB, 1])
                tot = sbuf(sc, "tot", [NB, 1])
                wts = sbuf(sc, "wts", [NB, 8])
                kern = sbuf(sc, "kern", [NB, SEQ])
                term = corr
                kernT = sbuf(sc, "kernT", [P, FC, NB])
                cr, ci, cr2 = sbuf(sc, "cr", [P, 2, NB]), sbuf(sc, "ci", [P, 2, NB]), sbuf(sc, "cr2", [P, 2, NB])
                re, im, qiki = cross[0], cross[2], cross[1]

                def cross_spectrum():
                    a = dve(lambda e: e.tensor_copy(hold[:, :], cross[0][0:1, 0, :]), S["cross"], start)
                    a = dve(lambda e: e.tensor_tensor(re[:, :, :], cross[0][:, :, :], qiki[:, :, :], ALU.add), a)
                    a = dve(lambda e: e.tensor_copy(re[0:1, 0, :], hold[:, :]), a)
                    a = dve(lambda e: e.tensor_tensor(im[:, :, :], cross[2][:, :, :], cross[3][:, :, :],
                                                      ALU.subtract), a)
                    S["re_im"] = dve(lambda e: e.tensor_copy(im[0:1, 0, :], qiki[0:1, 0, :]), a)

                def correlation():
                    bank = ring.next()
                    m = mm(bank.ap[0:NB, :], [(re[:, 0, :], inv[:, 0, :]), (re[:, 1, :], inv[:, 1, :]),
                                              (im[:, 0, :], inv[:, 2, :]), (im[:, 1, :], inv[:, 3, :])],
                           S["re_im"], w_ready, bank.free)
                    a = dve(lambda e: e.tensor_scalar(corr[:, :], bank.ap[0:NB, :], 1.0 / DH, None, ALU.mult), m, start)
                    bank.free = [a]
                    a = dve(lambda e: e.max(top8[:, :], corr[:, :]), a)
                    a = dve(lambda e: e.max_index(idx[:, :], top8[:, :], corr[:, :]), a)
                    a = dve(lambda e: e.tensor_copy(idxf[:, :], idx[:, :]), a)
                    a = dve(lambda e: e.tensor_scalar(neg[:, :], top8[:, 0:1], -1.0, None, ALU.mult), a)
                    a = act(lambda e: e.activation(wts[:, 0:TOP], top8[:, 0:TOP], ACT.Exp, bias=neg[:, 0:1]), a)
                    a = dve(lambda e: e.tensor_reduce(tot[:, :], wts[:, 0:TOP], AX.X, ALU.add), a)
                    a = dve(lambda e: e.reciprocal(tot[:, :], tot[:, :]), a)
                    S["kern"] = dve(lambda e: e.tensor_scalar(wts[:, 0:TOP], wts[:, 0:TOP], tot[:, 0:1], None,
                                                              ALU.mult), a)

                def kernel_term(i):
                    dst = term if i else kern
                    a = dve(lambda e: e.tensor_scalar(dst[:, :], iota[0:NB, :], idxf[:, i:i + 1], wts[:, i:i + 1],
                                                      ALU.is_equal, ALU.mult), S["kern"], iota_ready, start)
                    if i:
                        a = dve(lambda e: e.tensor_tensor(kern[:, :], kern[:, :], term[:, :], ALU.add), a)
                    S["kern"] = a

                def turn_kernel():
                    bank = ring.next()
                    for t in range(FC):
                        m = pe(lambda e, t=t: e.transpose(bank.ap[:, t * NB:(t + 1) * NB],
                                                          kern[:, t * P:(t + 1) * P], ident[0:NB, 0:NB]),
                               S["kern"], bank.free)
                    a = act(lambda e: e.activation(kernT[:, :, :].rearrange("p t n -> p (t n)"),
                                                   bank.ap[:, 0:FC * NB], ACT.Copy), m, start)
                    bank.free = [a]
                    S["kernT"] = a

                def kernel_spectrum():
                    bank = ring.next()
                    for f in range(FC):
                        m = mm(bank.ap[:, f * NB:(f + 1) * NB],
                               [(fwd[:, t, f * P:(f + 1) * P], kernT[:, t, :]) for t in range(FC)],
                               S["kernT"], bank.free)
                    view = bank.ap[:, 0:FC * NB].rearrange("p (f n) -> p f n", n=NB)
                    a1 = dve(lambda e: e.tensor_copy(cr[:, :, :], view[:, 0:2, :]), m, start)
                    a2 = dve(lambda e: e.tensor_copy(cr2[:, :, :], view[:, 0:2, :]), m)
                    a3 = dve(lambda e: e.tensor_copy(ci[:, :, :], view[:, 2:4, :]), m)
                    a4 = dve(lambda e: e.tensor_copy(cr2[0:1, 0, :], ci[0:1, 0, :]), a1, a2, a3)
                    S["c"] = dve(lambda e: e.memset(ci[0:1, 0, :], 0.0), a4)
                    bank.free = [a3]

                of, oT = freq, time_

                def turned(slot):
                    return slot.ap[:, :, :].rearrange("p f d -> p (f d)").rearrange("p (c s) -> p c s", s=SEQ)

                def heads(v):
                    return v.rearrange("p (h d) -> p h d", d=DH)

                def output(b):
                    o, ot = of.next(), oT.next()

                    def per_head(c, f):
                        return c[:, f, b * HEADS:(b + 1) * HEADS].unsqueeze(2).to_broadcast([P, HEADS, DH])

                    def products(f):
                        p1, p2 = prod.next(), prod.next()
                        plans = ((0, cr, 2, ci, o.ap[:, f, :], ALU.add), (2, cr2, 0, ci, o.ap[:, 2 + f, :], ALU.subtract))
                        for n, (v1, c1, v2, c2, dst, op) in enumerate(plans):
                            def times(p, v, c, n=n):
                                left, right = heads(vf[b][:, v + f, :]), per_head(c, f)
                                return dve(lambda e: e.tensor_tensor(heads(p.ap[:, n, :]), left, right, ALU.mult),
                                           S["c"], vf_ready[b], p.free)

                            m1, m2 = times(p1, v1, c1), times(p2, v2, c2)
                            s = dve(lambda e, dst=dst, op=op, n=n: e.tensor_tensor(
                                dst, p1.ap[:, n, :], p2.ap[:, n, :], op), m1, m2, o.free)
                        p1.free = p2.free = [s]
                        o.ready = s

                    def to_time(c):
                        bank = ring.next()
                        m = mm(bank.ap, [(o.ap[:, f, c * P:(c + 1) * P], inv[:, f, :]) for f in range(FC)],
                               o.ready, bank.free)
                        a = act(lambda e: e.activation(turned(ot)[:, c, :], bank.ap, ACT.Copy), m, ot.free)
                        bank.free = [a]
                        if c == KC - 1:
                            o.free = [m]
                        ot.ready = a

                    def project(t0):
                        bank = ring.next()
                        for j in range(2):
                            q0 = (t0 + j) * P
                            m = mm(bank.ap[:, j * DM:(j + 1) * DM],
                                   [(turned(ot)[:, k, q0:q0 + P], w["wo"][:, k, :]) for k in range(KC)], ot.ready, bank.free)
                        rows = x[:, 4 * b + t0:4 * b + t0 + 2, :].rearrange("p t d -> p (t d)")
                        a = dve(lambda e: e.tensor_tensor(rows, rows, bank.ap, ALU.add), m, S["x_biased"])
                        bank.free = [a]
                        x_ready[b] = [a] if t0 == 0 else x_ready[b] + [a]
                        if t0:
                            ot.free = [m]
                    return [lambda: products(0), lambda: products(1)], \
                        [lambda: to_time(0), lambda: to_time(1), lambda: project(0), lambda: project(2)]

                def add_output_bias():
                    bo_rows = w["bo"][:, :].unsqueeze(1).to_broadcast([P, TILES, DM])
                    S["x_biased"] = pool(lambda e: e.tensor_tensor(x[:, :, :], x[:, :, :], bo_rows, ALU.add),
                                         w_ready, hT_ready, x_ready)

                timed = []
                for b in mine:
                    timed += spread_over(layer_norm(b, ring), b - 1, b - 0.1)
                for b in range(BATCH):
                    timed += spread_over(correlate(b), b, b + 1)
                timed.append((BATCH - 0.9, add_output_bias))
                chain = [cross_spectrum, correlation] + [lambda i=i: kernel_term(i) for i in range(TOP)]
                chain += [lambda: None, turn_kernel, lambda: None, kernel_spectrum]
                timed += spread_over(chain, BATCH, BATCH + 3)
                timed += spread_over([s for b in range(BATCH) for s in value_spectrum(b)], BATCH - 0.1, BATCH + 3.5)
                first = BATCH + 4
                for b in range(BATCH):
                    products, rest_ = output(b)
                    at = first + b
                    timed += spread_over(products, at - 0.9, at - 0.4) + spread_over(rest_, at, at + 1)
                    if b + 1 < BATCH:
                        timed += spread_over(next_layer_norm(b, ring), at + 1.2, at + 2)
                in_time(timed)

        E1, INNER = 4, 1024
        IC = INNER // P

        def ffn1_inputs(sc):
            w = {"w1": sbuf(sc, "w1", [P, KC, E1, INNER]), "b1": sbuf(sc, "b1", [E1, INNER]),
                 "wo": sbuf(sc, "wo", [P, IC, DM]), "wr": sbuf(sc, "wr", [P, KC, E1])}
            w |= place_vectors(sc, bo=DM, gam=DM, bet=DM)

            def start_loads(start, behind):
                G, W = input_count("ffn1_router"), input_count("ffn1_w")
                w["router_ready"] = fill_weight(G, w["wr"], I["L1_ffn_W_router"], start, behind)
                load(W, w["b1"][:, :], I["L1_ffn_b1"], start, behind)
                for k in range(KC):
                    load(W, w["w1"][:, k, :, :], I["L1_ffn_W1"][:, k * P:(k + 1) * P, :].rearrange("e p n -> p e n"),
                         start, behind)
                fill_weight(W, w["wo"], I["L1_ffn_Wo"], start, behind)
                fill_rows(W, w["bo"], I["L1_ffn_bo"], start, behind)
                fill_rows(W, w["gam"], I["L1_ffn_ln_gamma"], start, behind)
                w["ready"] = fill_rows(W, w["bet"], I["L1_ffn_ln_beta"], start, behind)
            return w, start_loads

        def ffn1(w):
            start = fence()
            with ExitStack() as sc:
                w1, b1, wo, w_ready = w["w1"], w["b1"], w["wo"], w["ready"]
                gates = Gates(sc, 8, 1)
                low = dve(lambda e: e.memset(gates.v[:, :, :], -3.4e38), start)
                hotT = Ring([Slot(sbuf(sc, "hotT", [8, SEQ])) for _ in range(2)])
                pick = sbuf(sc, "pick", [8, E1, P])
                p = pool(lambda e: e.memset(pick[:, :, :], 0.0), start)
                pick_ready = pool(lambda e: e.affine_select(
                    out=pick[:, :, :], in_=pick[:, :, :], compare_op=ALU.not_equal, fill=1.0, base=0,
                    pattern=[[-1, E1], [0, P]], channel_multiplier=1), p)
                masked = Ring([Slot(sbuf(sc, "masked", [P, E1, KC, SEQ])) for _ in range(2)])
                inner = Ring([Slot(sbuf(sc, "inner", [P, IC, SEQ])) for _ in range(1)])
                ybuf = Ring([Slot(sbuf(sc, "y", [P, 4, DM])) for _ in range(2)])
                mean2, veps2 = sbuf(sc, "meanvar2", [P, TILES, 2]), sbuf(sc, "veps2", [P, TILES])
                rstd2, ntmp2 = sbuf(sc, "rstd2", [P, TILES]), sbuf(sc, "ntmp2", [P, TILES])
                for s in hotT.slots + masked.slots + inner.slots + ybuf.slots:
                    s.free = [start]
                ring = Ring(banks)
                S = {}

                def prepare(g):
                    hot, mk = hotT.next(), masked.next()
                    S["masked", g] = hot, mk

                    def logits():
                        token_logits(gates, g, w["wr"], w["router_ready"], ring,
                                     lambda dst, src, m: dve(lambda e: e.tensor_copy(dst, src), m, low))

                    def turn():
                        hot.ready = turn_gates(hot.ap[:, :], gates.hot[0], g, 8, ring, gates.done[g], hot.free)

                    def mask(ex):
                        bank = ring.next()
                        m = mm(bank.ap, [(pick[:, ex, :], hot.ap[:, :])], hot.ready, pick_ready, bank.free)
                        for k in range(KC):
                            a = dve(lambda e, k=k: e.tensor_tensor(mk.ap[:, ex, k, :], hT[:, k, rows_of(g)], bank.ap,
                                                                   ALU.mult), m, mk.free, hT_ready[g])
                        hT_free[g] = bank.free = [a]
                        mk.ready = a
                    return [logits] + gates.largest(g) + [idle, turn] + [lambda ex=ex: mask(ex) for ex in range(E1)]

                def main(g):
                    inn, y = inner.next(), ybuf.next()
                    ts = tiles_of(g)

                    def residual():
                        for i in range(4):
                            a = normed(y.ap[:, i, :], x[:, 4 * g + i, :], 4 * g + i, y.free, x_ready[g])
                        y.ready = pool(lambda e: e.tensor_tensor(
                            y.ap[:, :, :], y.ap[:, :, :], w["bo"][:, :].unsqueeze(1).to_broadcast([P, 4, DM]), ALU.add),
                            a, w_ready)
                        x_ready[g] = [pool(lambda e: e.tensor_tensor(
                            x[:, ts, :], x[:, ts, :], w["bet"][:, :].unsqueeze(1).to_broadcast([P, 4, DM]), ALU.add), a)]

                    def first(i):
                        hot, mk = S["masked", g]
                        bank = ring.next()
                        cols = slice(i * P, (i + 1) * P)
                        pairs = [(b1[:, cols], hot.ap[0:E1, :])]
                        pairs += [(w1[:, k, ex, cols], mk.ap[:, ex, k, :]) for ex in range(E1) for k in range(KC)]
                        m = mm(bank.ap, pairs, mk.ready, hot.ready, w_ready, bank.free)
                        inn.ready = act(lambda e: e.activation(inn.ap[:, i, :], bank.ap, ACT.Gelu), m, inn.free)
                        bank.free = [inn.ready]
                        if i == IC - 1:
                            mk.free, hot.free = [m], [m]

                    def second(i):
                        bank = ring.next()
                        m = mm(bank.ap[:, 0:DM], [(inn.ap[:, j, i * P:(i + 1) * P], wo[:, j, :]) for j in range(IC)],
                               inn.ready, bank.free)
                        a = dve(lambda e: e.tensor_tensor(y.ap[:, i, :], y.ap[:, i, :], bank.ap[:, 0:DM], ALU.add),
                                m, y.ready)
                        bank.free = [a]
                        S["y_stats", g] = moments(y.ap[:, i, :], 4 * g + i, a, mean2)
                        if i == 3:
                            inn.free = [m]
                    return [residual] + [lambda i=i: first(i) for i in range(IC)] + \
                        [lambda i=i: second(i) for i in range(4)]

                def close(g):
                    ts = tiles_of(g)
                    y = ybuf.slots[g % 2]

                    power, newton = rsqrt(ts, 1e-12, (mean2, veps2, rstd2, ntmp2))

                    def root():
                        S["r2"] = newton()

                    def scale():
                        for i in range(4):
                            n = normed(y.ap[:, i, :], y.ap[:, i, :], 4 * g + i, S["r2"], stat=(mean2, rstd2))
                        S["gam"] = pool(lambda e: e.tensor_tensor(
                            y.ap[:, :, :], y.ap[:, :, :], w["gam"][:, :].unsqueeze(1).to_broadcast([P, 4, DM]),
                            ALU.mult), n)

                    def add():
                        x_ready[g] = y.free = [dve(lambda e: e.tensor_tensor(x[:, ts, :], x[:, ts, :], y.ap[:, :, :],
                                                                             ALU.add), S["gam"], x_ready[g])]
                    return [lambda: power(S["y_stats", g]), root, scale, idle, add]

                mine = own_layer_norms()
                timed = []
                for g in range(BATCH):
                    ready = (layer_norm(g, ring) if g in mine else []) + prepare(g)
                    timed += spread_over(ready, g - 0.9, g - 0.15)
                    timed += spread_over(main(g), g, g + 1)
                    timed += spread_over(close(g), g + 1.02, g + 1.3)
                    if g + 1 < BATCH:
                        timed += spread_over(next_layer_norm(g, ring), g + 1.4, g + 1.9)
                in_time(timed)

        E2 = 8

        def ffn2_inputs(sc):
            w = {"wsi": sbuf(sc, "wsi", [P, KC, 2 * DM]), "w1": sbuf(sc, "w1", [P, KC, 2 * DM]),
                 "w2": sbuf(sc, "w2", [P, KC, E2, DM]), "wso": sbuf(sc, "wso", [P, KC, DM]),
                 "wg": sbuf(sc, "wg", [P, KC, E2])}
            w |= place_vectors(sc, gb=E2)

            def start_loads(start, behind):
                G, H, W = input_count("ffn2_gate"), input_count("ffn2_hidden"), input_count("ffn2_w")
                fill_weight(G, w["wg"], I["L2_ffn_w_gate"], start, behind)
                w["gate_ready"] = fill_rows(G, w["gb"], I["L2_ffn_gate_bias"], start, behind)
                fill_weight(H, w["wsi"], I["L2_ffn_w_shared_in"], start, behind)
                w["hidden_ready"] = fill_weight(H, w["w1"], I["L2_ffn_w1_shared"], start, behind)
                fill_weight(W, w["wso"], I["L2_ffn_w_shared_out"], start, behind)
                for k in range(KC):
                    w["ready"] = load(W, w["w2"][:, k, :, :],
                                      I["L2_ffn_w2"][:, k * P:(k + 1) * P, :].rearrange("e p n -> p e n"), start, behind)
            return w, start_loads

        def ffn2(w):
            start = fence()
            with ExitStack() as sc:
                gates = Gates(sc, E2, 2)
                hidden = Ring([Slot(sbuf(sc, "hidden", [P, 2, KC, SEQ])) for _ in range(2)])
                silu = Ring([Slot(sbuf(sc, "silu", [P, SEQ])) for _ in range(2)])
                for s in hidden.slots + silu.slots:
                    s.free = [start]
                ring = Ring(banks)

                def prepare(g):
                    ts = tiles_of(g)

                    def logits():
                        gb = w["gb"][:, :].unsqueeze(1).to_broadcast([P, 4, E2])
                        token_logits(gates, g, w["wg"], w["gate_ready"], ring,
                                     lambda dst, src, m: dve(lambda e: e.tensor_tensor(dst, src, gb, ALU.add), m))
                    return [logits] + gates.softmax(g) + gates.largest(g) + [
                        lambda: gates.weigh(g, lambda i: gates.top8[:, ts, i])]

                def main(g):
                    hid = hidden.next()
                    steps = []
                    for which, name in enumerate(("wsi", "w1")):
                        for c in range(KC):
                            def half_hidden(which=which, name=name, c=c):
                                ba, bb, s = ring.next(), ring.next(), silu.next()
                                ma, mb = [mm(bank.ap, [(w[name][:, k, at + c * P:at + (c + 1) * P],
                                                        hT[:, k, rows_of(g)]) for k in range(KC)],
                                             hT_ready[g], w["hidden_ready"], bank.free)
                                          for bank, at in ((ba, 0), (bb, DM))]
                                hT_free[g] = [mb]
                                a = act(lambda e: e.activation(s.ap[:, :], ba.ap, ACT.Silu), ma, s.free)
                                ba.free = [a]
                                hid.ready = dve(lambda e: e.tensor_tensor(hid.ap[:, which, c, :], s.ap[:, :], bb.ap,
                                                                          ALU.mult), a, mb, hid.free)
                                s.free = [hid.ready]
                                bb.free = [hid.ready]
                            steps.append(half_hidden)
                    for j in range(4):
                        t = 4 * g + j
                        cols = slice(j * P, (j + 1) * P)

                        def shared(t=t, cols=cols):
                            bank = ring.next()
                            m = mm(bank.ap[:, 0:DM], [(hid.ap[:, 0, k, cols], w["wso"][:, k, :]) for k in range(KC)],
                                   hid.ready, w["ready"], bank.free)
                            a = dve(lambda e: e.tensor_tensor(x[:, t, :], x[:, t, :], bank.ap[:, 0:DM], ALU.add),
                                    m, x_ready[g])
                            x_ready[g] = bank.free = [a]
                        steps.append(shared)
                        for e2 in range(E2 // 2):
                            def routed(t=t, e2=e2, cols=cols):
                                bank = ring.next()
                                m = mm(bank.ap, [(hid.ap[:, 1, k, cols], w["w2"][:, k, 2 * e2:2 * e2 + 2, :]
                                                  .rearrange("p e n -> p (e n)")) for k in range(KC)],
                                       hid.ready, w["ready"], bank.free)
                                for i in range(2):
                                    a = dve(lambda e, i=i: e.scalar_tensor_tensor(
                                        out=x[:, t, :], in0=bank.ap[:, i * DM:(i + 1) * DM],
                                        scalar=gates.v[:, t, 2 * e2 + i:2 * e2 + i + 1],
                                        in1=x[:, t, :], op0=ALU.mult, op1=ALU.add), m, gates.done[g], x_ready[g])
                                    x_ready[g] = [a]
                                bank.free = [a]
                                hid.free = [m]
                            steps.append(routed)
                    return steps
                by_batch(prepare, main, ring)

        E3, RH = 16, 128

        def ffn3_inputs(sc):
            w = {"w1": sbuf(sc, "w1", [P, KC, RH]), "wg1": sbuf(sc, "wg1", [P, KC, RH]),
                 "w2": sbuf(sc, "w2", [P, 1, E3]), "wg2": sbuf(sc, "wg2", [P, 1, 1]),
                 "scale_bias": sbuf(sc, "scale_bias", [E3, 2, DM])}
            w |= place_vectors(sc, b1=1, bg1=1, b2=E3, bg2=1)

            def start_loads(start, behind):
                W = input_count("ffn3_w")
                for name, src in (("w1", "W1"), ("wg1", "Wg1"), ("w2", "W2"), ("wg2", "Wg2")):
                    fill_weight(W, w[name], I["L3_ffn_" + src], start, behind)
                fill_columns(W, w["b1"], I["L3_ffn_b1"], start, behind)
                fill_columns(W, w["bg1"], I["L3_ffn_bg1"], start, behind)
                fill_rows(W, w["b2"], I["L3_ffn_b2"], start, behind)
                fill_rows(W, w["bg2"], I["L3_ffn_bg2"], start, behind)
                load(W, w["scale_bias"][:, 0, :], I["L3_ffn_expert_scales"], start, behind)
                w["ready"] = load(W, w["scale_bias"][:, 1, :], I["L3_ffn_expert_biases"], start, behind)
            return w, start_loads

        def ffn3(w):
            start = fence()
            with ExitStack() as sc:
                gates = Gates(sc, E3, 1)
                relu = Ring([Slot(sbuf(sc, "relu", [P, SEQ])) for _ in range(2)])
                tanh = Ring([Slot(sbuf(sc, "tanh", [P, SEQ])) for _ in range(2)])
                gate = sbuf(sc, "gate", [P, TILES])
                hotT = Ring([Slot(sbuf(sc, "hotT", [E3, SEQ])) for _ in range(2)])
                hrows = Ring([Slot(sbuf(sc, "h", [P, 4, DM])) for _ in range(2)])
                for s in relu.slots + tanh.slots + hotT.slots + hrows.slots:
                    s.free = [start]
                ring = Ring(banks)
                S = {}

                def prepare(g):
                    r, th, hot, h = relu.next(), tanh.next(), hotT.next(), hrows.next()
                    S["hot", g] = hot, h
                    ts = tiles_of(g)

                    def hidden():
                        for slot, name, b, fn in ((r, "w1", "b1", ACT.Relu), (th, "wg1", "bg1", ACT.Tanh)):
                            bank = ring.next()
                            m = mm(bank.ap, [(w[name][:, k, :], hT[:, k, rows_of(g)]) for k in range(KC)],
                                   hT_ready[g], w["ready"], bank.free)
                            slot.ready = act(lambda e, slot=slot, b=b, fn=fn, bank=bank: e.activation(
                                slot.ap[:, :], bank.ap, fn, bias=w[b][:, 0:1]), m, slot.free)
                            bank.free = [slot.ready]

                    def scores():
                        b1_, b2_ = ring.next(), ring.next()
                        for i in range(4):
                            m = mm(b1_.ap[:, i * E3:(i + 1) * E3], [(r.ap[:, i * P:(i + 1) * P], w["w2"][:, 0, :])],
                                   r.ready, b1_.free)
                        for i in range(4):
                            m2 = mm(b2_.ap[:, i:i + 1], [(th.ap[:, i * P:(i + 1) * P], w["wg2"][:, 0, :])],
                                    th.ready, b2_.free)
                        r.free, th.free = [m], [m2]
                        v = gates.v[:, ts, :]
                        a = dve(lambda e: e.tensor_tensor(
                            v, b1_.ap[:, 0:4 * E3].rearrange("p (t e) -> p t e", e=E3),
                            w["b2"][:, :].unsqueeze(1).to_broadcast([P, 4, E3]), ALU.add), m)
                        b1_.free = [a]
                        s = act(lambda e: e.activation(gate[:, ts], b2_.ap[:, 0:4], ACT.Sigmoid,
                                                       bias=w["bg2"][:, 0:1]), m2, start)
                        b2_.free = [s]
                        gates.done[g] = dve(lambda e: e.tensor_tensor(v, v, over(gate[:, ts], E3), ALU.mult), a, s)

                    def turn():
                        hot.ready = turn_gates(hot.ap[:, :], gates.hot[0], g, E3, ring, gates.done[g], hot.free)

                    def rows():
                        for i in range(4):
                            h.ready = normed(h.ap[:, i, :], x[:, 4 * g + i, :], 4 * g + i, h.free, x_ready[g])
                    return [hidden, scores, rows] + gates.softmax(g) + gates.largest(g) + [idle, turn]

                def main(g):
                    hot, h = S["hot", g]

                    def step(i):
                        t = 4 * g + i
                        bank = ring.next()
                        m = mm(bank.ap, [(hot.ap[:, i * P:(i + 1) * P],
                                          w["scale_bias"][:, :, :].rearrange("e a d -> e (a d)"))], hot.ready, bank.free)
                        a = dve(lambda e: e.tensor_tensor(h.ap[:, i, :], h.ap[:, i, :], bank.ap[:, 0:DM], ALU.mult),
                                m, h.ready)
                        a2 = dve(lambda e: e.tensor_tensor(x[:, t, :], x[:, t, :], bank.ap[:, DM:2 * DM], ALU.add), m)
                        bank.free = [a2]
                        a = dve(lambda e: e.tensor_tensor(x[:, t, :], x[:, t, :], h.ap[:, i, :], ALU.add), a, a2)
                        x_ready[g] = h.free = [a]
                        hot.free = [m]
                    return [lambda i=i: step(i) for i in range(4)]

                timed = []
                mine = own_layer_norms()
                for g in range(BATCH):
                    if g in mine:
                        timed += spread_over(layer_norm(g, ring), g - 2, g - 1.2)
                    timed += spread_over(prepare(g), g - 1, g + 0.5)
                    timed += spread_over(main(g), g + 0.6, g + 1.3)
                in_time(timed)

        table = {0: (attention_inputs("L0", True), lambda w: attention("L0", True, True, w)),
                 1: (ffn0_inputs, ffn0),
                 2: (autocorrelation_inputs, autocorrelation),
                 3: (ffn1_inputs, ffn1),
                 4: (attention_inputs("L2", False), lambda w: attention("L2", False, False, w)),
                 5: (ffn2_inputs, ffn2),
                 6: (attention_inputs("L3", True), lambda w: attention("L3", True, True, w)),
                 7: (ffn3_inputs, ffn3)}
        for chain in CHAINS:
            phases = [table[n] for n in chain if n in LAYERS]
            scopes = [ExitStack() for _ in phases]
            start = fence()
            placed = [place(scope) for (place, _), scope in zip(phases[::-1], scopes[::-1])][::-1]
            behind = None
            for w, start_loads in placed:
                start_loads(start, behind)
                if not x_ready[0]:
                    load_x()
                behind = w["ready"]
            for (_, run_phase), (w, _), scope in zip(phases, placed, scopes):
                run_phase(w)
                scope.close()
        store = [new_count(f"store{b}") for b in range(BATCH)]
        stored = [load(store[b], out[b].rearrange("(t p) d -> p t d", p=P), x[:, 4 * b:4 * b + 4, :], x_ready[b])
                  for b in range(BATCH)]
        sp(lambda e: e.nop(), stored, signal=False)

        block = top.enter_context(nc.Block())

        @block.tensor
        def _(e):
            pe.run(e)

        @block.vector
        def _(e):
            dve.run(e)

        @block.scalar
        def _(e):
            act.run(e)

        @block.gpsimd
        def _(e):
            pool.run(e)

        @block.sync
        def _(e):
            sp.run(e)


LAYERS = range(8)
CHAINS = ((0,), (1, 2, 3, 4), (5, 6), (7,))


def dft_tables():
    n, half = SEQ, SEQ // 2
    t = np.arange(n)
    f = np.arange(half)
    angle = 2 * np.pi * ((t[:, None] * f[None, :]) % n) / n
    nyquist = np.where(t % 2 == 0, 1.0, -1.0)
    fwd = np.concatenate([np.cos(angle), -np.sin(angle)], 1)
    fwd[:, half] = nyquist
    weight = np.where(f == 0, 1.0, 2.0) / n
    inv = np.concatenate([(np.cos(angle) * weight).T, (-np.sin(angle) * weight).T], 0)
    inv[half] = nyquist / n
    return fwd.astype(np.float32), inv.astype(np.float32)


TRANSPOSED = {"L0_wq": "L0_xattn_wq_w", "L0_wk": "L0_xattn_wk_w", "L0_wv": "L0_xattn_wv_w", "L0_wo": "L0_xattn_dense_w",
              "L2_wq": "L2_xattn_Wq", "L2_wk": "L2_xattn_Wk", "L2_wv": "L2_xattn_Wv", "L2_wo": "L2_xattn_Wo",
              "L3_wq": "L3_xattn_Wq", "L3_wk": "L3_xattn_Wk", "L3_wv": "L3_xattn_Wv", "L3_wo": "L3_xattn_Wo"}
RENAMED = {"L0_bq": "L0_xattn_wq_b", "L0_bk": "L0_xattn_wk_b", "L0_bv": "L0_xattn_wv_b", "L0_bo": "L0_xattn_dense_b",
           "L3_bq": "L3_xattn_bq", "L3_bk": "L3_xattn_bk", "L3_bv": "L3_xattn_bv", "L3_bo": "L3_xattn_bo"}
AS_IS = ["x", "L0_ffn_Wg", "L0_ffn_We", "L0_ffn_be",
         "L1_xattn_Wq", "L1_xattn_bq", "L1_xattn_Wk", "L1_xattn_bk", "L1_xattn_Wv", "L1_xattn_bv", "L1_xattn_Wo",
         "L1_xattn_bo", "L1_ffn_W_router", "L1_ffn_W1", "L1_ffn_b1", "L1_ffn_Wo", "L1_ffn_bo", "L1_ffn_ln_gamma",
         "L1_ffn_ln_beta", "L2_ffn_w_shared_in", "L2_ffn_w_shared_out", "L2_ffn_w1_shared", "L2_ffn_w2",
         "L2_ffn_w_gate", "L2_ffn_gate_bias", "L3_ffn_W1", "L3_ffn_b1", "L3_ffn_W2", "L3_ffn_b2", "L3_ffn_Wg1",
         "L3_ffn_bg1", "L3_ffn_Wg2", "L3_ffn_bg2", "L3_ffn_expert_scales", "L3_ffn_expert_biases"]


def kernel(**inputs):
    import numpy as _np
    import concourse.bacc as _bacc
    from concourse import mybir as _mybir
    from concourse.bass_utils import run_bass_kernel_spmd as _run

    arrays = {name: _np.ascontiguousarray(inputs[name]) for name in AS_IS}
    arrays |= {name: _np.ascontiguousarray(inputs[src]) for name, src in RENAMED.items()}
    arrays |= {name: _np.ascontiguousarray(_np.asarray(inputs[src]).T) for name, src in TRANSPOSED.items()}
    arrays["ctxT"] = _np.ascontiguousarray(_np.asarray(inputs["ctx_1024"]).transpose(2, 0, 1))
    arrays["dft"], arrays["idft"] = dft_tables()

    nc = _bacc.Bacc("TRN2", target_bir_lowering=False, num_devices=1)
    named, I = {}, {}
    for name, a in arrays.items():
        named[f"in_{name}"] = a
        I[name] = nc.dram_tensor(f"in_{name}", a.shape, _mybir.dt.from_np(a.dtype), kind="ExternalInput").ap()
    out = nc.dram_tensor("out_dram", (BATCH, SEQ, DM), F32, kind="ExternalOutput").ap()
    build(nc, I, out)
    r = _run(nc, [named], core_ids=[0])
    return r.results[0]["out_dram"]
```

```python
from contextlib import ExitStack

import numpy as np
import concourse.bass as bass
from concourse import mybir

F32 = mybir.dt.float32
F32R = mybir.dt.float32r
BF16 = mybir.dt.bfloat16
U32 = mybir.dt.uint32
ALU = mybir.AluOpType
ACT = mybir.ActivationFunctionType
AX = mybir.AxisListType

P = 128
BATCH, SEQ, DM = 4, 512, 256
CTX = 1601
HEADS, DH = 16, 16
TOK = BATCH * SEQ
TILES = TOK // P
KC = DM // P
BANK = 512
LN_EPS = 1e-5

GROUP = 4
GROUPS = HEADS // GROUP
KEY_CHUNKS = [(k, min(P, CTX - k)) for k in range(0, CTX, P)]
KEY_BLOCKS = [(k, min(BANK, CTX - k)) for k in range(0, CTX, BANK)]
MAX_SPLIT = 4
MAX_BLOCKS = [(CTX * i // MAX_SPLIT, CTX * (i + 1) // MAX_SPLIT - CTX * i // MAX_SPLIT) for i in range(MAX_SPLIT)]
K_PART = [0, 1, 2, 0, 1, 2, 0]
Q_PART = [0, 0, 0, 1, 1, 1, 2]
PAIR_ROWS = DH * len(K_PART)
MAX_ROWS = 3
STACK = PAIR_ROWS + MAX_ROWS
LEAD = 0.182
LAG = 1
BEHIND = 2
PROBS = 10
VW = DH + 1


class Count:

    def __init__(self, sem):
        self.sem, self.n = sem, 0


def flat(needs):
    for t in needs:
        if isinstance(t, list):
            yield from flat(t)
        elif t is not None:
            yield t


class Queue:

    def __init__(self, engine, done):
        self.engine, self.done, self.items, self.passed = engine, done, [], {}

    def __call__(self, emit, *needs, done=None, by=1, signal=True):
        most = {}
        for count, value in flat(needs):
            most[count] = max(value, most.get(count, 0))
        waits = [(c, v) for c, v in most.items() if self.passed.get(c, 0) < v]
        self.passed.update(waits)
        count = (done or self.done) if signal else None
        if count:
            count.n += by
        self.items.append((waits, emit, count, by))
        return (count, count.n) if count else None

    def run(self, eng):
        for waits, emit, count, by in self.items:
            for c, v in waits:
                eng.wait_ge(c.sem, v)
            ins = emit(eng)
            if count:
                ins.then_inc(count.sem, by)


class Slot:

    def __init__(self, ap, count=None):
        self.ap, self.free, self.count = ap, [], count


class Ring:
    def __init__(self, slots):
        self.slots, self.at = slots, -1

    def next(self):
        self.at += 1
        return self.slots[self.at % len(self.slots)]


class Pair:

    def __init__(self, hi, lo):
        self.hi, self.lo = hi, lo

    def __getitem__(self, at):
        return Pair(self.hi[at], self.lo[at])

    def rearrange(self, *a, **k):
        return Pair(self.hi.rearrange(*a, **k), self.lo.rearrange(*a, **k))


def spread_over(steps, begin, end):
    return [(begin + (i + 0.5) * (end - begin) / len(steps), step) for i, step in enumerate(steps)]


def in_time(timed):
    for _, _, step in sorted((time, n, step) for n, (time, step) in enumerate(timed)):
        step()


def build(nc, I, out):
    with ExitStack() as top:
        sem_n = [0]

        def new_count(name):
            sem_n[0] += 1
            return Count(top.enter_context(nc.semaphore(f"{name}_{sem_n[0]}")))

        pe = Queue("tensor", new_count("pe_done"))
        dve = Queue("vector", new_count("dve_done"))
        act = Queue("scalar", new_count("act_done"))
        pool = Queue("gpsimd", new_count("pool_done"))
        sp = Queue("sync", None)
        compute = [pe, dve, act, pool]
        dma_counts = []

        def dma_count(name):
            c = new_count(name)
            dma_counts.append(c)
            return c

        input_count = new_count

        def load(count, dst, src, *needs):
            return sp(lambda e: e.dma_start(dst, src), *needs, done=count, by=16)

        def fence():
            return [(q.done, q.done.n) for q in compute if q.done.n] + [(c, c.n) for c in dma_counts if c.n]

        def sbuf(scope, name, shape, dt=F32):
            sem_n[0] += 1
            return scope.enter_context(nc.sbuf_tensor(f"{name}_{sem_n[0]}", shape, dt))

        def scratch(name, shape, dt):
            return nc.dram_tensor(name, shape, dt, kind="Internal").ap()

        x = sbuf(top, "x", [P, TILES, DM])
        hT = sbuf(top, "hT", [P, KC, TOK])
        hT_ready = [None] * BATCH
        hT_free = [[] for _ in range(BATCH)]
        x_ready = [[] for _ in range(BATCH)]
        ahead = [False] * BATCH
        hrow = Ring([Slot(sbuf(top, "hrow", [P, DM])) for _ in range(4)])
        half = sbuf(top, "half", [P, 4])
        ident = sbuf(top, "ident", [P, P])
        identb = sbuf(top, "identb", [P, P], BF16)
        sel_den = sbuf(top, "sel_den", [P, GROUP])
        stats = sbuf(top, "stats", [P, TILES, 6])
        meanvar = sbuf(top, "meanvar", [P, TILES, 2])
        veps = sbuf(top, "veps", [P, TILES])
        rstd = sbuf(top, "rstd", [P, TILES])
        ntmp = sbuf(top, "ntmp", [P, TILES])
        psum = top.enter_context(nc.psum_tensor("psum", [P, 8, BANK], F32))
        banks = [Slot(psum[:, i, :]) for i in range(8)]

        def mm(dst, pairs, *needs, tile_position=None):
            for i, (lhsT, rhs) in enumerate(pairs):
                first, last = i == 0, i == len(pairs) - 1

                def emit(e, lhsT=lhsT, rhs=rhs, first=first, last=last):
                    if tile_position is None:
                        return e.matmul(dst, lhsT, rhs, start=first, stop=last)
                    return e.matmul(dst, lhsT, rhs, start=first, stop=last, tile_position=tile_position)

                token = pe(emit, *(needs if first else ()), signal=last)
            return token

        def mm3(dst, items, *needs):
            passes = []
            for a, b in items:
                passes += [(a.hi, b.hi), (a.hi, b.lo), (a.lo, b.hi)]
            return mm(dst, passes, *needs)

        def new_pair(scope, name, shape):
            return Pair(sbuf(scope, name + "_hi", shape, F32R), sbuf(scope, name + "_lo", shape, F32R))

        def split_pair(dst, src, *needs, hi_on=None, lo_on=None):
            hi_on, lo_on = hi_on or act, lo_on or pool
            if hi_on is act:
                hi = act(lambda e: e.activation(dst.hi, src, ACT.Copy), *needs)
            else:
                hi = hi_on(lambda e: e.tensor_copy(dst.hi, src), *needs)
            return [hi, lo_on(lambda e: e.tensor_tensor(dst.lo, src, dst.hi.bitcast(F32), ALU.subtract), hi, *needs)]

        x_in = [new_count(f"x_in{b}") for b in range(BATCH)]

        def idle():
            pass

        def tiles_of(b):
            return slice(4 * b, 4 * b + 4)

        def load_x(b):
            if not x_ready[b]:
                x_ready[b] = [load(x_in[b], x[:, 4 * b:4 * b + 4, :], I["x"][b].rearrange("(t p) d -> p t d", p=P))]

        half_ready = pool(lambda e: e.memset(half[:, :], -0.5))
        zero = pool(lambda e: e.memset(ident[:, :], 0.0))
        ident_ready = pool(lambda e: e.affine_select(out=ident[:, :], in_=ident[:, :], compare_op=ALU.not_equal,
                                                     fill=1.0, base=0, pattern=[[-1, P]], channel_multiplier=1), zero)
        identb_ready = pool(lambda e: e.tensor_copy(identb[:, :], ident[:, :]), ident_ready)
        zero = pool(lambda e: e.memset(sel_den[:, :], 0.0))
        sel_ready = pool(lambda e: e.affine_select(out=sel_den[:, :], in_=sel_den[:, :], compare_op=ALU.not_equal,
                                                   fill=1.0, base=-DH, pattern=[[-32, GROUP]], channel_multiplier=1), zero)

        def rsqrt(ts, eps, stat=(meanvar, veps, rstd, ntmp)):
            mv, v, r, n = stat[0], stat[1][:, ts], stat[2][:, ts], stat[3][:, ts]
            S = {}

            def power(needs):
                a = dve(lambda e: e.tensor_scalar(v, mv[:, ts, 1], eps, None, ALU.add), needs)
                S["power"] = pool(lambda e: e.tensor_tensor(r, v, half[:, :], ALU.pow), a, half_ready)

            def newton():
                a = dve(lambda e: e.tensor_tensor(n, r, r, ALU.mult), S["power"])
                a = dve(lambda e: e.tensor_tensor(n, n, v, ALU.mult), a)
                a = dve(lambda e: e.tensor_scalar(n, n, -0.5, 1.5, ALU.mult, ALU.add), a)
                return dve(lambda e: e.tensor_tensor(r, r, n, ALU.mult), a)
            return power, newton

        def moments(src, t, needs, mv=meanvar):
            a = dve(lambda e: e.bn_stats(stats[:, t, :], src), needs)
            return dve(lambda e: e.bn_aggr(mv[:, t, :], stats[:, t, :]), a)

        def normed(dst, src, t, *needs, stat=(meanvar, rstd)):
            return dve(lambda e: e.tensor_scalar(dst, src, stat[0][:, t, 0:1], stat[1][:, t:t + 1],
                                                 ALU.subtract, ALU.mult), *needs)

        def layer_norm(b, ring):
            S = {"rows": []}
            power, newton = rsqrt(tiles_of(b), LN_EPS)

            def statistics(i):
                for t in range(4 * b + i, 4 * b + i + 2):
                    S["stats"] = moments(x[:, t, :], t, x_ready[b])

            def root():
                S["rstd"] = newton()

            def normalise(i):
                for t in range(4 * b + i, 4 * b + i + 2):
                    h = hrow.next()
                    S["rows"].append((h, normed(h.ap[:, :], x[:, t, :], t, S["rstd"], h.free)))

            def turn(i):
                bank = ring.next()
                for j, (h, ready) in enumerate(S["rows"][i:i + 2]):
                    for c in range(KC):
                        at = (KC * j + c) * P
                        tr = pe(lambda e, h=h, c=c, at=at: e.transpose(
                            bank.ap[:, at:at + P], h.ap[:, c * P:(c + 1) * P], ident[:, :]),
                            ready, ident_ready, bank.free)
                    h.free = [tr]
                src = bank.ap.rearrange("p (t c q) -> p c t q", c=KC, q=P)
                cols = slice((4 * b + i) * P, (4 * b + i + 2) * P)
                dst = hT[:, :, cols].rearrange("p c (t q) -> p c t q", q=P)
                w = act(lambda e: e.activation(dst, src, ACT.Copy), tr, hT_free[b])
                bank.free = [w]
                hT_ready[b] = hT_ready[b] + [w] if i else [w]
                if i:
                    hT_free[b] = []
            return [lambda: statistics(0), lambda: statistics(2), lambda: power(S["stats"]), root,
                    lambda: normalise(0), lambda: normalise(2), idle, lambda: turn(0), lambda: turn(2)]

        def own_layer_norms():
            mine = [b for b in range(BATCH) if not ahead[b]]
            ahead[:] = [False] * BATCH
            return mine

        def next_layer_norm(b, ring):
            ahead[b] = True
            return layer_norm(b, ring)

        def fill_weight(count, w, src, *needs):
            return load(count, w[:, :, :], src.rearrange("(k p) n -> p k n", p=P), *needs)

        def fill_columns(count, w, src, *needs):
            return sp(lambda e: e.dma_start(w[:, :], src.rearrange("(k p) -> p k", p=P),
                                            allow_slow_non_contiguous=True), *needs, done=count, by=16)

        def fill_rows(count, w, src, *needs):
            return load(count, w[:, :], src.rearrange("(a n) -> a n", a=1).partition_broadcast(P), *needs)

        k_parts_dram = scratch("k_parts_dram", [2, HEADS, 3 * DH, CTX], BF16)
        q_parts_dram = scratch("q_parts_dram", [2, HEADS, PAIR_ROWS, SEQ], BF16)

        def load_context(ctxT, b, *needs):
            src = I["ctxT"][:, b, :].rearrange("(k p) s -> p k s", p=P)
            return [load(count, ctxT.ap[:, :, k0:k0 + kn], src[:, :, k0:k0 + kn], *needs)
                    for count, (k0, kn) in zip(ctxT.count, KEY_BLOCKS)]

        def attention_inputs(tag, biased):
            def place(sc):
                w = {name: sbuf(sc, name, [P, KC, DM]) for name in ("wk", "wq", "wv")}
                w["wo"] = sbuf(sc, "wo", [P, GROUPS, DM])
                w["ctxT"] = Slot(sbuf(sc, "ctxT", [P, KC, CTX]), [input_count(f"{tag}_ctx") for _ in KEY_BLOCKS])
                if biased:
                    w["bk"], w["bq"] = sbuf(sc, "bk", [P, KC]), sbuf(sc, "bq", [P, KC])
                    w["bv"], w["bo"] = sbuf(sc, "bv", [P, DM]), sbuf(sc, "bo", [P, DM])

                def start_loads(start, behind):
                    WK, W = input_count(f"{tag}_key_weights"), input_count(f"{tag}_weights")
                    first = not x_ready[0]
                    if first:
                        load_x(0)
                    w["wk_ready"] = fill_weight(WK, w["wk"], I[f"{tag}_wk"], start, behind)
                    if biased:
                        w["wk_ready"] = fill_columns(WK, w["bk"], I[f"{tag}_bk"], start, behind)
                    w["ctx_ready"] = load_context(w["ctxT"], 0, start, behind)
                    fill_weight(W, w["wq"], I[f"{tag}_wq"], start, behind)
                    if first:
                        for b in range(1, BATCH):
                            load_x(b)
                    fill_weight(W, w["wv"], I[f"{tag}_wv"], start, behind)
                    w["wo_zero"] = pool(lambda e: e.memset(w["wo"][:, :, :], 0.0), start)
                    if biased:
                        fill_columns(W, w["bq"], I[f"{tag}_bq"], start, behind)
                        fill_rows(W, w["bv"], I[f"{tag}_bv"], start, behind)
                        fill_rows(W, w["bo"], I[f"{tag}_bo"], start, behind)
                    wo_src = I[f"{tag}_wo"].rearrange("(g j d) n -> j d g n", g=GROUPS, j=GROUP)
                    for j in range(GROUP):
                        w["ready"] = load(W, w["wo"][32 * j:32 * j + DH, :, :], wo_src[j], w["wo_zero"])
                return w, start_loads
            return place

        def attention(tag, softmax, biased, w):
            start = fence()
            mine = own_layer_norms()
            with ExitStack() as sc:
                wk, wq, wv, wo, ctxT = w["wk"], w["wq"], w["wv"], w["wo"], w["ctxT"]
                wk_ready, w_ready, wo_zero = w["wk_ready"], w["ready"], w["wo_zero"]
                if biased:
                    bk, bq, bv, bo = w["bk"], w["bq"], w["bv"], w["bo"]
                S = {"ctx": w["ctx_ready"]}

                def load_ctx(b):
                    def step():
                        S["ctx"] = load_context(ctxT, b, ctxT.free)
                        ctxT.free = []
                    return [step]

                wide = 1 if softmax else 2
                kp = [Slot(sbuf(sc, "kp", [P, 3, CTX], BF16)) for _ in range(KC)]
                kp_stores = [dma_count(f"{tag}_kp{c}") for c in range(KC)]
                qp = [Slot(sbuf(sc, "qp", [P, 3, SEQ], BF16)) for _ in range(KC)]
                qp_stores = [dma_count(f"{tag}_qp{c}") for c in range(KC)]
                rest = Ring([Slot(sbuf(sc, "rest", [P, BANK])) for _ in range(2)])
                vt = Ring([Slot(sbuf(sc, "vt", [P, len(KEY_CHUNKS), HEADS, VW])) for _ in range(2)])
                kst = [Slot(sbuf(sc, "kst", [P, GROUP, CTX], BF16), dma_count(f"{tag}_kst{i}")) for i in range(3)]
                qst = [Slot(sbuf(sc, "qst", [P, GROUP, SEQ], BF16), dma_count(f"{tag}_qst{i}")) for i in range(3)]
                probs = Ring([Slot(sbuf(sc, "probs", [P, wide, BANK])) for _ in range(PROBS // wide)])
                accs = Slot(sbuf(sc, "accs", [P, BANK]))
                rsmall = sbuf(sc, "rsmall", [P, 4 * GROUP])
                rden = Slot(sbuf(sc, "rden", [P, 4 * GROUP, 32]))
                ctxn = Slot(sbuf(sc, "ctxn", [P, GROUPS, SEQ]))
                mpart = Slot(sbuf(sc, "mpart", [P, 4 * GROUP, MAX_SPLIT]))
                mrow = sbuf(sc, "mrow", [P, 4 * GROUP])
                mrest = sbuf(sc, "mrest", [P, 4 * GROUP])
                mpb = sbuf(sc, "mpb", [P, MAX_ROWS, 4 * GROUP], BF16)
                mT = Slot(sbuf(sc, "mT", [MAX_ROWS * 4 * GROUP, P], BF16), dma_count(f"{tag}_mT"))

                for s in kp + qp + rest.slots + probs.slots + [accs, rden, ctxn, mpart, mT]:
                    s.free = [start]

                s_slots = Ring([banks[i:i + wide] for i in ((0, 1, 2) if softmax else (0, 2, 4))])
                acc = banks[3 if softmax else 6]
                m_banks = Ring(banks[4:7])
                misc = Ring(banks[7:8])
                prelude = Ring([banks[i] for i in ((4, 5, 6, 7) if softmax else (3, 4, 5, 7))])
                turn_banks = Ring(banks[0:3])

                S["ones"] = wo_zero

                def fill_ones(slot, part):
                    def step():
                        S["ones"] = pool(lambda e: e.memset(part, 1.0), start, S["ones"])
                        slot.free = [S["ones"]]
                    return step

                if softmax:
                    fill_ones(kst[0], kst[0].ap[:, :, :])()
                for s in vt.slots:
                    fill_ones(s, s.ap[:, :, :, DH:VW])()
                ones_later = [fill_ones(s, s.ap[:, :, :]) for s in kst[1:]] if softmax else []

                def add_output_bias(b):
                    if biased:
                        bo_rows = bo[:, :].unsqueeze(1).to_broadcast([P, 4, DM])
                        ts = tiles_of(b)
                        x_ready[b] = [pool(lambda e: e.tensor_tensor(x[:, ts, :], x[:, ts, :], bo_rows, ALU.add),
                                           hT_ready[b], w_ready, S["ones"], x_ready[b])]
                    S["x_biased", b] = x_ready[b]

                acc.free = [dve(lambda e: e.memset(acc.ap, 0.0), acc.free, start)]


                def split(dst, part_slot, bank, n, bias, bias_ready, mmt):
                    r = rest.next()
                    v = r.ap[:, 0:n]
                    src = bank.ap[:, 0:n]
                    if bias is None:
                        hi = act(lambda e: e.activation(dst(0), src, ACT.Copy), mmt, part_slot.free)
                        r1 = dve(lambda e: e.tensor_tensor(v, src, dst(0), ALU.subtract), hi, r.free)
                    else:
                        hi = act(lambda e: e.activation(dst(0), src, ACT.Identity, bias=bias), mmt,
                                 bias_ready, part_slot.free)
                        r1 = dve(lambda e: e.scalar_tensor_tensor(out=v, in0=src, scalar=bias, in1=dst(0),
                                                                  op0=ALU.add, op1=ALU.subtract), hi, r.free)
                    bank.free = [r1]
                    mid = act(lambda e: e.activation(dst(1), v, ACT.Copy), r1)
                    lo = pool(lambda e: e.tensor_tensor(dst(2), v, dst(1), ALU.subtract), mid)
                    r.free = [lo]
                    return [mid, lo]

                def make_keys(b, c, misc=misc):
                    steps = []
                    for block, (k0, kn) in enumerate(KEY_BLOCKS):
                        def step(block=block, k0=k0, kn=kn):
                            bank = misc.next()
                            t = mm(bank.ap[:, 0:kn], [(wk[:, k, c * P:(c + 1) * P], ctxT.ap[:, k, k0:k0 + kn])
                                                      for k in range(KC)], S["ctx"][block], wk_ready, bank.free)
                            ctxT.free.append(t)
                            S.setdefault(("kp", b, c), []).append(split(
                                lambda part: kp[c].ap[:, part, k0:k0 + kn], kp[c], bank, kn,
                                bk[:, c:c + 1] if biased else None, wk_ready, t))
                        steps.append(step)

                    def store():
                        dst = k_parts_dram[b % 2, 8 * c:8 * c + 8].rearrange("h (d a) t -> (h d) a t", a=3)
                        last = load(kp_stores[c], dst, kp[c].ap[:, :, :],
                                    S[("kp", b, c)], S.get(("kst_read", b - 2)))
                        S["k_stored", b, c] = last
                        kp[c].free = [last]
                    return steps + [store]

                def make_queries(b, misc=misc):
                    steps = []
                    for c in range(KC):
                        def step(c=c):
                            bank = misc.next()
                            t = mm(bank.ap, [(wq[:, k, c * P:(c + 1) * P], hT[:, k, b * SEQ:(b + 1) * SEQ])
                                             for k in range(KC)], hT_ready[b], w_ready, bank.free)
                            S["qp", b, c] = split(lambda part: qp[c].ap[:, part, :], qp[c], bank, SEQ,
                                                  bq[:, c:c + 1] if biased else None, w_ready, t)
                            hT_free[b].append(t)
                        steps.append(step)

                        def store(c=c):
                            for j, part in enumerate(Q_PART):
                                first, step_ = divmod(j, 3)
                                rows = slice(3 * DH * first + step_, min(3 * DH * (first + 1), PAIR_ROWS),
                                             3 if first < 2 else 1)
                                last = load(qp_stores[c], q_parts_dram[b % 2, 8 * c:8 * c + 8, rows, :],
                                            qp[c].ap[:, part, :], S["qp", b, c], S.get(("kst_read", b - 2)))
                            S["q_stored", b, c] = last
                            qp[c].free = [last]
                        steps.append(store)
                    return steps

                def make_values(b, misc=misc):
                    slot = vt.slots[b % 2]
                    steps = []
                    for i in range(0, len(KEY_CHUNKS), 2):
                        def step(i=i):
                            bank = misc.next()
                            chunks = KEY_CHUNKS[i:i + 2]
                            for j, (k0, kn) in enumerate(chunks):
                                t = mm(bank.ap[0:kn, j * DM:(j + 1) * DM],
                                       [(ctxT.ap[:, k, k0:k0 + kn], wv[:, k, :]) for k in range(KC)],
                                       S["ctx"], w_ready, bank.free)
                            n = len(chunks)
                            dst = slot.ap[0:kn, i:i + n, :, 0:DH]
                            src = bank.ap[0:kn, 0:n * DM].rearrange("p (c h d) -> p c h d", c=n, d=DH)
                            if biased:
                                rows = bv[0:kn, :].rearrange("p (h d) -> p h d", d=DH).unsqueeze(1)
                                rows = rows.to_broadcast([kn, n, HEADS, DH])
                                e = dve(lambda e: e.tensor_tensor(dst, src, rows, ALU.add), t, slot.free, w_ready)
                            else:
                                e = dve(lambda e: e.tensor_copy(dst, src), t, slot.free)
                            ctxT.free.append(t)
                            bank.free = [e]
                            S["v", b] = [e, slot.free]
                        steps.append(step)
                    return steps

                def load_unit(u):
                    b, g = divmod(u, GROUPS)

                    def step():
                        ks, qs = kst[u % 3], qst[u % 3]
                        stored = [S["k_stored", b, 4 * g // 8], S["q_stored", b, 4 * g // 8]]
                        src = k_parts_dram[b % 2, 4 * g:4 * g + 4, :, :].rearrange("h r t -> r h t")
                        load(ks.count, ks.ap[0:48, :, :], src, stored, ks.free)
                        load(ks.count, ks.ap[48:96, :, :], src, stored, ks.free)
                        t = load(ks.count, ks.ap[96:PAIR_ROWS, :, :], src[0:3 * DH:3], stored, ks.free)
                        q = load(qs.count, qs.ap[0:PAIR_ROWS, :, :],
                                 q_parts_dram[b % 2, 4 * g:4 * g + 4, :, :].rearrange("h r t -> r h t"),
                                 stored, qs.free)
                        S["unit", u] = [t, q, list(ks.free)]
                        if g == GROUPS - 1:
                            S["kst_read", b] = [t, q]
                    return [step]

                def maxima(u):
                    ks, qs = kst[u % 3], qst[u % 3]
                    steps = []
                    for h in range(GROUP):
                        for qt in range(SEQ // P):
                            row = h * (SEQ // P) + qt
                            for i, (k0, kn) in enumerate(MAX_BLOCKS):
                                def step(h=h, qt=qt, row=row, i=i, k0=k0, kn=kn):
                                    bank = m_banks.next()
                                    t = mm(bank.ap[:, 0:kn], [(qs.ap[0:PAIR_ROWS, h, qt * P:(qt + 1) * P],
                                                               ks.ap[0:PAIR_ROWS, h, k0:k0 + kn])],
                                           S["unit", u], bank.free)
                                    r = dve(lambda e: e.tensor_reduce(mpart.ap[:, row, i:i + 1], bank.ap[:, 0:kn],
                                                                      AX.X, ALU.max), t, mpart.free)
                                    bank.free = [r]
                                    S["max", u] = r
                                steps.append(step)

                    def close():
                        t = dve(lambda e: e.tensor_reduce(mrow[:, :], mpart.ap[:, :, :], AX.X, ALU.max), S["max", u])
                        mpart.free = [t]
                        a = dve(lambda e: e.tensor_scalar(mpb[:, 0, :], mrow[:, :], -1.0, None, ALU.mult), t,
                                S.get("mpb_free"))
                        a = dve(lambda e: e.scalar_tensor_tensor(out=mrest[:, :], in0=mrow[:, :], scalar=-1.0,
                                                                 in1=mpb[:, 0, :], op0=ALU.mult, op1=ALU.subtract), a)
                        a = dve(lambda e: e.tensor_copy(mpb[:, 1, :], mrest[:, :]), a)
                        a = dve(lambda e: e.tensor_tensor(mpb[:, 2, :], mrest[:, :], mpb[:, 1, :], ALU.subtract), a)
                        S["mparts", u] = a

                    def turn():
                        bank = misc.next()
                        rows = MAX_ROWS * 4 * GROUP
                        view = bank.ap.bitcast(BF16)[0:rows, 0:P]
                        t = pe(lambda e: e.transpose(view, mpb[:, :, :].rearrange("p a b -> p (a b)"), identb[:, :]),
                               S["mparts", u], identb_ready, bank.free)
                        S["mpb_free"] = t
                        c = act(lambda e: e.activation(mT.ap[:, :], view, ACT.Copy), t, mT.free)
                        bank.free = [c]
                        for i in range(MAX_ROWS):
                            d = load(mT.count, qs.ap[PAIR_ROWS + i:PAIR_ROWS + i + 1, :, :]
                                     .rearrange("p h (a q) -> p (h a) q", q=P),
                                     mT.ap[i * 4 * GROUP:(i + 1) * 4 * GROUP, :], c, qs.free, S["unit", u])
                        mT.free = [d]
                        S["maxrows", u] = d
                    return steps + [close, turn]

                def finish(u):
                    b, g = divmod(u, GROUPS)

                    def evacuate():
                        if softmax:
                            t = act(lambda e: e.activation(accs.ap[:, :], acc.ap, ACT.Copy), S["acc", u], accs.free)
                        else:
                            t = dve(lambda e: e.tensor_copy(ctxn.ap[:, g, :], acc.ap), S["acc", u], ctxn.free)
                            S["ctxn", b] = t
                        acc.free = [t]
                        S["accs", u] = t

                    def denominators():
                        bank = misc.next()
                        for qt in range(SEQ // P):
                            t = mm(bank.ap[:, qt * GROUP:(qt + 1) * GROUP],
                                   [(accs.ap[:, qt * P:(qt + 1) * P], sel_den[:, :])], S["accs", u], sel_ready, bank.free)
                        r = dve(lambda e: e.reciprocal(rsmall[:, :], bank.ap[:, 0:4 * GROUP]), t, rden.free)
                        bank.free = [r]
                        r = pool(lambda e: e.tensor_copy(
                            rden.ap[:, :, :], rsmall[:, :].unsqueeze(2).to_broadcast([P, 4 * GROUP, 32])), r)
                        S["rden", u] = r

                    def divide():
                        bank = misc.next()
                        for qt in range(SEQ // P):
                            spread = rden.ap[:, qt * GROUP:(qt + 1) * GROUP, :].rearrange("p j r -> p (j r)")
                            t = mm(bank.ap[:, qt * P:(qt + 1) * P], [(spread, ident[:, :])],
                                   S["rden", u], bank.free)
                        r = dve(lambda e: e.tensor_tensor(ctxn.ap[:, g, :], accs.ap[:, :], bank.ap, ALU.mult),
                                t, ctxn.free)
                        rden.free, accs.free, bank.free = [t], [r], [r]
                        S["ctxn", b] = r
                    return [evacuate], ([denominators, divide] if softmax else [])

                def project(b):
                    steps = []
                    for t0 in range(0, SEQ // P, 2):
                        def step(t0=t0):
                            bank = misc.next()
                            for j in range(2):
                                q0 = (t0 + j) * P
                                t = mm(bank.ap[:, j * DM:(j + 1) * DM],
                                       [(ctxn.ap[:, g, q0:q0 + P], wo[:, g, :]) for g in range(GROUPS)],
                                       S["ctxn", b], w_ready, bank.free)
                            rows = x[:, 4 * b + t0:4 * b + t0 + 2, :].rearrange("p t d -> p (t d)")
                            a = dve(lambda e: e.tensor_tensor(rows, rows, bank.ap, ALU.add), t, S["x_biased", b])
                            bank.free = [a]
                            x_ready[b] = [a] if t0 == 0 else x_ready[b] + [a]
                            ctxn.free = [t]
                        steps.append(step)
                    return steps

                def attend(u):
                    b, g = divmod(u, GROUPS)
                    ks, qs = kst[u % 3], qst[u % 3]
                    rows = STACK if softmax else PAIR_ROWS
                    steps = []
                    made = {}

                    def scores(kc, h0):
                        k0, kn = KEY_CHUNKS[kc]
                        slots, p = s_slots.next(), probs.next()
                        for h, slot in enumerate(slots, h0):
                            t = mm(slot.ap[0:kn, :], [(ks.ap[0:rows, h, k0:k0 + kn], qs.ap[0:rows, h, :])],
                                   S["unit", u], S.get(("maxrows", u)), slot.free)
                        at = banks.index(slots[0])
                        src = psum[0:kn, at:at + wide, :]
                        a = act(lambda e: e.activation(p.ap[0:kn, :, :], src, ACT.Exp if softmax else ACT.Sigmoid,
                                                       scale=DH ** -0.5), t, p.free)
                        for slot in slots:
                            slot.free = [a]
                        p.free = []
                        made[kc, h0] = (p, a)
                        if kc == len(KEY_CHUNKS) - 1 and h0 + wide == GROUP:
                            ks.free, qs.free = [t], [t]

                    def values(kc):
                        k0, kn = KEY_CHUNKS[kc]
                        all_made = [made[kc, h][1] for h in range(0, GROUP, wide)]
                        for h in range(GROUP):
                            p, _ = made[kc, h - h % wide]
                            lhsT = vt.slots[b % 2].ap[0:kn, kc, GROUP * g + h, :]
                            dst, rhs = acc.ap[32 * h:32 * h + VW, :], p.ap[0:kn, h % wide, :]
                            t = pe(lambda e, dst=dst, lhsT=lhsT, rhs=rhs, h=h: e.matmul(
                                dst, lhsT, rhs, start=kc == 0, stop=kc == len(KEY_CHUNKS) - 1,
                                tile_position=(0, 32 * h)), all_made, S["v", b], acc.free)
                            p.free = [t]
                        S["acc", u] = t
                        if g == GROUPS - 1:
                            vt.slots[b % 2].free = [t]

                    for kc in range(len(KEY_CHUNKS)):
                        for h in range(0, GROUP, wide):
                            steps.append(lambda kc=kc, h=h: scores(kc, h))
                            if kc >= LAG and h == BEHIND:
                                steps.append(lambda kc=kc: values(kc - LAG))
                    for kc in range(len(KEY_CHUNKS) - LAG, len(KEY_CHUNKS)):
                        steps.append(lambda kc=kc: values(kc))
                    return steps

                UNITS = BATCH * GROUPS
                timed = spread_over(make_keys(0, 0, prelude), -3.5, -2.5)
                if 0 in mine:
                    timed += spread_over(layer_norm(0, turn_banks), -3.4, -2.6)
                for b in mine:
                    if b:
                        timed += spread_over(layer_norm(b, misc), 1.1 * b - 2.2, 1.1 * b - 1.2)
                timed += spread_over(make_queries(0, prelude), -2.4, -2.2)
                timed += spread_over(load_unit(0), -2.1, -2.1)
                timed += spread_over(make_keys(0, 1, prelude), -2, -1.6)
                timed += spread_over(make_values(0, Ring(misc.slots + (banks[0:3] if softmax else banks[3:4]))), -1.5, -0.3)
                timed += list(zip((-1.45, -1.1), ones_later))
                timed += spread_over(load_unit(1), -1.2, -1.2)
                timed += spread_over(load_ctx(1), -0.25, -0.25)
                for b in range(BATCH):
                    first = b * GROUPS
                    if b + 1 < BATCH:
                        timed += spread_over(make_queries(b + 1), first + 0.28, first + 0.63)
                        timed += spread_over(make_keys(b + 1, 0), first + 0.7, first + 1.75)
                        timed += spread_over(make_keys(b + 1, 1), first + 1.8, first + 2.5)
                        timed += spread_over(make_values(b + 1), first + 2.5, first + 3.85)
                    if b + 2 < BATCH:
                        timed += spread_over(load_ctx(b + 2), first + 3.87, first + 3.87)
                    timed.append((first + 0.6, lambda b=b: add_output_bias(b)))
                    timed += spread_over(project(b), first + GROUPS + 0.37, first + GROUPS + 0.81)
                    if b + 1 < BATCH:
                        timed += spread_over(next_layer_norm(b, misc), first + GROUPS + 1.39, first + GROUPS + 3.27)
                for u in range(UNITS):
                    timed += spread_over(attend(u), u, u + 1)
                    evacuate, divide = finish(u)
                    timed += spread_over(evacuate, u + 1, u + 1)
                    timed += spread_over(divide, u + 1.06, u + 1.41) if divide else []
                    if softmax:
                        timed += spread_over(maxima(u), u - 1 - LEAD if u else -1.2, u - LEAD)
                    if u + 2 < UNITS:
                        timed += spread_over(load_unit(u + 2), u + 0.02, u + 0.02)
                in_time(timed)
        def iota_rows(sc, n, start):
            t32 = sbuf(sc, "iota_i", [P, n], mybir.dt.int32)
            t = sbuf(sc, "iota", [P, n])
            a = pool(lambda e: e.iota(t32[:, :], pattern=[[1, n]], base=0, channel_multiplier=0), start)
            return t, pool(lambda e: e.tensor_copy(t[:, :], t32[:, :]), a)

        def rows_of(g):
            return slice(g * SEQ, (g + 1) * SEQ)

        def over(ap2, n):
            return ap2.unsqueeze(2).to_broadcast([P, 4, n])

        class Gates:

            def __init__(self, sc, n, top):
                self.n, self.iota = n, iota_rows(sc, n, fence())
                self.v = sbuf(sc, "gate_v", [P, TILES, n])
                self.m = sbuf(sc, "gate_m", [P, TILES])
                self.top8 = sbuf(sc, "gate_top8", [P, TILES, 8])
                self.idx = sbuf(sc, "gate_idx", [P, TILES, 8], U32)
                self.idxf = sbuf(sc, "gate_idxf", [P, TILES, 8])
                self.hot = [sbuf(sc, "gate_hot", [P, TILES, n]) for _ in range(top)]
                self.done = [None] * BATCH

            def softmax(self, g):
                ts = tiles_of(g)
                v, m = self.v[:, ts, :], self.m[:, ts]

                def exponentials():
                    a = dve(lambda e: e.tensor_reduce(m, v, AX.X, ALU.max), self.done[g])
                    a = dve(lambda e: e.tensor_tensor(v, v, over(m, self.n), ALU.subtract), a)
                    self.done[g] = act(lambda e: e.activation(v, v, ACT.Exp), a)

                def divide():
                    a = dve(lambda e: e.tensor_reduce(m, v, AX.X, ALU.add), self.done[g])
                    a = dve(lambda e: e.reciprocal(m, m), a)
                    self.done[g] = dve(lambda e: e.tensor_tensor(v, v, over(m, self.n), ALU.mult), a)
                return [exponentials, idle, divide]

            def largest(self, g):
                ts = tiles_of(g)

                def values():
                    for t in range(4 * g, 4 * g + 4):
                        a = dve(lambda e, t=t: e.max(self.top8[:, t, :], self.v[:, t, :]), self.done[g])
                    self.done[g] = a

                def places():
                    for t in range(4 * g, 4 * g + 4):
                        a = dve(lambda e, t=t: e.max_index(self.idx[:, t, :], self.top8[:, t, :], self.v[:, t, :]),
                                self.done[g])
                    self.done[g] = dve(lambda e: e.tensor_copy(self.idxf[:, ts, :], self.idx[:, ts, :]), a)

                def onehots():
                    iota, iota_ready = self.iota
                    for i, o in enumerate(self.hot):
                        a = dve(lambda e, o=o, i=i: e.tensor_tensor(
                            o[:, ts, :], iota[:, :].unsqueeze(1).to_broadcast([P, 4, self.n]),
                            over(self.idxf[:, ts, i], self.n), ALU.is_equal), self.done[g], iota_ready)
                    self.done[g] = a
                return [values, places, onehots]

            def weigh(self, g, weight):
                ts = tiles_of(g)
                for i, o in enumerate(self.hot):
                    a = dve(lambda e, o=o, i=i: e.tensor_tensor(o[:, ts, :], o[:, ts, :], over(weight(i), self.n),
                                                                ALU.mult), self.done[g])
                self.done[g] = dve(lambda e: e.tensor_tensor(self.v[:, ts, :], self.hot[0][:, ts, :],
                                                             self.hot[1][:, ts, :], ALU.add), a)

        def turn_gates(dst, src, g, n_rows, ring, needs, dst_free=None):
            bank = ring.next()
            for i in range(4):
                t = pe(lambda e, i=i: e.transpose(bank.ap[0:n_rows, i * P:(i + 1) * P], src[:, 4 * g + i, :],
                                                  ident[:, :]), needs, bank.free)
            c = act(lambda e: e.activation(dst, bank.ap[0:n_rows, :], ACT.Copy), t, dst_free)
            bank.free = [c]
            return c

        def by_batch(prepare, main, ring, before):
            mine = own_layer_norms()
            timed = [(-0.14, before)]
            for g in range(BATCH):
                at = g - 1 if g else -1
                ready = (layer_norm(g, ring) if g in mine else []) + prepare(g)
                timed += spread_over(ready, at + 0.1, at + 0.85)
                timed += spread_over(main(g), g, g + 1)
                if g + 1 < BATCH:
                    timed += spread_over(next_layer_norm(g, ring), g + 1.1, g + 1.9)
            in_time(timed)

        def place_vectors(sc, **columns):
            return {name: sbuf(sc, name, [P, n]) for name, n in columns.items()}

        def split_rows(ring, g):
            slot = ring.next()

            def step():
                slot.ready = split_pair(slot.ap[:, :, :], hT[:, :, rows_of(g)], hT_ready[g], slot.free)
                hT_free[g] = hT_free[g] + slot.ready
            return slot, step

        def pair_ring(scope, name, shape, n, start):
            ring = Ring([Slot(new_pair(scope, name, shape)) for _ in range(n)])
            for s in ring.slots:
                s.free = [start]
            return ring

        E0 = 8

        def ffn0_inputs(sc):
            w = {"we": sbuf(sc, "we", [P, KC, E0, DM]), "be": sbuf(sc, "be", [E0, DM]), "wg": sbuf(sc, "wg", [P, KC, E0])}

            def start_loads(start, behind):
                G, W = input_count("ffn0_gate"), input_count("ffn0_w")
                w["gate_ready"] = fill_weight(G, w["wg"], I["L0_ffn_Wg"], start, behind)
                load(W, w["be"][:, :], I["L0_ffn_be"], start, behind)
                for k in range(KC):
                    w["ready"] = load(W, w["we"][:, k, :, :],
                                      I["L0_ffn_We"][:, k * P:(k + 1) * P, :].rearrange("e p n -> p e n"), start, behind)
            return w, start_loads

        def ffn0(w):
            start = fence()
            with ExitStack() as sc:
                gates = Gates(sc, E0, 2)
                dT = sbuf(sc, "dT", [E0, TOK])
                dT_ready = {}
                ring = Ring(banks)
                hpair = pair_ring(sc, "hpair", [P, KC, SEQ], 2, start)
                hp = {}
                we = new_pair(sc, "we_pair", [P, KC, E0, DM])
                we_ready = [[] for _ in range(E0 // 2)]

                def split_weights():
                    for e2 in range(E0 // 2):
                        es = slice(2 * e2, 2 * e2 + 2)
                        for k in range(KC):
                            we_ready[e2] += split_pair(we[:, k, es, :], w["we"][:, k, es, :], w["ready"], start,
                                                       lo_on=dve if k else pool)

                def prepare(g):
                    ts = tiles_of(g)
                    hp[g], split = split_rows(hpair, g)

                    def logits():
                        token_logits(gates, g, w["wg"], w["gate_ready"], ring)

                    def shares():
                        top, m = gates.top8[:, ts, :], gates.m[:, ts]
                        a = dve(lambda e: e.tensor_tensor(m, top[:, :, 0], top[:, :, 1], ALU.add), gates.done[g])
                        a = dve(lambda e: e.reciprocal(m, m), a)
                        gates.done[g] = dve(lambda e: e.tensor_tensor(top[:, :, 0:2], top[:, :, 0:2], over(m, 2),
                                                                      ALU.mult), a)

                    def turn():
                        dT_ready[g] = turn_gates(dT[:, rows_of(g)], gates.v, g, E0, ring, gates.done[g])
                    return [logits, split] + gates.softmax(g) + gates.largest(g) + [
                        shares, lambda: gates.weigh(g, lambda i: gates.top8[:, ts, i]), idle, turn]

                def main(g):
                    steps = []
                    for t in range(4 * g, 4 * g + 4):
                        cols = slice(t * P, (t + 1) * P)
                        for e2 in range(E0 // 2):
                            def step(t=t, e2=e2, local=slice(t % 4 * P, (t % 4 + 1) * P)):
                                bank = ring.next()
                                m = mm3(bank.ap, [(hp[g].ap[:, k, local], we[:, k, 2 * e2:2 * e2 + 2, :]
                                                   .rearrange("p e n -> p (e n)")) for k in range(KC)],
                                        hp[g].ready, we_ready[e2], bank.free)
                                hp[g].free = [m]
                                for i in range(2):
                                    a = dve(lambda e, i=i: e.scalar_tensor_tensor(
                                        out=x[:, t, :], in0=bank.ap[:, i * DM:(i + 1) * DM],
                                        scalar=gates.v[:, t, 2 * e2 + i:2 * e2 + i + 1],
                                        in1=x[:, t, :], op0=ALU.mult, op1=ALU.add), m, gates.done[g], x_ready[g])
                                    x_ready[g] = [a]
                                bank.free = [a]
                            steps.append(step)

                        def biases(t=t, cols=cols):
                            bank = ring.next()
                            m = mm(bank.ap[:, 0:DM], [(dT[:, cols], w["be"][:, :])], dT_ready[g], w["ready"], bank.free)
                            a = dve(lambda e: e.tensor_tensor(x[:, t, :], x[:, t, :], bank.ap[:, 0:DM], ALU.add),
                                    m, x_ready[g])
                            x_ready[g] = bank.free = [a]
                        steps.append(biases)
                    return steps
                by_batch(prepare, main, ring, split_weights)

        def token_logits(gates, g, w, w_ready, ring, after=lambda dst, src, m: dve(
                lambda e: e.tensor_copy(dst, src), m)):
            n = w.shape[2]
            bank = ring.next()
            for i in range(4):
                t = 4 * g + i
                m = mm(bank.ap[:, i * n:(i + 1) * n], [(hT[:, k, t * P:(t + 1) * P], w[:, k, :]) for k in range(KC)],
                       hT_ready[g], w_ready, bank.free)
            hT_free[g] = hT_free[g] + [m]
            src = bank.ap[:, 0:4 * n].rearrange("p (t e) -> p t e", e=n)
            gates.done[g] = after(gates.v[:, tiles_of(g), 0:n], src, m)
            bank.free = [gates.done[g]]

        FC = SEQ // P

        def autocorrelation_inputs(sc):
            w = {name: sbuf(sc, name, [P, KC, DM]) for name in ("wq", "wk", "wv", "wo")}
            w |= place_vectors(sc, bq=DM, bk=DM, bv=DM, bo=DM)
            w |= {name: sbuf(sc, name, [P, FC, SEQ]) for name in ("fwd", "inv")}

            def start_loads(start, behind):
                W = input_count("l1x_w")
                for name in ("wq", "wk", "wv", "wo"):
                    fill_weight(W, w[name], I["L1_xattn_W" + name[1]], start, behind)
                for name in ("bq", "bk", "bv", "bo"):
                    fill_rows(W, w[name], I["L1_xattn_" + name], start, behind)
                fill_weight(W, w["fwd"], I["dft"], start, behind)
                w["ready"] = fill_weight(W, w["inv"], I["idft"], start, behind)
            return w, start_loads

        def autocorrelation(w):
            TOP = 6
            NB = BATCH * HEADS
            start = fence()
            mine = own_layer_norms()
            w_ready, fwd, inv = w["ready"], w["fwd"], w["inv"]
            with ExitStack() as sc:
                ctx = [Slot(sbuf(sc, "ctx", [P, KC, SEQ]), dma_count(f"l1x_ctx{i}")) for i in range(BATCH)]
                ctx_ready = [load(ctx[b].count, ctx[b].ap[:, :, :],
                                  I["ctxT"][:, b, 0:SEQ].rearrange("(k p) s -> p k s", p=P), start)
                             for b in range(BATCH)]
                iota, iota_ready = iota_rows(sc, SEQ, start)
                time_ = Ring([Slot(sbuf(sc, "time", [P, FC, DM])) for _ in range(2)])
                freq = Ring([Slot(sbuf(sc, "freq", [P, FC, DM])) for _ in range(2)])
                vf = [sbuf(sc, "vf", [P, FC, DM]) for _ in range(BATCH)]
                prod = Ring([Slot(sbuf(sc, "prod", [P, 2, DM])) for _ in range(2)])
                cross = [sbuf(sc, "cross", [P, 2, NB]) for _ in range(4)]
                for s in time_.slots + freq.slots + prod.slots:
                    s.free = [start]
                ring = Ring(banks)
                vf_ready, S = {}, {"cross": []}

                def linear(left, name, left_ready, on_read):
                    dst = time_.next()
                    bias = w["b" + name]

                    def step(t0):
                        bank = ring.next()
                        for j in range(2):
                            m = mm(bank.ap[:, j * DM:(j + 1) * DM],
                                   [(left(k, t0 + j), w["w" + name][:, k, :]) for k in range(KC)],
                                   left_ready(), w_ready, bank.free)
                        a = dve(lambda e: e.tensor_tensor(
                            dst.ap[:, t0:t0 + 2, :], bank.ap.rearrange("p (t d) -> p t d", d=DM),
                            bias[:, :].unsqueeze(1).to_broadcast([P, 2, DM]), ALU.add), m, dst.free)
                        bank.free = [a]
                        dst.ready = a
                        on_read(m)
                    return dst, [lambda: step(0), lambda: step(2)]

                def spectrum(dst, src):
                    def step(f0):
                        bank = ring.next()
                        for j in range(2):
                            f = f0 + j
                            m = mm(bank.ap[:, j * DM:(j + 1) * DM],
                                   [(fwd[:, t, f * P:(f + 1) * P], src.ap[:, t, :]) for t in range(FC)],
                                   src.ready, w_ready, bank.free)
                        a = act(lambda e: e.activation(dst.ap[:, f0:f0 + 2, :].rearrange("p f d -> p (f d)"),
                                                       bank.ap, ACT.Copy), m, dst.free)
                        bank.free = [a]
                        dst.ready = a
                        if f0:
                            src.free = [m]
                    return [lambda: step(0), lambda: step(2)]

                def correlate(b):
                    def use_hT(m):
                        hT_free[b] = [m]

                    q, q_steps = linear(lambda k, t: hT[:, k, b * SEQ + t * P:b * SEQ + (t + 1) * P], "q",
                                        lambda: hT_ready[b], use_hT)
                    k_, k_steps = linear(lambda k, t: ctx[b].ap[:, k, t * P:(t + 1) * P], "k",
                                         lambda: ctx_ready[b], lambda m: None)
                    qf, kf = freq.next(), freq.next()

                    def products():
                        for i, (qo, ko) in enumerate(((0, 0), (2, 2), (2, 0), (0, 2))):
                            p = prod.next()
                            a = dve(lambda e, qo=qo, ko=ko, p=p: e.tensor_tensor(
                                p.ap[:, :, :], qf.ap[:, qo:qo + 2, :], kf.ap[:, ko:ko + 2, :], ALU.mult),
                                qf.ready, kf.ready, p.free)
                            qf.free = kf.free = [a]
                            r = dve(lambda e, i=i, p=p: e.tensor_reduce(
                                cross[i][:, :, b * HEADS:(b + 1) * HEADS],
                                p.ap[:, :, :].rearrange("p f (h d) -> p f h d", d=DH), AX.X, ALU.add), a, start)
                            p.free = [r]
                            S["cross"] = [r]
                    return q_steps + k_steps + spectrum(qf, q) + spectrum(kf, k_) + [products]

                def value_spectrum(b):
                    v, steps = linear(lambda k, t: ctx[b].ap[:, k, t * P:(t + 1) * P], "v",
                                      lambda: ctx_ready[b], lambda m: None)
                    dst = Slot(vf[b])
                    dst.free = [start]

                    def done():
                        vf_ready[b] = dst.ready
                    return steps + spectrum(dst, v) + [done]

                hold = sbuf(sc, "hold", [1, NB])
                corr = sbuf(sc, "corr", [NB, SEQ])
                top8 = sbuf(sc, "top8", [NB, 8])
                idx = sbuf(sc, "idx", [NB, 8], U32)
                idxf = sbuf(sc, "idxf", [NB, 8])
                neg = sbuf(sc, "neg", [NB, 1])
                tot = sbuf(sc, "tot", [NB, 1])
                wts = sbuf(sc, "wts", [NB, 8])
                kern = sbuf(sc, "kern", [NB, SEQ])
                term = corr
                kernT = sbuf(sc, "kernT", [P, FC, NB])
                cr, ci, cr2 = sbuf(sc, "cr", [P, 2, NB]), sbuf(sc, "ci", [P, 2, NB]), sbuf(sc, "cr2", [P, 2, NB])
                re, im, qiki = cross[0], cross[2], cross[1]

                def cross_spectrum():
                    a = dve(lambda e: e.tensor_copy(hold[:, :], cross[0][0:1, 0, :]), S["cross"], start)
                    a = dve(lambda e: e.tensor_tensor(re[:, :, :], cross[0][:, :, :], qiki[:, :, :], ALU.add), a)
                    a = dve(lambda e: e.tensor_copy(re[0:1, 0, :], hold[:, :]), a)
                    a = dve(lambda e: e.tensor_tensor(im[:, :, :], cross[2][:, :, :], cross[3][:, :, :],
                                                      ALU.subtract), a)
                    S["re_im"] = dve(lambda e: e.tensor_copy(im[0:1, 0, :], qiki[0:1, 0, :]), a)

                def correlation():
                    bank = ring.next()
                    m = mm(bank.ap[0:NB, :], [(re[:, 0, :], inv[:, 0, :]), (re[:, 1, :], inv[:, 1, :]),
                                              (im[:, 0, :], inv[:, 2, :]), (im[:, 1, :], inv[:, 3, :])],
                           S["re_im"], w_ready, bank.free)
                    a = dve(lambda e: e.tensor_scalar(corr[:, :], bank.ap[0:NB, :], 1.0 / DH, None, ALU.mult), m, start)
                    bank.free = [a]
                    a = dve(lambda e: e.max(top8[:, :], corr[:, :]), a)
                    a = dve(lambda e: e.max_index(idx[:, :], top8[:, :], corr[:, :]), a)
                    a = dve(lambda e: e.tensor_copy(idxf[:, :], idx[:, :]), a)
                    a = dve(lambda e: e.tensor_scalar(neg[:, :], top8[:, 0:1], -1.0, None, ALU.mult), a)
                    a = act(lambda e: e.activation(wts[:, 0:TOP], top8[:, 0:TOP], ACT.Exp, bias=neg[:, 0:1]), a)
                    a = dve(lambda e: e.tensor_reduce(tot[:, :], wts[:, 0:TOP], AX.X, ALU.add), a)
                    a = dve(lambda e: e.reciprocal(tot[:, :], tot[:, :]), a)
                    S["kern"] = dve(lambda e: e.tensor_scalar(wts[:, 0:TOP], wts[:, 0:TOP], tot[:, 0:1], None,
                                                              ALU.mult), a)

                def kernel_term(i):
                    dst = term if i else kern
                    a = dve(lambda e: e.tensor_scalar(dst[:, :], iota[0:NB, :], idxf[:, i:i + 1], wts[:, i:i + 1],
                                                      ALU.is_equal, ALU.mult), S["kern"], iota_ready, start)
                    if i:
                        a = dve(lambda e: e.tensor_tensor(kern[:, :], kern[:, :], term[:, :], ALU.add), a)
                    S["kern"] = a

                def turn_kernel():
                    bank = ring.next()
                    for t in range(FC):
                        m = pe(lambda e, t=t: e.transpose(bank.ap[:, t * NB:(t + 1) * NB],
                                                          kern[:, t * P:(t + 1) * P], ident[0:NB, 0:NB]),
                               S["kern"], bank.free)
                    a = act(lambda e: e.activation(kernT[:, :, :].rearrange("p t n -> p (t n)"),
                                                   bank.ap[:, 0:FC * NB], ACT.Copy), m, start)
                    bank.free = [a]
                    S["kernT"] = a

                def kernel_spectrum():
                    bank = ring.next()
                    for f in range(FC):
                        m = mm(bank.ap[:, f * NB:(f + 1) * NB],
                               [(fwd[:, t, f * P:(f + 1) * P], kernT[:, t, :]) for t in range(FC)],
                               S["kernT"], bank.free)
                    view = bank.ap[:, 0:FC * NB].rearrange("p (f n) -> p f n", n=NB)
                    a1 = dve(lambda e: e.tensor_copy(cr[:, :, :], view[:, 0:2, :]), m, start)
                    a2 = dve(lambda e: e.tensor_copy(cr2[:, :, :], view[:, 0:2, :]), m)
                    a3 = dve(lambda e: e.tensor_copy(ci[:, :, :], view[:, 2:4, :]), m)
                    a4 = dve(lambda e: e.tensor_copy(cr2[0:1, 0, :], ci[0:1, 0, :]), a1, a2, a3)
                    S["c"] = dve(lambda e: e.memset(ci[0:1, 0, :], 0.0), a4)
                    bank.free = [a3]

                of, oT = freq, time_

                def turned(slot):
                    return slot.ap[:, :, :].rearrange("p f d -> p (f d)").rearrange("p (c s) -> p c s", s=SEQ)

                def heads(v):
                    return v.rearrange("p (h d) -> p h d", d=DH)

                def output(b):
                    o, ot = of.next(), oT.next()

                    def per_head(c, f):
                        return c[:, f, b * HEADS:(b + 1) * HEADS].unsqueeze(2).to_broadcast([P, HEADS, DH])

                    def products(f):
                        p1, p2 = prod.next(), prod.next()
                        plans = ((0, cr, 2, ci, o.ap[:, f, :], ALU.add), (2, cr2, 0, ci, o.ap[:, 2 + f, :], ALU.subtract))
                        for n, (v1, c1, v2, c2, dst, op) in enumerate(plans):
                            def times(p, v, c, n=n):
                                left, right = heads(vf[b][:, v + f, :]), per_head(c, f)
                                return dve(lambda e: e.tensor_tensor(heads(p.ap[:, n, :]), left, right, ALU.mult),
                                           S["c"], vf_ready[b], p.free)

                            m1, m2 = times(p1, v1, c1), times(p2, v2, c2)
                            s = dve(lambda e, dst=dst, op=op, n=n: e.tensor_tensor(
                                dst, p1.ap[:, n, :], p2.ap[:, n, :], op), m1, m2, o.free)
                        p1.free = p2.free = [s]
                        o.ready = s

                    def to_time(c):
                        bank = ring.next()
                        m = mm(bank.ap, [(o.ap[:, f, c * P:(c + 1) * P], inv[:, f, :]) for f in range(FC)],
                               o.ready, bank.free)
                        a = act(lambda e: e.activation(turned(ot)[:, c, :], bank.ap, ACT.Copy), m, ot.free)
                        bank.free = [a]
                        if c == KC - 1:
                            o.free = [m]
                        ot.ready = a

                    def project(t0):
                        bank = ring.next()
                        for j in range(2):
                            q0 = (t0 + j) * P
                            m = mm(bank.ap[:, j * DM:(j + 1) * DM],
                                   [(turned(ot)[:, k, q0:q0 + P], w["wo"][:, k, :]) for k in range(KC)], ot.ready, bank.free)
                        rows = x[:, 4 * b + t0:4 * b + t0 + 2, :].rearrange("p t d -> p (t d)")
                        a = dve(lambda e: e.tensor_tensor(rows, rows, bank.ap, ALU.add), m, S["x_biased", b])
                        bank.free = [a]
                        x_ready[b] = [a] if t0 == 0 else x_ready[b] + [a]
                        if t0:
                            ot.free = [m]
                    return [lambda: products(0), lambda: products(1)], \
                        [lambda: to_time(0), lambda: to_time(1), lambda: project(0), lambda: project(2)]

                def add_output_bias(b):
                    bo_rows = w["bo"][:, :].unsqueeze(1).to_broadcast([P, 4, DM])
                    ts = tiles_of(b)
                    S["x_biased", b] = pool(lambda e: e.tensor_tensor(x[:, ts, :], x[:, ts, :], bo_rows, ALU.add),
                                            w_ready, hT_ready[b], x_ready[b])

                timed = []
                for b in mine:
                    timed += spread_over(layer_norm(b, ring), b - 1, b - 0.1)
                for b in range(BATCH):
                    timed += spread_over(correlate(b), b, b + 1)
                timed += [(BATCH + 0.5 * b, lambda b=b: add_output_bias(b)) for b in range(BATCH)]
                chain = [cross_spectrum, correlation] + [lambda i=i: kernel_term(i) for i in range(TOP)]
                chain += [lambda: None, turn_kernel, lambda: None, kernel_spectrum]
                timed += spread_over(chain, BATCH, BATCH + 3)
                timed += spread_over([s for b in range(BATCH) for s in value_spectrum(b)], BATCH - 0.1, BATCH + 3.5)
                first = BATCH + 4
                for b in range(BATCH):
                    products, rest_ = output(b)
                    at = first + b
                    timed += spread_over(products, at - 0.9, at - 0.4) + spread_over(rest_, at, at + 1)
                    if b + 1 < BATCH:
                        timed += spread_over(next_layer_norm(b, ring), at + 1.2, at + 2)
                in_time(timed)

        E1, INNER = 4, 1024
        IC = INNER // P
        HALF = SEQ // 2
        STAGE = 1024

        def ffn1_inputs(sc):
            w = {"wr": sbuf(sc, "wr", [P, KC, E1])}
            w |= place_vectors(sc, bo=DM, gam=DM, bet=DM)
            w["stage"] = Ring([Slot(sbuf(sc, "stage", [P, STAGE]), input_count(f"ffn1_stage{i}")) for i in range(2)])

            w1, wo = I["L1_ffn_W1"], I["L1_ffn_Wo"].rearrange("(c p) n -> p c n", p=P)
            w["staged"] = [(lambda ap: ap[0:E1, :], lambda v: [(v, I["L1_ffn_b1"])])]
            for i in range(IC):
                w["staged"].append((
                    lambda ap: ap.rearrange("p (k e n) -> p k e n", k=KC, n=P),
                    lambda v, i=i: [(v[:, k, :, :], w1[:, k * P:(k + 1) * P, i * P:(i + 1) * P]
                                     .rearrange("e p n -> p e n")) for k in range(KC)]))
            for c in range(0, IC, STAGE // DM):
                w["staged"].append((lambda ap: ap.rearrange("p (c n) -> p c n", n=DM),
                                    lambda v, c=c: [(v, wo[:, c:c + STAGE // DM, :])]))
            w["arrived"] = []

            def load_next(*needs):
                view, parts = w["staged"][len(w["arrived"])]
                slot = w["stage"].next()
                v = view(slot.ap[:, :])
                for dst, src in parts(v):
                    t = load(slot.count, dst, src, slot.free, *needs)
                w["arrived"].append((slot, v, t))
            w["load_next"] = load_next

            def start_loads(start, behind):
                W = input_count("ffn1_w")
                fill_weight(W, w["wr"], I["L1_ffn_W_router"], start, behind)
                fill_rows(W, w["bo"], I["L1_ffn_bo"], start, behind)
                fill_rows(W, w["gam"], I["L1_ffn_ln_gamma"], start, behind)
                w["ready"] = fill_rows(W, w["bet"], I["L1_ffn_ln_beta"], start, behind)
                for _ in w["stage"].slots:
                    load_next(start, behind)
            return w, start_loads

        def ffn1(w):
            start = fence()
            with ExitStack() as sc:
                gates = Gates(sc, 8, 1)
                low = dve(lambda e: e.memset(gates.v[:, :, :], -3.4e38), start)
                hotT = Ring([Slot(sbuf(sc, "hotT", [8, SEQ], F32R)) for _ in range(2)])
                hotb = Ring([Slot(sbuf(sc, "hotb", [8, SEQ], BF16)) for _ in range(2)])
                pick = sbuf(sc, "pick", [8, E1, P])
                pickb = sbuf(sc, "pickb", [8, E1, P], BF16)
                p = pool(lambda e: e.memset(pick[:, :, :], 0.0), start)
                p = pool(lambda e: e.affine_select(
                    out=pick[:, :, :], in_=pick[:, :, :], compare_op=ALU.not_equal, fill=1.0, base=0,
                    pattern=[[-1, E1], [0, P]], channel_multiplier=1), p)
                pick_ready = pool(lambda e: e.tensor_copy(pickb[:, :, :], pick[:, :, :]), p)
                b1 = new_pair(sc, "b1", [E1, INNER])
                w1 = new_pair(sc, "w1", [P, IC, KC, E1, P])
                wo = new_pair(sc, "wo", [P, IC, DM])
                hhalf = Slot(new_pair(sc, "hhalf", [P, KC, HALF]))
                masked = pair_ring(sc, "masked", [P, E1, KC, HALF], 2, start)
                inner = Slot(new_pair(sc, "inner", [P, IC, HALF]))
                gelu = Ring([Slot(sbuf(sc, "gelu", [P, HALF])) for _ in range(3)])
                y = Slot(sbuf(sc, "y", [P, 4, DM]))
                mean2, veps2 = sbuf(sc, "meanvar2", [P, TILES, 2]), sbuf(sc, "veps2", [P, TILES])
                rstd2, ntmp2 = sbuf(sc, "rstd2", [P, TILES]), sbuf(sc, "ntmp2", [P, TILES])
                for s in hotT.slots + hotb.slots + gelu.slots + [hhalf, inner, y]:
                    s.free = [start]
                ring = Ring(banks)
                S = {"stats": {}}
                piece = {}

                def take_piece(n):
                    slot, v, t = w["arrived"][n]
                    dst = b1[:, :] if n == 0 else w1[:, n - 1] if n <= IC else \
                        wo[:, (n - 1 - IC) * (STAGE // DM):(n - IC) * (STAGE // DM), :]
                    piece[n] = split_pair(dst, v, t, start, lo_on=dve)
                    slot.free = piece[n]
                    if len(w["arrived"]) < len(w["staged"]):
                        w["load_next"]()

                def route(g):
                    hot, hb = hotT.next(), hotb.next()
                    S["hot", g] = hot, hb

                    def logits():
                        token_logits(gates, g, w["wr"], w["ready"], ring,
                                     lambda dst, src, m: dve(lambda e: e.tensor_copy(dst, src), m, low))

                    def turn():
                        hot.ready = turn_gates(hot.ap[:, :], gates.hot[0], g, 8, ring, gates.done[g], hot.free)
                        hb.ready = dve(lambda e: e.tensor_copy(hb.ap[:, :], hot.ap[:, :].bitcast(F32)), hot.ready,
                                       hb.free)
                    return [logits] + gates.largest(g) + [idle, turn]

                def mask(hf):
                    g, at = divmod(hf, 2)
                    mk = masked.next()
                    S["masked", hf] = mk
                    cols = slice(at * HALF, (at + 1) * HALF)

                    def split():
                        src = hT[:, :, hf * HALF:(hf + 1) * HALF]
                        hhalf.ready = split_pair(hhalf.ap[:, :, :], src, hT_ready[g], hhalf.free)
                        hT_free[g] = hT_free[g] + hhalf.ready

                    def expert(ex):
                        _, hb = S["hot", g]
                        bank = ring.next()
                        m = mm(bank.ap[:, 0:HALF], [(pickb[:, ex, :], hb.ap[:, cols])], hb.ready, pick_ready, bank.free)
                        hb.free = [m]
                        rows = bank.ap[:, 0:HALF].unsqueeze(1).to_broadcast([P, KC, HALF])
                        for part in ("hi", "lo"):
                            dst, src = (mk.ap.hi, hhalf.ap.hi) if part == "hi" else (mk.ap.lo, hhalf.ap.lo)
                            a = dve(lambda e, dst=dst, src=src: e.tensor_tensor(
                                dst[:, ex, :, :], src[:, :, :].bitcast(F32), rows, ALU.mult),
                                m, mk.free, hhalf.ready)
                        bank.free = hhalf.free = [a]
                        mk.ready = a
                    return [split, idle] + [lambda ex=ex: expert(ex) for ex in range(E1)]

                def residual(g):
                    ts = tiles_of(g)
                    for i in range(4):
                        a = normed(y.ap[:, i, :], x[:, 4 * g + i, :], 4 * g + i, y.free, x_ready[g])
                    y.ready = pool(lambda e: e.tensor_tensor(
                        y.ap[:, :, :], y.ap[:, :, :], w["bo"][:, :].unsqueeze(1).to_broadcast([P, 4, DM]), ALU.add),
                        a, w["ready"])
                    x_ready[g] = [pool(lambda e: e.tensor_tensor(
                        x[:, ts, :], x[:, ts, :], w["bet"][:, :].unsqueeze(1).to_broadcast([P, 4, DM]), ALU.add), a)]

                def first(hf, i):
                    g, at = divmod(hf, 2)
                    hot, mk = S["hot", g][0], S["masked", hf]
                    bank, ge = ring.next(), gelu.next()
                    rows = hot.ap[0:E1, at * HALF:(at + 1) * HALF]
                    cols = slice(i * P, (i + 1) * P)
                    passes = []
                    for ex in range(E1):
                        for k in range(KC):
                            a, b = w1[:, i, k, ex, :], mk.ap[:, ex, k, :]
                            passes += [(a.hi, b.hi), (a.hi, b.lo), (a.lo, b.hi)]
                    passes += [(b1.hi[:, cols], rows), (b1.lo[:, cols], rows)]
                    m = mm(bank.ap[:, 0:HALF], passes, mk.ready, hot.ready, piece[0], piece[i + 1], bank.free)
                    ge.ready = act(lambda e: e.activation(ge.ap[:, :], bank.ap[:, 0:HALF], ACT.Gelu), m, ge.free)
                    bank.free = [ge.ready]
                    S["gelu", hf, i] = ge
                    if i == IC - 1:
                        mk.free, hot.free = [m], [m]

                def keep(hf, i):
                    ge = S["gelu", hf, i]
                    ge.free = split_pair(inner.ap[:, i, :], ge.ap[:, :], ge.ready, inner.free)
                    inner.ready = ge.free if i == 0 else inner.ready + ge.free

                def second(hf, i):
                    g, at = divmod(hf, 2)
                    bank = ring.next()
                    tile = 2 * at + i
                    m = mm3(bank.ap[:, 0:DM], [(inner.ap[:, j, i * P:(i + 1) * P], wo[:, j, :])
                                               for j in range(IC)], inner.ready, piece[IC + 1], piece[IC + 2],
                            bank.free)
                    a = dve(lambda e: e.tensor_tensor(y.ap[:, tile, :], y.ap[:, tile, :], bank.ap[:, 0:DM], ALU.add),
                            m, y.ready)
                    bank.free = [a]
                    S["stats"][g] = moments(y.ap[:, tile, :], 4 * g + tile, a, mean2)
                    if i:
                        inner.free = [m]

                def close(g):
                    ts = tiles_of(g)
                    power, newton = rsqrt(ts, 1e-12, (mean2, veps2, rstd2, ntmp2))

                    def root():
                        S["r2"] = newton()

                    def scale():
                        for i in range(4):
                            n = normed(y.ap[:, i, :], y.ap[:, i, :], 4 * g + i, S["r2"], stat=(mean2, rstd2))
                        S["gam"] = pool(lambda e: e.tensor_tensor(
                            y.ap[:, :, :], y.ap[:, :, :], w["gam"][:, :].unsqueeze(1).to_broadcast([P, 4, DM]),
                            ALU.mult), n)

                    def add():
                        x_ready[g] = y.free = [dve(lambda e: e.tensor_tensor(x[:, ts, :], x[:, ts, :], y.ap[:, :, :],
                                                                             ALU.add), S["gam"], x_ready[g])]
                    return [lambda: power(S["stats"][g]), root, scale, idle, add]

                mine = own_layer_norms()
                timed = []
                for n in range(2 + IC + 1):
                    at = (-0.9, -0.8, 0.02)[n] if n < 3 else (n - 2.7) / IC if n <= IC else 0.85 + 0.05 * (n - IC)
                    timed.append((at, lambda n=n: take_piece(n)))
                for g in range(BATCH):
                    at = 2 * g
                    ready = (layer_norm(g, ring) if g in mine else []) + route(g)
                    timed += spread_over(ready, at - 1.9, at - 0.85)
                    timed.append((at + 0.75, lambda g=g: residual(g)))
                    timed += spread_over(close(g), at + 2.3, at + 2.7)
                    if g + 1 < BATCH:
                        timed += spread_over(next_layer_norm(g, ring), at + 2.8, at + 3.6)
                for hf in range(2 * BATCH):
                    timed += spread_over(mask(hf), hf - 0.8, hf - 0.05)
                    timed += spread_over([lambda hf=hf, i=i: first(hf, i) for i in range(IC)], hf, hf + 1)
                    timed += spread_over([lambda hf=hf, i=i: keep(hf, i) for i in range(IC)], hf + 0.15, hf + 1.15)
                    timed += [(hf + 1.15, lambda hf=hf: second(hf, 0)), (hf + 1.16, lambda hf=hf: second(hf, 1))]
                in_time(timed)

        E2 = 8

        def ffn2_inputs(sc):
            w = {"wsi": sbuf(sc, "wsi", [P, KC, 2 * DM]), "w1": sbuf(sc, "w1", [P, KC, 2 * DM]),
                 "w2": sbuf(sc, "w2", [P, KC, E2, DM]), "wso": sbuf(sc, "wso", [P, KC, DM]),
                 "wg": sbuf(sc, "wg", [P, KC, E2])}
            w |= place_vectors(sc, gb=E2)

            def start_loads(start, behind):
                G, H, W = input_count("ffn2_gate"), input_count("ffn2_hidden"), input_count("ffn2_w")
                fill_weight(G, w["wg"], I["L2_ffn_w_gate"], start, behind)
                w["gate_ready"] = fill_rows(G, w["gb"], I["L2_ffn_gate_bias"], start, behind)
                fill_weight(H, w["wsi"], I["L2_ffn_w_shared_in"], start, behind)
                w["hidden_ready"] = fill_weight(H, w["w1"], I["L2_ffn_w1_shared"], start, behind)
                fill_weight(W, w["wso"], I["L2_ffn_w_shared_out"], start, behind)
                for k in range(KC):
                    w["ready"] = load(W, w["w2"][:, k, :, :],
                                      I["L2_ffn_w2"][:, k * P:(k + 1) * P, :].rearrange("e p n -> p e n"), start, behind)
            return w, start_loads

        def ffn2(w):
            start = fence()
            with ExitStack() as sc:
                gates = Gates(sc, E2, 2)
                hidden = pair_ring(sc, "hidden", [P, 2, KC, SEQ], 2, start)
                silu = Ring([Slot(sbuf(sc, "silu", [P, SEQ])) for _ in range(3)])
                for s in silu.slots:
                    s.free = [start]
                ring = Ring(banks)
                hpair = pair_ring(sc, "hpair", [P, KC, SEQ], 2, start)
                hp = {}
                pairs = {name: new_pair(sc, name + "_pair", w[name].shape) for name in ("wsi", "w1", "wso", "w2")}
                pair_ready = {name: [] for name in pairs}

                def split_weights():
                    for name, ready in (("wsi", w["hidden_ready"]), ("w1", w["hidden_ready"]),
                                        ("wso", w["ready"]), ("w2", w["ready"])):
                        for k in range(KC):
                            for at in range(0, E2, 2) if name == "w2" else (slice(None),):
                                part = slice(at, at + 2) if name == "w2" else at
                                pair_ready[name] += split_pair(pairs[name][:, k, part], w[name][:, k, part], ready,
                                                               start, lo_on=dve if k else pool)

                def prepare(g):
                    ts = tiles_of(g)
                    hp[g], split = split_rows(hpair, g)

                    def logits():
                        gb = w["gb"][:, :].unsqueeze(1).to_broadcast([P, 4, E2])
                        token_logits(gates, g, w["wg"], w["gate_ready"], ring,
                                     lambda dst, src, m: dve(lambda e: e.tensor_tensor(dst, src, gb, ALU.add), m))
                    return [split, logits] + gates.softmax(g) + gates.largest(g) + [
                        lambda: gates.weigh(g, lambda i: gates.top8[:, ts, i])]

                def main(g):
                    hid = hidden.next()
                    steps = []
                    for which, name in enumerate(("wsi", "w1")):
                        for c in range(KC):
                            def half_hidden(which=which, name=name, c=c):
                                ba, bb, s = ring.next(), ring.next(), silu.next()
                                ma, mb = [mm3(bank.ap, [(pairs[name][:, k, at + c * P:at + (c + 1) * P],
                                                         hp[g].ap[:, k, :]) for k in range(KC)],
                                              hp[g].ready, pair_ready[name], bank.free)
                                          for bank, at in ((ba, 0), (bb, DM))]
                                hp[g].free = [mb]
                                a = act(lambda e: e.activation(s.ap[:, :], ba.ap, ACT.Silu), ma, s.free)
                                ba.free = [a]
                                b = dve(lambda e: e.tensor_tensor(s.ap[:, :], s.ap[:, :], bb.ap, ALU.mult), a, mb)
                                bb.free = [b]
                                made = split_pair(hid.ap[:, which, c, :], s.ap[:, :], b, hid.free)
                                s.free = made
                                hid.ready = made if which == c == 0 else hid.ready + made
                            steps.append(half_hidden)
                    for j in range(4):
                        t = 4 * g + j
                        cols = slice(j * P, (j + 1) * P)

                        def shared(t=t, cols=cols):
                            bank = ring.next()
                            m = mm3(bank.ap[:, 0:DM], [(hid.ap[:, 0, k, cols], pairs["wso"][:, k, :])
                                                       for k in range(KC)], hid.ready, pair_ready["wso"], bank.free)
                            a = dve(lambda e: e.tensor_tensor(x[:, t, :], x[:, t, :], bank.ap[:, 0:DM], ALU.add),
                                    m, x_ready[g])
                            x_ready[g] = bank.free = [a]
                        steps.append(shared)
                        for e2 in range(E2 // 2):
                            def routed(t=t, e2=e2, cols=cols):
                                bank = ring.next()
                                m = mm3(bank.ap, [(hid.ap[:, 1, k, cols], pairs["w2"][:, k, 2 * e2:2 * e2 + 2, :]
                                                   .rearrange("p e n -> p (e n)")) for k in range(KC)],
                                        hid.ready, pair_ready["w2"], bank.free)
                                for i in range(2):
                                    a = dve(lambda e, i=i: e.scalar_tensor_tensor(
                                        out=x[:, t, :], in0=bank.ap[:, i * DM:(i + 1) * DM],
                                        scalar=gates.v[:, t, 2 * e2 + i:2 * e2 + i + 1],
                                        in1=x[:, t, :], op0=ALU.mult, op1=ALU.add), m, gates.done[g], x_ready[g])
                                    x_ready[g] = [a]
                                bank.free = [a]
                                hid.free = [m]
                            steps.append(routed)
                    return steps
                by_batch(prepare, main, ring, split_weights)

        E3, RH = 16, 128

        def ffn3_inputs(sc):
            w = {"w1": sbuf(sc, "w1", [P, KC, RH]), "wg1": sbuf(sc, "wg1", [P, KC, RH]),
                 "w2": sbuf(sc, "w2", [P, 1, E3]), "wg2": sbuf(sc, "wg2", [P, 1, 1]),
                 "scale_bias": sbuf(sc, "scale_bias", [E3, 2, DM])}
            w |= place_vectors(sc, b1=1, bg1=1, b2=E3, bg2=1)

            def start_loads(start, behind):
                W = input_count("ffn3_w")
                for name, src in (("w1", "W1"), ("wg1", "Wg1"), ("w2", "W2"), ("wg2", "Wg2")):
                    fill_weight(W, w[name], I["L3_ffn_" + src], start, behind)
                fill_columns(W, w["b1"], I["L3_ffn_b1"], start, behind)
                fill_columns(W, w["bg1"], I["L3_ffn_bg1"], start, behind)
                fill_rows(W, w["b2"], I["L3_ffn_b2"], start, behind)
                fill_rows(W, w["bg2"], I["L3_ffn_bg2"], start, behind)
                load(W, w["scale_bias"][:, 0, :], I["L3_ffn_expert_scales"], start, behind)
                w["ready"] = load(W, w["scale_bias"][:, 1, :], I["L3_ffn_expert_biases"], start, behind)
            return w, start_loads

        def ffn3(w):
            start = fence()
            with ExitStack() as sc:
                gates = Gates(sc, E3, 1)
                relu = Ring([Slot(sbuf(sc, "relu", [P, SEQ])) for _ in range(2)])
                tanh = Ring([Slot(sbuf(sc, "tanh", [P, SEQ])) for _ in range(2)])
                gate = sbuf(sc, "gate", [P, TILES])
                hotT = Ring([Slot(sbuf(sc, "hotT", [E3, SEQ])) for _ in range(2)])
                hrows = Ring([Slot(sbuf(sc, "h", [P, 4, DM])) for _ in range(2)])
                for s in relu.slots + tanh.slots + hotT.slots + hrows.slots:
                    s.free = [start]
                ring = Ring(banks)
                S = {}

                def prepare(g):
                    r, th, hot, h = relu.next(), tanh.next(), hotT.next(), hrows.next()
                    S["hot", g] = hot, h
                    ts = tiles_of(g)

                    def hidden():
                        for slot, name, b, fn in ((r, "w1", "b1", ACT.Relu), (th, "wg1", "bg1", ACT.Tanh)):
                            bank = ring.next()
                            m = mm(bank.ap, [(w[name][:, k, :], hT[:, k, rows_of(g)]) for k in range(KC)],
                                   hT_ready[g], w["ready"], bank.free)
                            slot.ready = act(lambda e, slot=slot, b=b, fn=fn, bank=bank: e.activation(
                                slot.ap[:, :], bank.ap, fn, bias=w[b][:, 0:1]), m, slot.free)
                            bank.free = [slot.ready]

                    def scores():
                        b1_, b2_ = ring.next(), ring.next()
                        for i in range(4):
                            m = mm(b1_.ap[:, i * E3:(i + 1) * E3], [(r.ap[:, i * P:(i + 1) * P], w["w2"][:, 0, :])],
                                   r.ready, b1_.free)
                        for i in range(4):
                            m2 = mm(b2_.ap[:, i:i + 1], [(th.ap[:, i * P:(i + 1) * P], w["wg2"][:, 0, :])],
                                    th.ready, b2_.free)
                        r.free, th.free = [m], [m2]
                        v = gates.v[:, ts, :]
                        a = dve(lambda e: e.tensor_tensor(
                            v, b1_.ap[:, 0:4 * E3].rearrange("p (t e) -> p t e", e=E3),
                            w["b2"][:, :].unsqueeze(1).to_broadcast([P, 4, E3]), ALU.add), m)
                        b1_.free = [a]
                        s = act(lambda e: e.activation(gate[:, ts], b2_.ap[:, 0:4], ACT.Sigmoid,
                                                       bias=w["bg2"][:, 0:1]), m2, start)
                        b2_.free = [s]
                        gates.done[g] = dve(lambda e: e.tensor_tensor(v, v, over(gate[:, ts], E3), ALU.mult), a, s)

                    def turn():
                        hot.ready = turn_gates(hot.ap[:, :], gates.hot[0], g, E3, ring, gates.done[g], hot.free)

                    def rows():
                        for i in range(4):
                            h.ready = normed(h.ap[:, i, :], x[:, 4 * g + i, :], 4 * g + i, h.free, x_ready[g])
                    return [hidden, scores, rows] + gates.softmax(g) + gates.largest(g) + [idle, turn]

                def main(g):
                    hot, h = S["hot", g]

                    def step(i):
                        t = 4 * g + i
                        bank = ring.next()
                        m = mm(bank.ap, [(hot.ap[:, i * P:(i + 1) * P],
                                          w["scale_bias"][:, :, :].rearrange("e a d -> e (a d)"))], hot.ready, bank.free)
                        a = dve(lambda e: e.tensor_tensor(h.ap[:, i, :], h.ap[:, i, :], bank.ap[:, 0:DM], ALU.mult),
                                m, h.ready)
                        a2 = dve(lambda e: e.tensor_tensor(x[:, t, :], x[:, t, :], bank.ap[:, DM:2 * DM], ALU.add), m)
                        bank.free = [a2]
                        a = dve(lambda e: e.tensor_tensor(x[:, t, :], x[:, t, :], h.ap[:, i, :], ALU.add), a, a2)
                        x_ready[g] = h.free = [a]
                        hot.free = [m]
                    return [lambda i=i: step(i) for i in range(4)]

                timed = []
                mine = own_layer_norms()
                for g in range(BATCH):
                    if g in mine:
                        timed += spread_over(layer_norm(g, ring), g - 2, g - 1.2)
                    timed += spread_over(prepare(g), g - 1, g + 0.5)
                    timed += spread_over(main(g), g + 0.6, g + 1.3)
                in_time(timed)

        table = {0: (attention_inputs("L0", True), lambda w: attention("L0", True, True, w)),
                 1: (ffn0_inputs, ffn0),
                 2: (autocorrelation_inputs, autocorrelation),
                 3: (ffn1_inputs, ffn1),
                 4: (attention_inputs("L2", False), lambda w: attention("L2", False, False, w)),
                 5: (ffn2_inputs, ffn2),
                 6: (attention_inputs("L3", True), lambda w: attention("L3", True, True, w)),
                 7: (ffn3_inputs, ffn3)}
        for chain in CHAINS:
            phases = [table[n] for n in chain if n in LAYERS]
            scopes = [ExitStack() for _ in phases]
            start = fence()
            placed = [place(scope) for (place, _), scope in zip(phases[::-1], scopes[::-1])][::-1]
            behind = None
            for w, start_loads in placed:
                start_loads(start, behind)
                for b in range(BATCH):
                    load_x(b)
                behind = w["ready"]
            for (_, run_phase), (w, _), scope in zip(phases, placed, scopes):
                run_phase(w)
                scope.close()
        store = [new_count(f"store{b}") for b in range(BATCH)]
        stored = [load(store[b], out[b].rearrange("(t p) d -> p t d", p=P), x[:, 4 * b:4 * b + 4, :], x_ready[b])
                  for b in range(BATCH)]
        sp(lambda e: e.nop(), stored, signal=False)

        block = top.enter_context(nc.Block())

        @block.tensor
        def _(e):
            pe.run(e)

        @block.vector
        def _(e):
            dve.run(e)

        @block.scalar
        def _(e):
            act.run(e)

        @block.gpsimd
        def _(e):
            pool.run(e)

        @block.sync
        def _(e):
            sp.run(e)


LAYERS = range(8)
CHAINS = ((0,), (1, 2, 3), (4,), (5, 6), (7,))


def dft_tables():
    n, half = SEQ, SEQ // 2
    t = np.arange(n)
    f = np.arange(half)
    angle = 2 * np.pi * ((t[:, None] * f[None, :]) % n) / n
    nyquist = np.where(t % 2 == 0, 1.0, -1.0)
    fwd = np.concatenate([np.cos(angle), -np.sin(angle)], 1)
    fwd[:, half] = nyquist
    weight = np.where(f == 0, 1.0, 2.0) / n
    inv = np.concatenate([(np.cos(angle) * weight).T, (-np.sin(angle) * weight).T], 0)
    inv[half] = nyquist / n
    return fwd.astype(np.float32), inv.astype(np.float32)


TRANSPOSED = {"L0_wq": "L0_xattn_wq_w", "L0_wk": "L0_xattn_wk_w", "L0_wv": "L0_xattn_wv_w", "L0_wo": "L0_xattn_dense_w",
              "L2_wq": "L2_xattn_Wq", "L2_wk": "L2_xattn_Wk", "L2_wv": "L2_xattn_Wv", "L2_wo": "L2_xattn_Wo",
              "L3_wq": "L3_xattn_Wq", "L3_wk": "L3_xattn_Wk", "L3_wv": "L3_xattn_Wv", "L3_wo": "L3_xattn_Wo"}
RENAMED = {"L0_bq": "L0_xattn_wq_b", "L0_bk": "L0_xattn_wk_b", "L0_bv": "L0_xattn_wv_b", "L0_bo": "L0_xattn_dense_b",
           "L3_bq": "L3_xattn_bq", "L3_bk": "L3_xattn_bk", "L3_bv": "L3_xattn_bv", "L3_bo": "L3_xattn_bo"}
AS_IS = ["x", "L0_ffn_Wg", "L0_ffn_We", "L0_ffn_be",
         "L1_xattn_Wq", "L1_xattn_bq", "L1_xattn_Wk", "L1_xattn_bk", "L1_xattn_Wv", "L1_xattn_bv", "L1_xattn_Wo",
         "L1_xattn_bo", "L1_ffn_W_router", "L1_ffn_W1", "L1_ffn_b1", "L1_ffn_Wo", "L1_ffn_bo", "L1_ffn_ln_gamma",
         "L1_ffn_ln_beta", "L2_ffn_w_shared_in", "L2_ffn_w_shared_out", "L2_ffn_w1_shared", "L2_ffn_w2",
         "L2_ffn_w_gate", "L2_ffn_gate_bias", "L3_ffn_W1", "L3_ffn_b1", "L3_ffn_W2", "L3_ffn_b2", "L3_ffn_Wg1",
         "L3_ffn_bg1", "L3_ffn_Wg2", "L3_ffn_bg2", "L3_ffn_expert_scales", "L3_ffn_expert_biases"]


def kernel(**inputs):
    import numpy as _np
    import concourse.bacc as _bacc
    from concourse import mybir as _mybir
    from concourse.bass_utils import run_bass_kernel_spmd as _run

    arrays = {name: _np.ascontiguousarray(inputs[name]) for name in AS_IS}
    arrays |= {name: _np.ascontiguousarray(inputs[src]) for name, src in RENAMED.items()}
    arrays |= {name: _np.ascontiguousarray(_np.asarray(inputs[src]).T) for name, src in TRANSPOSED.items()}
    arrays["ctxT"] = _np.ascontiguousarray(_np.asarray(inputs["ctx_1024"]).transpose(2, 0, 1))
    arrays["dft"], arrays["idft"] = dft_tables()

    nc = _bacc.Bacc("TRN2", target_bir_lowering=False, num_devices=1)
    named, I = {}, {}
    for name, a in arrays.items():
        named[f"in_{name}"] = a
        I[name] = nc.dram_tensor(f"in_{name}", a.shape, _mybir.dt.from_np(a.dtype), kind="ExternalInput").ap()
    out = nc.dram_tensor("out_dram", (BATCH, SEQ, DM), F32, kind="ExternalOutput").ap()
    build(nc, I, out)
    r = _run(nc, [named], core_ids=[0])
    return r.results[0]["out_dram"]
```
